# Optimizing a Trainium2 kernel written in Bass

```python
import numpy as np
import jax
import jax.numpy as jnp

def _softmax(x, axis=-1):
    return jax.nn.softmax(x, axis=axis)

def _gelu(x):
    return jax.nn.gelu(x, approximate=True)

def _silu(x):
    return jax.nn.silu(x)

def _sigmoid(x):
    return jax.nn.sigmoid(x)

def _layernorm(x, axis=-1, eps=1e-05):
    m = jnp.mean(x, axis=axis, keepdims=True)
    v = jnp.var(x, axis=axis, keepdims=True)
    return (x - m) / jnp.sqrt(v + eps)

def _scatter_add(tgt, idx, src, axis=0):
    return tgt.at[idx].add(src)

def _segment_sum(src, seg, n):
    return jax.ops.segment_sum(src, seg, n)
kernel_name = 'mk_seq_preln_d1_jaxref_r8_d210f3'

def setup_inputs(seed: int=0):
    np.random.seed(seed)
    _w = jnp.asarray

    def _L0_attn_setup():
        import jax, jax.numpy as jnp
        import numpy as np
        B, S, HID = (2, 256, 256)
        NH, DN, DR, DV, RANK = (16, 128, 64, 128, 64)
        DQK = DN + DR
        SCALE = DQK ** (-0.5)
        EPS = 1e-05

        def _rope(x, theta):
            x1, x2 = (x[..., 0::2], x[..., 1::2])
            c, s = (jnp.cos(theta), jnp.sin(theta))
            return jnp.stack([x1 * c - x2 * s, x1 * s + x2 * c], axis=-1).reshape(x.shape)

        def _layernorm(x, gamma, beta):
            mu = jnp.mean(x, axis=-1, keepdims=True)
            var = jnp.var(x, axis=-1, keepdims=True)
            return (x - mu) * jax.lax.rsqrt(var + EPS) * gamma + beta
        key = jax.random.key(seed)
        ks = jax.random.split(key, 8)

        def xavier(k, fan_in, fan_out, gain=1.0):
            lim = gain * np.sqrt(6.0 / (fan_in + fan_out))
            return jax.random.uniform(k, (fan_in, fan_out), jnp.float32, -lim, lim)
        return {'hidden_states': jax.random.normal(ks[0], (B, S, HID), jnp.float32), 'freqs_cis': jax.random.uniform(ks[1], (S, DR // 2), jnp.float32) * 2.0 * np.pi, 'Wq': xavier(ks[2], HID, NH * DQK), 'Wkv_a': xavier(ks[3], HID, RANK + DR), 'kv_gamma': jnp.ones((RANK,), jnp.float32), 'kv_beta': jnp.zeros((RANK,), jnp.float32), 'Wkv_b': xavier(ks[4], RANK, NH * (DN + DV)), 'Wout': xavier(ks[5], NH * DV, HID, gain=1.0 / np.sqrt(2.0))}
    _L0_attn_in = _L0_attn_setup()

    def _L0_ffn_setup():
        import jax, jax.numpy as jnp
        import numpy as np
        B, S, D = (4, 64, 256)
        E, K, H = (8, 2, 176)
        HS = 2 * 176
        ALPHA = 0.001
        W_SCALE = 0.02

        def _moe_forward(hidden_states, gate_w, w_gate, w_up, w_down, sw_gate, sw_up, sw_down):
            b, s, d = hidden_states.shape
            x = hidden_states.reshape(-1, d)
            T = x.shape[0]
            logits = x @ gate_w
            scores = jax.nn.softmax(logits, axis=-1)
            topk_w, topk_idx = jax.lax.top_k(scores, K)
            mask = jax.nn.one_hot(topk_idx, E, dtype=scores.dtype).sum(axis=1)
            ce = mask.mean(axis=0)
            Pi = scores.mean(axis=0)
            aux_loss = (Pi * ce * E).sum() * ALPHA
            comb = jnp.zeros((T, E), dtype=x.dtype)
            comb = comb.at[jnp.arange(T)[:, None], topk_idx].add(topk_w)
            g = jax.nn.silu(jnp.einsum('td,edh->teh', x, w_gate)) * jnp.einsum('td,edh->teh', x, w_up)
            routed = jnp.einsum('teh,ehd,te->td', g, w_down, comb)
            shared = jax.nn.silu(x @ sw_gate) * (x @ sw_up) @ sw_down
            out = (routed + shared).reshape(b, s, d)
            return (out, aux_loss)
        key = jax.random.key(seed)
        ks = jax.random.split(key, 8)
        rn = lambda k, sh: jax.random.normal(k, sh, dtype=jnp.float32)
        return {'hidden_states': rn(ks[0], (B, S, D)), 'gate_w': rn(ks[1], (D, E)) * W_SCALE, 'w_gate': rn(ks[2], (E, D, H)) * W_SCALE, 'w_up': rn(ks[3], (E, D, H)) * W_SCALE, 'w_down': rn(ks[4], (E, H, D)) * W_SCALE, 'sw_gate': rn(ks[5], (D, HS)) * W_SCALE, 'sw_up': rn(ks[6], (D, HS)) * W_SCALE, 'sw_down': rn(ks[7], (HS, D)) * W_SCALE}
    _L0_ffn_in = _L0_ffn_setup()
    _d = {'L0_attn_hidden_states': _L0_attn_in['hidden_states'], 'L0_attn_freqs_cis': _L0_attn_in['freqs_cis'], 'L0_attn_Wq': _L0_attn_in['Wq'], 'L0_attn_Wkv_a': _L0_attn_in['Wkv_a'], 'L0_attn_kv_gamma': _L0_attn_in['kv_gamma'], 'L0_attn_kv_beta': _L0_attn_in['kv_beta'], 'L0_attn_Wkv_b': _L0_attn_in['Wkv_b'], 'L0_attn_Wout': _L0_attn_in['Wout'], 'L0_ffn_gate_w': _L0_ffn_in['gate_w'], 'L0_ffn_w_gate': _L0_ffn_in['w_gate'], 'L0_ffn_w_up': _L0_ffn_in['w_up'], 'L0_ffn_w_down': _L0_ffn_in['w_down'], 'L0_ffn_sw_gate': _L0_ffn_in['sw_gate'], 'L0_ffn_sw_up': _L0_ffn_in['sw_up'], 'L0_ffn_sw_down': _L0_ffn_in['sw_down']}
    _x0 = _d['L0_attn_hidden_states']
    _d['L0_attn_hidden_states'] = jax.random.normal(jax.random.fold_in(jax.random.key(seed), 1), (8, 256, 256), dtype=_x0.dtype)
    del _x0
    return _d

def reference(L0_attn_hidden_states, L0_attn_freqs_cis, L0_attn_Wq, L0_attn_Wkv_a, L0_attn_kv_gamma, L0_attn_kv_beta, L0_attn_Wkv_b, L0_attn_Wout, L0_ffn_gate_w, L0_ffn_w_gate, L0_ffn_w_up, L0_ffn_w_down, L0_ffn_sw_gate, L0_ffn_sw_up, L0_ffn_sw_down):

    def _L0_attn_ref(hidden_states, freqs_cis, Wq, Wkv_a, kv_gamma, kv_beta, Wkv_b, Wout):
        import jax, jax.numpy as jnp
        import numpy as np
        B, S, HID = (2, 256, 256)
        NH, DN, DR, DV, RANK = (16, 128, 64, 128, 64)
        DQK = DN + DR
        SCALE = DQK ** (-0.5)
        EPS = 1e-05

        def _rope(x, theta):
            x1, x2 = (x[..., 0::2], x[..., 1::2])
            c, s = (jnp.cos(theta), jnp.sin(theta))
            return jnp.stack([x1 * c - x2 * s, x1 * s + x2 * c], axis=-1).reshape(x.shape)

        def _layernorm(x, gamma, beta):
            mu = jnp.mean(x, axis=-1, keepdims=True)
            var = jnp.var(x, axis=-1, keepdims=True)
            return (x - mu) * jax.lax.rsqrt(var + EPS) * gamma + beta
        b, s, _ = hidden_states.shape
        max_len = freqs_cis.shape[0]
        pos = jnp.arange(s) % max_len
        theta = freqs_cis[pos]
        q = (hidden_states @ Wq).reshape(b, s, NH, DQK)
        q_nope, q_rope = (q[..., :DN], q[..., DN:])
        q_rope = _rope(q_rope, theta[None, :, None, :])
        kv = hidden_states @ Wkv_a
        kv_c, k_rope = (kv[..., :RANK], kv[..., RANK:])
        k_rope = _rope(k_rope, theta[None, :, :])
        kv_c = _layernorm(kv_c, kv_gamma, kv_beta)
        kvb = (kv_c @ Wkv_b).reshape(b, s, NH, DN + DV)
        k_nope, v = (kvb[..., :DN], kvb[..., DN:])
        k = jnp.concatenate([k_nope, jnp.broadcast_to(k_rope[:, :, None, :], (b, s, NH, DR))], axis=-1)
        q = jnp.concatenate([q_nope, q_rope], axis=-1)
        scores = jnp.einsum('bthd,bshd->btsh', q, k) * SCALE
        weights = jax.nn.softmax(scores.astype(jnp.float32), axis=2).astype(q.dtype)
        attn = jnp.einsum('btsh,bshd->bthd', weights, v).reshape(b, s, NH * DV)
        return attn @ Wout

    def _L0_ffn_ref(hidden_states, gate_w, w_gate, w_up, w_down, sw_gate, sw_up, sw_down):
        import jax, jax.numpy as jnp
        import numpy as np
        B, S, D = (4, 64, 256)
        E, K, H = (8, 2, 176)
        HS = 2 * 176
        ALPHA = 0.001
        W_SCALE = 0.02

        def _moe_forward(hidden_states, gate_w, w_gate, w_up, w_down, sw_gate, sw_up, sw_down):
            b, s, d = hidden_states.shape
            x = hidden_states.reshape(-1, d)
            T = x.shape[0]
            logits = x @ gate_w
            scores = jax.nn.softmax(logits, axis=-1)
            topk_w, topk_idx = jax.lax.top_k(scores, K)
            mask = jax.nn.one_hot(topk_idx, E, dtype=scores.dtype).sum(axis=1)
            ce = mask.mean(axis=0)
            Pi = scores.mean(axis=0)
            aux_loss = (Pi * ce * E).sum() * ALPHA
            comb = jnp.zeros((T, E), dtype=x.dtype)
            comb = comb.at[jnp.arange(T)[:, None], topk_idx].add(topk_w)
            g = jax.nn.silu(jnp.einsum('td,edh->teh', x, w_gate)) * jnp.einsum('td,edh->teh', x, w_up)
            routed = jnp.einsum('teh,ehd,te->td', g, w_down, comb)
            shared = jax.nn.silu(x @ sw_gate) * (x @ sw_up) @ sw_down
            out = (routed + shared).reshape(b, s, d)
            return (out, aux_loss)
        out, _aux = _moe_forward(hidden_states, gate_w, w_gate, w_up, w_down, sw_gate, sw_up, sw_down)
        return out
    x = L0_attn_hidden_states
    x = x + _L0_attn_ref(_layernorm(x, axis=-1), L0_attn_freqs_cis, L0_attn_Wq, L0_attn_Wkv_a, L0_attn_kv_gamma, L0_attn_kv_beta, L0_attn_Wkv_b, L0_attn_Wout)
    x = x + _L0_ffn_ref(_layernorm(x, axis=-1), L0_ffn_gate_w, L0_ffn_w_gate, L0_ffn_w_up, L0_ffn_w_down, L0_ffn_sw_gate, L0_ffn_sw_up, L0_ffn_sw_down)
    return x

_drawn_inputs = setup_inputs


def setup_inputs(seed=0):
    import zlib

    import numpy as np

    out = dict(_drawn_inputs(seed))
    spreads = {'L0_attn_kv_gamma': (1.0, 0.6), 'L0_attn_kv_beta': (0.0, 0.415)}
    factors = {'L0_attn_freqs_cis': 8.0,
     'L0_attn_Wq': 8.0,
     'L0_attn_Wkv_a': 4.793,
     'L0_ffn_gate_w': 8.0,
     'L0_ffn_w_gate': 8.0,
     'L0_ffn_w_up': 8.0,
     'L0_ffn_w_down': 8.0,
     'L0_ffn_sw_gate': 2.881,
     'L0_ffn_sw_up': 2.851,
     'L0_ffn_sw_down': 2.845}
    for name, (base, spread) in spreads.items():
        noise = np.random.default_rng([zlib.crc32(name.encode()), seed]).standard_normal(out[name].shape)
        drawn = base * np.exp(spread * noise) if base else spread * noise
        out[name] = jnp.asarray(drawn.astype(out[name].dtype))
    for name, factor in factors.items():
        out[name] = (out[name] * factor).astype(out[name].dtype)
    return out
```

```python
from contextlib import ExitStack

import concourse.bass as bass
from concourse import mybir

F32 = mybir.dt.float32
F32R = mybir.dt.float32r
ALU = mybir.AluOpType
ACT = mybir.ActivationFunctionType
AX = mybir.AxisListType

P = 128
B, S, D = 8, 256, 256
NT = S // P
KD = D // P
NH, DN, DR, DV, RANK = 16, 128, 64, 128, 64
DQK = DN + DR
NP = NH // 2
HR = DR // 2
E, H = 8, 176
EH = E * H
HS = 2 * H
ER = EH // P
ES = -(-HS // P)
CH = ES + ER
LO = 32
CK = LO + E
TOP = 2
SCALE = float(DQK) ** -0.5
EPS = 1e-5
STAGE = 6
WO = 4
TW = 2 * P + 3 * RANK


def chunk_rows(m):
    return min(P, HS - m * P) if m < ES else P


def flat2(t):
    return t[:, :, :].rearrange("p a b -> p (a b)")


class Events:

    def __init__(self, sem, per_round, head=0):
        self.sem, self.per_round, self.head = sem, per_round, head

    def upto(self, i, n):
        return i * self.per_round + (n + self.head)

    def before(self, i, n):
        assert n + self.head - self.per_round >= 1
        return i * self.per_round + (n + self.head - self.per_round)


class AllEvents:

    def __init__(self, nc, ctx):
        def count(name, per_round, head=0):
            return Events(ctx.enter_context(nc.semaphore(name)), per_round, head)

        self.x_loaded = count("x_loaded", 16)
        self.out_stored = count("out_stored", 16, head=16)
        self.q_full = count("q_full", NP)
        self.out_done = count("out_done", NP)
        self.s_full = count("s_full", NH)
        self.t_full = count("t_full", NH)
        self.pv_done = count("pv_done", NH)
        self.gu_full = count("gu_full", CH)
        self.down_done = count("down_done", CH)
        self.cb_full = count("cb_full", ER)
        self.xf_turned = count("xf_turned", 1)
        self.logits_full = count("logits_full", 1)
        self.comb_turned = count("comb_turned", 1)
        self.xa_turned = count("xa_turned", 1)
        self.kv_full = count("kv_full", 1)
        self.k_turned = count("k_turned", 1)
        self.swap_done = count("swap_done", NP)
        self.qhi_done = count("qhi_done", NP)
        self.ohi_done = count("ohi_done", NP)
        self.exp_done = count("exp_done", NH)
        self.phi_done = count("phi_done", NH)
        self.silu_done = count("silu_done", CH)
        self.xfhi_done = count("xfhi_done", 1)
        self.gate_exp_done = count("gate_exp_done", 1)
        self.combhi_done = count("combhi_done", 1)
        self.xahi_done = count("xahi_done", 1)
        self.khi_done = count("khi_done", 1)
        self.qcos_done = count("qcos_done", NP)
        self.qlo_done = count("qlo_done", NP)
        self.olo_done = count("olo_done", NP, head=1)
        self.max_done = count("max_done", NH)
        self.rinv_done = count("rinv_done", NH)
        self.plo_done = count("plo_done", NH)
        self.su_done = count("su_done", CH, head=CH)
        self.cb_done = count("cb_done", ER, head=ER)
        self.x2_done = count("x2_done", 1)
        self.varf_done = count("varf_done", 1)
        self.xhf_done = count("xhf_done", 1)
        self.xflo_done = count("xflo_done", 1)
        self.lmax_done = count("lmax_done", 1)
        self.comb_done = count("comb_done", 1)
        self.osb_done = count("osb_done", 1, head=1)
        self.vara_done = count("vara_done", 1)
        self.xha_done = count("xha_done", 1)
        self.xalo_done = count("xalo_done", 1)
        self.vark_done = count("vark_done", 1)
        self.kn_done = count("kn_done", 1)
        self.kr_done = count("kr_done", 1)
        self.klo_done = count("klo_done", 1)
        self.ffn_step = count("ffn_step", 9)
        self.prep_step = count("prep_step", 4)
        self.qrot_part = count("qrot_part", NP)
        self.qrot_done = count("qrot_done", NP)
        self.pn_done = count("pn_done", NH)
        self.uhi_done = count("uhi_done", CH)
        self.ulo_done = count("ulo_done", CH)
        self.rsf_done = count("rsf_done", 1)
        self.rsa_done = count("rsa_done", 1)
        self.rsk_done = count("rsk_done", 1)
        self.kp_part = count("kp_part", 1)
        self.kp_done = count("kp_done", 1)
        self.kvhi_done = count("kvhi_done", 1)
        self.kvlo_done = count("kvlo_done", 1)
        self.latent_zero = ctx.enter_context(nc.semaphore("latent_zero"))
        self.ones_set = ctx.enter_context(nc.semaphore("ones_set"))


class Layer:

    def __init__(self, nc, ctx):
        def sb(name, shape, dt=F32):
            return ctx.enter_context(nc.sbuf_tensor(name, shape, dt))

        def bank(name):
            return ctx.enter_context(nc.psum_tensor(name, [P, 2, S], F32))

        self.events = AllEvents(nc, ctx)
        self.wq_hi, self.wq_lo = (sb(f"wq_{x}", [P, KD, NH, P], F32R) for x in ("hi", "lo"))
        self.wo_hi, self.wo_lo = (sb(f"wo_{x}", [P, NP, D], F32R) for x in ("hi", "lo"))
        self.wkva_hi, self.wkva_lo = (sb(f"wkva_{x}", [P, KD, RANK + DR], F32R) for x in ("hi", "lo"))
        self.gw_hi, self.gw_lo = (sb(f"gw_{x}", [P, KD, E], F32R) for x in ("hi", "lo"))
        self.mg_hi, self.mg_lo = (sb(f"mg_{x}", [P, KD, EH], F32R) for x in ("hi", "lo"))
        self.mu_hi, self.mu_lo = (sb(f"mu_{x}", [P, KD, EH], F32R) for x in ("hi", "lo"))
        self.md_hi, self.md_lo = (sb(f"md_{x}", [P, ER, D], F32R) for x in ("hi", "lo"))
        self.sgu_hi, self.sgu_lo = (sb(f"sgu_{x}", [P, 2 * KD, HS], F32R) for x in ("hi", "lo"))
        self.sd_hi, self.sd_lo = (sb(f"sd_{x}", [P, ES, D], F32R) for x in ("hi", "lo"))
        self.ident = sb("ident", [P, P])
        self.sel = sb("sel", [CK, EH], F32R)
        self.qcos = sb("qcos", [P, S])
        self.qsin = sb("qsin", [P, S])
        self.kcos = sb("kcos", [P, NT, HR])
        self.ksin = sb("ksin", [P, NT, HR])
        self.gamma = sb("gamma", [P, RANK])
        self.beta = sb("beta", [P, RANK])
        self.minus_half = sb("minus_half", [P, NT])
        self.sentinel = sb("sentinel", [P, E])
        self.ps_q = [bank(f"ps_q{n}") for n in range(2)]
        self.ps_s = [bank(f"ps_s{n}") for n in range(2)]
        self.ps_t = [bank(f"ps_t{n}") for n in range(2)]
        self.ps_o = bank("ps_o")
        self.ps_y = bank("ps_y")


def weights(nc, L, d):
    with ExitStack() as ctx:
        def sb(name, shape, dt=F32):
            return ctx.enter_context(nc.sbuf_tensor(name, shape, dt))

        def sem(name):
            return ctx.enter_context(nc.semaphore(name))

        wq_raw = sb("wq_raw", [P, KD, NH, DQK])
        wkvb_raw = sb("wkvb_raw", [RANK, NH, DN + DV])
        wout_raw = [sb(f"wout_raw{n}", [P, WO, D]) for n in range(2)]
        small_raw = sb("small_raw", [P, KD, RANK + DR + E])
        stage = sb("stage", [P, STAGE * D])
        turned = [sb(f"turned{n}", [P, TW]) for n in range(2)]
        theta = sb("theta", [P, NT, 4, HR])
        turns = sb("turns", [P, NT, 4, HR])
        angle = sb("angle", [P, NT, 4, HR])
        cos4 = sb("cos4", [P, NT, 4, HR])
        sin4 = sb("sin4", [P, NT, 4, HR])
        sel_f = stage[0:CK, 0:EH]

        theta_in, small_in, wkvb_in, wq_in = map(sem, ("theta_in", "small_in", "wkvb_in", "wq_in"))
        wout_in = [sem(f"wout_in{n}") for n in range(2)]
        stage_in, stage_hi, stage_used = map(sem, ("stage_in", "stage_hi", "stage_used"))
        ident_step, sel_step, rope_hi = map(sem, ("ident_step", "sel_step", "rope_hi"))
        w_turned, w_evac, w_full, whi_done, wlo_done = map(sem, ("w_turned", "w_evac", "w_full", "whi_done", "wlo_done"))
        angle_step, angle_done, cos_angle, sin_done, cos_done, trig_turned, small_hi = map(
            sem, ("angle_step", "angle_done", "cos_angle", "sin_done", "cos_done", "trig_turned", "small_hi"))

        per_e = "p (e h) -> p e h"
        tail = HS - (ES - 1) * P
        cut = (ES - 1) * D
        down_rows = d["w_down"].rearrange("e h n -> (e h) n").rearrange("(c p) n -> p c n", p=P)
        staged = [
            ([(stage[:, 0:EH].rearrange(per_e, e=E), src[:, k * P:(k + 1) * P, :].rearrange("e p h -> p e h"))],
             [(hi[:, k, :], lo[:, k, :], stage[:, 0:EH])])
            for src, hi, lo in ((d["w_gate"], L.mg_hi, L.mg_lo), (d["w_up"], L.mu_hi, L.mu_lo)) for k in range(KD)
        ] + [
            ([(stage[:, 0:(to - at) * D].rearrange("p (c n) -> p c n", n=D), down_rows[:, at:to, :])],
             [(flat2(L.md_hi)[:, at * D:to * D], flat2(L.md_lo)[:, at * D:to * D], stage[:, 0:(to - at) * D])])
            for at, to in ((0, STAGE), (STAGE, ER))
        ] + [
            ([(stage[:, n * KD * HS:(n + 1) * KD * HS].rearrange("p (k h) -> p k h", k=KD),
               src.rearrange("(k p) h -> p k h", p=P)) for n, src in enumerate((d["sw_gate"], d["sw_up"]))],
             [(flat2(L.sgu_hi), flat2(L.sgu_lo), stage[:, 0:2 * KD * HS])]),
            ([(stage[:, 0:cut].rearrange("p (c n) -> p c n", c=ES - 1),
               d["sw_down"][0:(ES - 1) * P, :].rearrange("(c p) n -> p c n", p=P)),
              (stage[0:tail, cut:cut + D], d["sw_down"][(ES - 1) * P:HS, :])],
             [(flat2(L.sd_hi)[:, 0:cut], flat2(L.sd_lo)[:, 0:cut], stage[:, 0:cut]),
              (L.sd_hi[0:tail, ES - 1, :], L.sd_lo[0:tail, ES - 1, :], stage[0:tail, cut:cut + D])]),
        ]

        with nc.Block() as block:
            @block.sync
            def _(sp):
                for r in range(4):
                    sp.dma_start(theta[:, :, r, :], d["freqs"].rearrange("(j p) f -> p j f", p=P)).then_inc(theta_in, 16)
                sp.dma_start(wkvb_raw[:, :, :], d["Wkv_b"].rearrange("c (h n) -> c h n", h=NH)).then_inc(wkvb_in, 16)
                for k in range(KD):
                    sp.dma_start(wq_raw[:, k, :, :],
                                 d["Wq"][k * P:(k + 1) * P, :].rearrange("p (h n) -> p h n", h=NH)).then_inc(wq_in, 16)
                for g in range(NH // WO):
                    if g >= 2:
                        sp.wait_ge(w_full, WO * (g - 1))
                    sp.dma_start(wout_raw[g % 2][:, :, :], d["Wout"].rearrange("(h n) m -> n h m", n=DV)[:, g * WO:(g + 1) * WO, :]
                                 ).then_inc(wout_in[g % 2], 16)
                for events in (L.events.su_done, L.events.cb_done, L.events.olo_done, L.events.osb_done, L.events.out_stored):
                    sp.sem_inc(events.sem, events.head)

            @block.scalar
            def _(act):
                act.dma_start(small_raw[:, :, 0:RANK + DR], d["Wkv_a"].rearrange("(k p) n -> p k n", p=P)).then_inc(small_in, 16)
                act.dma_start(small_raw[:, :, RANK + DR:], d["gate_w"].rearrange("(k p) n -> p k n", p=P)).then_inc(small_in, 16)
                act.dma_start(L.gamma[:, :], d["gamma"].partition_broadcast(P)).then_inc(small_in, 16)
                act.dma_start(L.beta[:, :], d["beta"].partition_broadcast(P)).then_inc(small_in, 16)
                act.wait_ge(angle_done, 1)
                nc.scalar.activation(sin4[:, :, :, :], angle[:, :, :, :], ACT.Sin).then_inc(sin_done, 1)
                act.wait_ge(cos_angle, 1)
                nc.scalar.activation(cos4[:, :, :, :], turns[:, :, :, :], ACT.Sin).then_inc(cos_done, 1)
                act.wait_ge(small_in, 64)
                nc.scalar.activation(L.wkva_hi[:, :, :], small_raw[:, :, 0:RANK + DR], ACT.Copy).then_inc(small_hi, 1)
                nc.scalar.activation(L.gw_hi[:, :, :], small_raw[:, :, RANK + DR:], ACT.Copy).then_inc(small_hi, 1)

                def evacuate(h):
                    act.wait_ge(w_turned, h + 1)
                    if h >= 2:
                        act.wait_ge(w_full, h - 1)
                    nc.scalar.activation(turned[h % 2][:, :], flat2(L.ps_t[h % 2])[:, 0:TW], ACT.Copy).then_inc(w_evac, 1)

                evacuate(0)
                for h in range(NH):
                    if h + 1 < NH:
                        evacuate(h + 1)
                    act.wait_ge(w_full, h + 1)
                    prod = flat2(L.ps_s[h % 2])
                    rows = slice(RANK * (h % 2), RANK * (h % 2) + RANK)
                    nc.scalar.activation(L.wq_hi[:, :, h, 0:RANK], prod[:, 0:KD * RANK].rearrange("p (k c) -> p k c", k=KD), ACT.Copy)
                    nc.scalar.activation(L.wo_hi[rows, h // 2, :], prod[rows, KD * RANK:KD * RANK + D], ACT.Copy).then_inc(whi_done, 1)

            @block.tensor
            def _(pe):
                pe.wait_ge(ident_step, 2)
                pe.wait_ge(sin_done, 1)
                pe.wait_ge(cos_done, 1)
                for n, trig in enumerate((cos4, sin4)):
                    for j in range(NT):
                        last = nc.tensor.transpose(L.ps_q[n][:, 0, j * P:(j + 1) * P],
                                                   trig[:, j, :, :].rearrange("p r f -> p (r f)"), L.ident[:, :])
                last.then_inc(trig_turned, 1)
                pe.wait_ge(wkvb_in, 16)
                pe.wait_ge(wq_in, 16 * KD)

                def turn(h):
                    if h >= 2:
                        pe.wait_ge(w_evac, h - 1)
                    to = flat2(L.ps_t[h % 2])
                    for k in range(KD):
                        nc.tensor.transpose(to[:, k * P:(k + 1) * P], wq_raw[:, k, h, 0:DN], L.ident[:, :])
                    at = KD * P
                    for part in (0, DN, DN):
                        last = nc.tensor.transpose(to[:, at:at + RANK], wkvb_raw[:, h, part:part + DN], L.ident[0:RANK, 0:RANK])
                        at += RANK
                    last.then_inc(w_turned, 1)

                turn(0)
                for h in range(NH):
                    if h + 1 < NH:
                        turn(h + 1)
                    pe.wait_ge(w_evac, h + 1)
                    if h >= 2:
                        pe.wait_ge(wlo_done, h - 1)
                    g = h // WO
                    pe.wait_ge(wout_in[g % 2], 16 * (g // 2 + 1))
                    to, t = flat2(L.ps_s[h % 2]), turned[h % 2]
                    for k in range(KD):
                        nc.tensor.matmul(to[:, k * RANK:(k + 1) * RANK], t[:, k * P:(k + 1) * P],
                                         t[:, KD * P:KD * P + RANK], start=True, stop=True)
                    nc.tensor.matmul(to[:, KD * RANK:KD * RANK + D], t[:, KD * P + RANK:TW], wout_raw[g % 2][:, h % WO, :],
                                     start=True, stop=True).then_inc(w_full, 1)

            @block.vector
            def _(dve):
                nc.vector.memset(L.minus_half[:, :], -0.5)
                for n in range(E):
                    nc.vector.memset(L.sentinel[:, n:n + 1], -1.0 - n)
                nc.vector.memset(L.qcos[0:RANK, :], SCALE)
                nc.vector.memset(L.qsin[0:RANK, :], 0.0)
                steps = 0

                def step(ins):
                    nonlocal steps
                    steps += 1
                    ins.then_inc(angle_step, 1)
                    dve.wait_ge(angle_step, steps)

                two_pi, first, second = 6.283185307179586, 6.28125, 1.93500518798828125e-3
                to_round = 12582912.0
                th, tu, an = (t[:, :, :, :].rearrange("p j r f -> p (j r f)") for t in (theta, turns, angle))
                dve.wait_ge(theta_in, 64)
                step(nc.vector.tensor_scalar(tu, th, 1.0 / two_pi, to_round, ALU.mult, ALU.add))
                step(nc.vector.tensor_scalar(tu, tu, -to_round, None, ALU.add))
                step(nc.vector.scalar_tensor_tensor(an, tu, -first, th, ALU.mult, ALU.add))
                step(nc.vector.scalar_tensor_tensor(an, tu, -second, an, ALU.mult, ALU.add))
                step(nc.vector.scalar_tensor_tensor(an, tu, -(two_pi - first - second), an, ALU.mult, ALU.add))
                nc.vector.tensor_scalar(an, an, 3.1415925, -3.1415925, ALU.min, ALU.max).then_inc(angle_done, 1)
                dve.wait_ge(angle_done, 1)
                step(nc.vector.scalar_tensor_tensor(tu, an, -1.0, an, ALU.mult, ALU.min))
                nc.vector.tensor_scalar(tu, tu, two_pi / 4, None, ALU.add).then_inc(cos_angle, 1)
                dve.wait_ge(trig_turned, 1)
                even, odd = slice(RANK, RANK + HR), slice(RANK + HR, RANK + DR)
                nc.vector.tensor_scalar(L.qcos[RANK:P, :], L.ps_q[0][RANK:P, 0, :], SCALE, None, ALU.mult)
                nc.vector.tensor_scalar(L.qsin[even, :], L.ps_q[1][even, 0, :], -SCALE, None, ALU.mult)
                nc.vector.tensor_scalar(L.qsin[odd, :], L.ps_q[1][odd, 0, :], SCALE, None, ALU.mult)
                dve.wait_ge(sin_done, 1)
                dve.wait_ge(cos_done, 1)
                nc.vector.tensor_copy(L.kcos[:, :, :], cos4[:, :, 0, :])
                nc.vector.tensor_copy(L.ksin[:, :, :], sin4[:, :, 0, :])
                dve.wait_ge(small_hi, 2)
                nc.vector.tensor_tensor(L.wkva_lo[:, :, :], small_raw[:, :, 0:RANK + DR], L.wkva_hi[:, :, :].bitcast(F32), ALU.subtract)
                nc.vector.tensor_tensor(L.gw_lo[:, :, :], small_raw[:, :, RANK + DR:], L.gw_hi[:, :, :].bitcast(F32), ALU.subtract)
                for h in range(NH):
                    dve.wait_ge(whi_done, h + 1)
                    prod = flat2(L.ps_s[h % 2])
                    rows = slice(RANK * (h % 2), RANK * (h % 2) + RANK)
                    nc.vector.tensor_tensor(L.wq_lo[:, :, h, 0:RANK], prod[:, 0:KD * RANK].rearrange("p (k c) -> p k c", k=KD),
                                            L.wq_hi[:, :, h, 0:RANK].bitcast(F32), ALU.subtract)
                    nc.vector.tensor_tensor(L.wo_lo[rows, h // 2, :], prod[rows, KD * RANK:KD * RANK + D],
                                            L.wo_hi[rows, h // 2, :].bitcast(F32), ALU.subtract).then_inc(wlo_done, 1)

            @block.gpsimd
            def _(pool):
                nc.gpsimd.memset(L.ident[:, :], 0.0).then_inc(ident_step, 1)
                pool.wait_ge(ident_step, 1)
                nc.gpsimd.affine_select(out=L.ident[:, :], in_=L.ident[:, :], compare_op=ALU.not_equal, fill=1.0, base=0,
                                        pattern=[[-1, P]], channel_multiplier=1).then_inc(ident_step, 1)
                nc.gpsimd.memset(sel_f, 0.0).then_inc(sel_step, 1)
                pool.wait_ge(sel_step, 1)
                for row in (0, LO):
                    nc.gpsimd.memset(stage[row:row + E, 0:EH], 1.0).then_inc(sel_step, 1)
                pool.wait_ge(sel_step, 3)
                for row in (0, LO):
                    part = stage[row:row + E, 0:EH]
                    nc.gpsimd.affine_select(out=part, in_=part, compare_op=ALU.is_ge, fill=0.0, base=0,
                                            pattern=[[1, EH]], channel_multiplier=-H).then_inc(sel_step, 1)
                pool.wait_ge(sel_step, 5)
                for row in (0, LO):
                    part = stage[row:row + E, 0:EH]
                    nc.gpsimd.affine_select(out=part, in_=part, compare_op=ALU.is_ge, fill=0.0, base=H - 1,
                                            pattern=[[-1, EH]], channel_multiplier=H).then_inc(sel_step, 1)
                pool.wait_ge(sel_step, 7)
                nc.gpsimd.tensor_copy(L.sel[:, :], sel_f).then_inc(sel_step, 1)
                pool.wait_ge(sel_step, 8)
                pool.wait_ge(wq_in, 16 * KD)
                for k in range(KD):
                    for odd in range(2):
                        src = wq_raw[:, k, :, DN + odd:DQK:2]
                        cols = slice(RANK + odd * HR, RANK + (odd + 1) * HR)
                        nc.gpsimd.tensor_copy(L.wq_hi[:, k, :, cols], src).then_inc(rope_hi, 1)
                        pool.wait_ge(rope_hi, 2 * k + odd + 1)
                        nc.gpsimd.tensor_tensor(L.wq_lo[:, k, :, cols], src, L.wq_hi[:, k, :, cols].bitcast(F32), ALU.subtract)
                loaded, his = 0, 0
                for n, (loads, splits) in enumerate(staged):
                    for to, src in loads:
                        pool.dma_start(to, src).then_inc(stage_in, 16)
                    loaded += 16 * len(loads)
                    pool.wait_ge(stage_in, loaded)
                    for hi, _, src in splits:
                        nc.gpsimd.tensor_copy(hi, src).then_inc(stage_hi, 1)
                        his += 1
                    pool.wait_ge(stage_hi, his)
                    for hi, lo, src in splits:
                        last = nc.gpsimd.tensor_tensor(lo, src, hi.bitcast(F32), ALU.subtract)
                    last.then_inc(stage_used, 1)
                    pool.wait_ge(stage_used, n + 1)


def loop(nc, L, d):
    ev = L.events
    with ExitStack() as ctx:
        def sb(name, shape, dt=F32):
            return ctx.enter_context(nc.sbuf_tensor(name, shape, dt))

        xin = sb("xin", [P, NT, D])
        xhat = sb("xhat", [P, NT, D])
        x2 = sb("x2", [P, NT, D])
        bn = sb("bn", [P, NT, 6])
        one = sb("one", [P, 1])
        carrier = sb("carrier", [P, 1])
        mean_a, mean_k, mean_f = (sb(f"mean_{x}", [P, NT, 2]) for x in "akf")
        var_a, var_k, var_f = (sb(f"var_{x}", [P, NT]) for x in "akf")
        rstd_a, rstd_k, rstd_f = (sb(f"rstd_{x}", [P, NT]) for x in "akf")
        xa_hi, xa_lo = (sb(f"xa_{x}", [P, KD, S], F32R) for x in ("hi", "lo"))
        xf_hi, xf_lo = (sb(f"xf_{x}", [P, KD, S], F32R) for x in ("hi", "lo"))
        kp = sb("kp", [P, NT, P])
        krot = sb("krot", [P, 4, NT, HR])
        kT_hi, kT_lo = (sb(f"kT_{x}", [P, S], F32R) for x in ("hi", "lo"))
        kv_hi, kv_lo = (sb(f"kv_{x}", [P, NT, 2, RANK], F32R) for x in ("hi", "lo"))
        qswap = sb("qswap", [P, 2, S])
        qf = sb("qf", [P, 2, S])
        q_hi, q_lo = ([sb(f"q_{x}{n}", [P, 2, S], F32R) for n in range(2)] for x in ("hi", "lo"))
        nmax = sb("nmax", [P, NH, NT])
        rsum = sb("rsum", [P, NH, NT])
        rinv = sb("rinv", [P, NH, NT])
        probs = [sb(f"probs{n}", [P, NT, S]) for n in range(3)]
        pT_hi, pT_lo = ([sb(f"pT_{x}{n}", [P, NT, S], F32R) for n in range(3)] for x in ("hi", "lo"))
        o_hi, o_lo = ([sb(f"o_{x}{n}", [P, S], F32R) for n in range(2)] for x in ("hi", "lo"))
        lmax = sb("lmax", [P, NT])
        esum = sb("esum", [P, NT])
        einv = sb("einv", [P, NT])
        eprob = sb("eprob", [P, NT, E])
        score = sb("score", [P, NT, 2 * E])
        top = sb("top", [P, NT, E])
        rest = sb("rest", [P, NT, 2 * E])
        comb = sb("comb", [P, NT, E])
        comb2 = sb("comb2", [P, NT, P])
        cT = sb("cT", [CK, S], F32R)
        gate = [sb(f"gate{n}", [P, S]) for n in range(2)]
        prod = [sb(f"prod{n}", [P, S]) for n in range(2)]
        unit = [sb(f"unit{n}", [P, S]) for n in range(2)]
        u_hi, u_lo = ([t[:, 0, :] for t in ring] for ring in (pT_hi, pT_lo))

        half = (slice(0, RANK), slice(RANK, P))
        even, odd = slice(RANK, RANK + HR), slice(RANK + HR, P)

        def three(out, pairs, start=True, stop=True, skip=False):
            last = None
            terms = [t for sh, sl, mh, ml in pairs for t in ((sh, mh), (sh, ml), (sl, mh))]
            for n, (stat, mov) in enumerate(terms):
                last = nc.tensor.matmul(out, stat, mov, start=start and n == 0, stop=stop and n == len(terms) - 1,
                                        skip_group_check=skip)
            return last

        def tile(j):
            return slice(j * P, (j + 1) * P)

        block = ctx.enter_context(nc.Block())

        @block.sync
        def _(sp):
            by_token = "(j p) m -> p j m"
            sp.dma_start(xin[:, :, :], d["x"][0, :, :].rearrange(by_token, p=P)).then_inc(ev.x_loaded.sem, 16)

            def store(i):
                sp.wait_ge(ev.osb_done.sem, ev.osb_done.upto(i, 1))
                sp.dma_start(d["out"][bass.ds(i, 1), :, :].rearrange("b (j p) m -> p (b j) m", p=P),
                             x2[:, :, :]).then_inc(ev.out_stored.sem, 16)

            with sp.Fori(0, B - 1) as i:
                sp.wait_ge(ev.x2_done.sem, ev.x2_done.upto(i, 1))
                sp.dma_start(xin[:, :, :], d["x"][bass.ds(i + 1, 1), :, :].rearrange("b (j p) m -> p (b j) m", p=P)
                             ).then_inc(ev.x_loaded.sem, 16)
                store(i)
            store(B - 1)
            sp.wait_ge(ev.out_stored.sem, ev.out_stored.upto(B - 1, 16))

        @block.tensor
        def _(pe):
            def prep_turn(r):
                pe.wait_ge(ev.xha_done.sem, ev.xha_done.upto(r, 1))
                for k in range(KD):
                    for j in range(NT):
                        last = nc.tensor.transpose(L.ps_t[0][:, k, tile(j)], xhat[:, j, tile(k)], L.ident[:, :])
                last.then_inc(ev.xa_turned.sem, 1)

            def prep_kv(r):
                pe.wait_ge(ev.xahi_done.sem, ev.xahi_done.upto(r, 1))
                pe.wait_ge(ev.xalo_done.sem, ev.xalo_done.upto(r, 1))
                for j in range(NT):
                    last = three(L.ps_t[1][:, 0, tile(j)],
                                 [(xa_hi[:, k, tile(j)], xa_lo[:, k, tile(j)], L.wkva_hi[:, k, :], L.wkva_lo[:, k, :])
                                  for k in range(KD)])
                last.then_inc(ev.kv_full.sem, 1)

            def prep_k(r):
                pe.wait_ge(ev.kp_done.sem, ev.kp_done.upto(r, 1))
                for j in range(NT):
                    last = nc.tensor.transpose(L.ps_t[0][:, 0, tile(j)], kp[:, j, :], L.ident[:, :])
                last.then_inc(ev.k_turned.sem, 1)

            def query(i, p):
                if p < 2:
                    pe.wait_ge(ev.su_done.sem, ev.su_done.before(i, CH - 1 + p))
                else:
                    pe.wait_ge(ev.qcos_done.sem, ev.qcos_done.upto(i, p - 1))
                for n in range(2):
                    h = 2 * p + n
                    last = three(L.ps_q[p % 2][:, n, :],
                                 [(L.wq_hi[:, k, h, :], L.wq_lo[:, k, h, :], xa_hi[:, k, :], xa_lo[:, k, :]) for k in range(KD)])
                last.then_inc(ev.q_full.sem, 1)

            def scores(i, h):
                p, n = divmod(h, 2)
                pe.wait_ge(ev.qlo_done.sem, ev.qlo_done.upto(i, p + 1))
                if h == 0:
                    pe.wait_ge(ev.klo_done.sem, ev.klo_done.upto(i, 1))
                if h < 2:
                    pe.wait_ge(ev.cb_done.sem, ev.cb_done.before(i, ER))
                else:
                    pe.wait_ge(ev.exp_done.sem, ev.exp_done.upto(i, h - 1))
                for j in range(NT):
                    last = three(L.ps_s[h % 2][:, j, :],
                                 [(q_hi[p % 2][:, n, tile(j)], q_lo[p % 2][:, n, tile(j)], kT_hi[:, :], kT_lo[:, :])])
                last.then_inc(ev.s_full.sem, 1)

            def turn(i, h):
                pe.wait_ge(ev.pn_done.sem, ev.pn_done.upto(i, h + 1))
                if h == 0:
                    pe.wait_ge(ev.klo_done.sem, ev.klo_done.upto(i, 1))
                elif h == 1:
                    pe.wait_ge(ev.kn_done.sem, ev.kn_done.upto(i, 1))
                else:
                    pe.wait_ge(ev.plo_done.sem, ev.plo_done.upto(i, h - 1))
                for c in range(NT):
                    for j in range(NT):
                        last = nc.tensor.transpose(L.ps_t[h % 2][:, c, tile(j)], probs[h % 3][:, j, tile(c)], L.ident[:, :])
                last.then_inc(ev.t_full.sem, 1)

            def attend(i, h):
                p, n = divmod(h, 2)
                pe.wait_ge(ev.plo_done.sem, ev.plo_done.upto(i, h + 1))
                if n == 0:
                    pe.wait_ge(ev.olo_done.sem, ev.olo_done.upto(i, p))
                if h == 0:
                    pe.wait_ge(ev.kvlo_done.sem, ev.kvlo_done.upto(i, 1))
                twice = "p n c -> p (n c)"
                last = three(L.ps_o[:, n, :],
                             [(kv_hi[:, c, :, :].rearrange(twice), kv_lo[:, c, :, :].rearrange(twice),
                               pT_hi[h % 3][:, c, :], pT_lo[h % 3][:, c, :]) for c in range(NT)])
                last.then_inc(ev.pv_done.sem, 1)

            def project(i, p):
                pe.wait_ge(ev.olo_done.sem, ev.olo_done.upto(i, p + 1))
                if p == 0:
                    pe.wait_ge(ev.osb_done.sem, ev.osb_done.before(i, 1))
                for j in range(NT):
                    last = three(L.ps_y[:, j, :], [(o_hi[p % 2][:, tile(j)], o_lo[p % 2][:, tile(j)], L.wo_hi[:, p, :], L.wo_lo[:, p, :])],
                                 start=p == 0 and j == 0, stop=p == NP - 1, skip=True)
                last.then_inc(ev.out_done.sem, 1)

            def attention(i):
                pe.wait_ge(ev.xalo_done.sem, ev.xalo_done.upto(i, 1))
                query(i, 0)
                query(i, 1)
                for p in range(NP + 4):
                    if p < NP:
                        scores(i, 2 * p)
                    if 3 <= p < NP + 3:
                        project(i, p - 3)
                    if 1 <= p < NP + 1:
                        turn(i, 2 * p - 2)
                    if 2 <= p < NP + 2:
                        attend(i, 2 * p - 4)
                        attend(i, 2 * p - 3)
                    if p < NP:
                        scores(i, 2 * p + 1)
                    if p + 2 < NP:
                        query(i, p + 2)
                    if 1 <= p < NP + 1:
                        turn(i, 2 * p - 1)

            def gate_up(i, m):
                if m < 2:
                    pe.wait_ge(ev.qcos_done.sem, ev.qcos_done.upto(i, NP - 1 + m))
                else:
                    pe.wait_ge(ev.su_done.sem, ev.su_done.upto(i, m - 1))
                rows = chunk_rows(m)
                for n in range(2):
                    if m < ES:
                        cols = slice(m * P, m * P + rows)
                        w = [(L.sgu_hi[:, n * KD + k, cols], L.sgu_lo[:, n * KD + k, cols]) for k in range(KD)]
                    else:
                        hi, lo = ((L.mg_hi, L.mg_lo), (L.mu_hi, L.mu_lo))[n]
                        w = [(hi[:, k, tile(m - ES)], lo[:, k, tile(m - ES)]) for k in range(KD)]
                    last = three(L.ps_q[m % 2][0:rows, n, :],
                                 [(*w[k], xf_hi[:, k, :], xf_lo[:, k, :]) for k in range(KD)])
                last.then_inc(ev.gu_full.sem, 1)

            def spread(i, m):
                c = m - ES
                if c == 0:
                    pe.wait_ge(ev.combhi_done.sem, ev.combhi_done.upto(i, 1))
                if c >= 2:
                    pe.wait_ge(ev.cb_done.sem, ev.cb_done.upto(i, c - 1))
                nc.tensor.matmul(L.ps_s[c % 2][:, 0, :], L.sel[:, tile(c)], cT[:, :], start=True, stop=True
                                 ).then_inc(ev.cb_full.sem, 1)

            def down(i, m):
                pe.wait_ge(ev.ulo_done.sem, ev.ulo_done.upto(i, m + 1))
                if m == 0:
                    pe.wait_ge(ev.x2_done.sem, ev.x2_done.upto(i, 1))
                rows = chunk_rows(m)
                hi, lo, c = (L.sd_hi, L.sd_lo, m) if m < ES else (L.md_hi, L.md_lo, m - ES)
                for j in range(NT):
                    last = three(L.ps_y[:, j, :], [(u_hi[m % 3][0:rows, tile(j)], u_lo[m % 3][0:rows, tile(j)],
                                                    hi[0:rows, c, :], lo[0:rows, c, :])],
                                 start=m == 0 and j == 0, stop=m == CH - 1, skip=True)
                last.then_inc(ev.down_done.sem, 1)

            def experts(i, prep):
                pe.wait_ge(ev.xhf_done.sem, ev.xhf_done.upto(i, 1))
                pe.wait_ge(ev.plo_done.sem, ev.plo_done.upto(i, NH))
                for k in range(KD):
                    for j in range(NT):
                        last = nc.tensor.transpose(L.ps_t[0][:, k, tile(j)], xhat[:, j, tile(k)], L.ident[:, :])
                last.then_inc(ev.xf_turned.sem, 1)
                pe.wait_ge(ev.xfhi_done.sem, ev.xfhi_done.upto(i, 1))
                pe.wait_ge(ev.xflo_done.sem, ev.xflo_done.upto(i, 1))
                pe.wait_ge(ev.exp_done.sem, ev.exp_done.upto(i, NH))
                for j in range(NT):
                    last = three(L.ps_s[0][:, 0, j * E:(j + 1) * E],
                                 [(xf_hi[:, k, tile(j)], xf_lo[:, k, tile(j)], L.gw_hi[:, k, :], L.gw_lo[:, k, :]) for k in range(KD)])
                last.then_inc(ev.logits_full.sem, 1)
                for m in range(CH + 2):
                    if m < CH:
                        gate_up(i, m)
                    if m == ES - 1:
                        pe.wait_ge(ev.comb_done.sem, ev.comb_done.upto(i, 1))
                        for j in range(NT):
                            last = nc.tensor.transpose(L.ps_s[1][:, 0, tile(j)], comb2[:, j, :], L.ident[:, :])
                        last.then_inc(ev.comb_turned.sem, 1)
                    if ES <= m < CH:
                        spread(i, m)
                    if m >= 2:
                        down(i, m - 2)
                    if prep:
                        if m == 4:
                            prep_turn(i + 1)
                        if m == 6:
                            prep_kv(i + 1)
                        if m == 11:
                            prep_k(i + 1)

            prep_turn(0)
            prep_kv(0)
            prep_k(0)
            with pe.Fori(0, B - 1) as i:
                attention(i)
                experts(i, True)
            attention(B - 1)
            experts(B - 1, False)

        @block.scalar
        def _(act):
            copy = lambda out, src: nc.scalar.activation(out, src, ACT.Copy)

            def prep_x(r):
                act.wait_ge(ev.xa_turned.sem, ev.xa_turned.upto(r, 1))
                copy(xa_hi[:, :, :], L.ps_t[0][:, :, :]).then_inc(ev.xahi_done.sem, 1)

            def prep_k(r):
                act.wait_ge(ev.k_turned.sem, ev.k_turned.upto(r, 1))
                copy(kT_hi[:, :], L.ps_t[0][:, 0, :]).then_inc(ev.khi_done.sem, 1)

            def swap(i, p):
                act.wait_ge(ev.q_full.sem, ev.q_full.upto(i, p + 1))
                if p >= 1:
                    act.wait_ge(ev.qrot_done.sem, ev.qrot_done.upto(i, p))
                copy(qswap[even, :, :], L.ps_q[p % 2][odd, :, :])
                copy(qswap[odd, :, :], L.ps_q[p % 2][even, :, :]).then_inc(ev.swap_done.sem, 1)

            def query_hi(i, p):
                act.wait_ge(ev.qrot_done.sem, ev.qrot_done.upto(i, p + 1))
                if p >= 2:
                    act.wait_ge(ev.s_full.sem, ev.s_full.upto(i, 2 * p - 2))
                copy(q_hi[p % 2][:, :, :], qf[:, :, :]).then_inc(ev.qhi_done.sem, 1)

            def exps(i, h):
                act.wait_ge(ev.max_done.sem, ev.max_done.upto(i, h + 1))
                if h >= 3:
                    act.wait_ge(ev.t_full.sem, ev.t_full.upto(i, h - 2))
                for j in range(NT):
                    last = nc.scalar.activation(probs[h % 3][:, j, :], L.ps_s[h % 2][:, j, :], ACT.Exp,
                                                bias=nmax[:, h, j:j + 1], accum_out=rsum[:, h, j:j + 1])
                last.then_inc(ev.exp_done.sem, 1)

            def probs_hi(i, h):
                act.wait_ge(ev.t_full.sem, ev.t_full.upto(i, h + 1))
                if h >= 3:
                    act.wait_ge(ev.pv_done.sem, ev.pv_done.upto(i, h - 2))
                copy(pT_hi[h % 3][:, :, :], L.ps_t[h % 2][:, :, :]).then_inc(ev.phi_done.sem, 1)

            def attended_hi(i, p):
                act.wait_ge(ev.pv_done.sem, ev.pv_done.upto(i, 2 * p + 2))
                if p >= 2:
                    act.wait_ge(ev.out_done.sem, ev.out_done.upto(i, p - 1))
                for n in range(2):
                    last = copy(o_hi[p % 2][half[n], :], L.ps_o[half[n], n, :])
                last.then_inc(ev.ohi_done.sem, 1)

            def attention(i):
                swap(i, 0)
                query_hi(i, 0)
                swap(i, 1)
                for p in range(NP + 3):
                    if 2 <= p < NP + 2:
                        probs_hi(i, 2 * p - 3)
                    if p < NP:
                        exps(i, 2 * p)
                    if 1 <= p < NP + 1:
                        probs_hi(i, 2 * p - 2)
                    if 2 <= p < NP + 2:
                        attended_hi(i, p - 2)
                    if p + 1 < NP:
                        query_hi(i, p + 1)
                    if p < NP:
                        exps(i, 2 * p + 1)
                    if p + 2 < NP:
                        swap(i, p + 2)

            def experts(i, prep):
                act.wait_ge(ev.xf_turned.sem, ev.xf_turned.upto(i, 1))
                copy(xf_hi[:, :, :], L.ps_t[0][:, :, :]).then_inc(ev.xfhi_done.sem, 1)
                act.wait_ge(ev.lmax_done.sem, ev.lmax_done.upto(i, 1))
                for j in range(NT):
                    last = nc.scalar.activation(eprob[:, j, :], L.ps_s[0][:, 0, j * E:(j + 1) * E], ACT.Exp,
                                                bias=lmax[:, j:j + 1], accum_out=esum[:, j:j + 1])
                last.then_inc(ev.gate_exp_done.sem, 1)
                for m in range(CH):
                    act.wait_ge(ev.gu_full.sem, ev.gu_full.upto(i, m + 1))
                    if m >= 2:
                        act.wait_ge(ev.su_done.sem, ev.su_done.upto(i, m - 1))
                    rows = chunk_rows(m)
                    nc.scalar.activation(gate[m % 2][0:rows, :], L.ps_q[m % 2][0:rows, 0, :], ACT.Silu).then_inc(ev.silu_done.sem, 1)
                    if m == ES - 1:
                        act.wait_ge(ev.comb_turned.sem, ev.comb_turned.upto(i, 1))
                        copy(cT[:, :], L.ps_s[1][0:CK, 0, :]).then_inc(ev.combhi_done.sem, 1)
                    if prep:
                        if m == 4:
                            prep_x(i + 1)
                        if m == 11:
                            prep_k(i + 1)

            prep_x(0)
            prep_k(0)
            with act.Fori(0, B - 1) as i:
                attention(i)
                experts(i, True)
            attention(B - 1)
            experts(B - 1, False)

        @block.vector
        def _(dve):
            vec = nc.vector

            def minus_hi(lo, src, hi):
                return vec.tensor_tensor(lo, src, hi.bitcast(F32), ALU.subtract)

            class Steps:

                def __init__(self, events, i):
                    self.events, self.i, self.n = events, i, 0

                def __call__(self, ins, carry=False):
                    self.n += 1
                    ins.then_inc(self.events.sem, 1)
                    dve.wait_ge(self.events.sem, self.events.upto(self.i, self.n))
                    if carry:
                        vec.memset(carrier[:, :], 0.0)

                def end(self):
                    assert self.n == self.events.per_round

            def moments(step, src, mean, var, done):
                for j in range(NT):
                    last = vec.bn_stats(bn[:, j, :], src(j))
                step(last, carry=True)
                for j in range(NT):
                    last = vec.bn_aggr(mean[:, j, :], bn[:, j, :])
                step(last)
                vec.tensor_scalar(var[:, :], mean[:, :, 1], EPS, None, ALU.add).then_inc(done.sem, 1)

            def normalise(out, src, mean, rstd, done):
                for j in range(NT):
                    last = vec.tensor_scalar(out(j), src(j), mean[:, j, 0:1], rstd[:, j:j + 1], ALU.subtract, ALU.mult)
                last.then_inc(done.sem, 1)

            def kv_tile(j):
                return L.ps_t[1][:, 0, j * P:j * P + RANK]

            def prep_moments(r, step):
                dve.wait_ge(ev.x_loaded.sem, ev.x_loaded.upto(r, 16))
                moments(step, lambda j: xin[:, j, :], mean_a, var_a, ev.vara_done)

            def prep_normal(r):
                dve.wait_ge(ev.vara_done.sem, ev.vara_done.upto(r, 1))
                dve.wait_ge(ev.rsa_done.sem, ev.rsa_done.upto(r, 1))
                normalise(lambda j: xhat[:, j, :], lambda j: xin[:, j, :], mean_a, rstd_a, ev.xha_done)

            def prep_x(r):
                dve.wait_ge(ev.xahi_done.sem, ev.xahi_done.upto(r, 1))
                minus_hi(xa_lo[:, :, :], L.ps_t[0][:, :, :], xa_hi[:, :, :]).then_inc(ev.xalo_done.sem, 1)

            def prep_kv(r, step):
                dve.wait_ge(ev.kv_full.sem, ev.kv_full.upto(r, 1))
                moments(step, kv_tile, mean_k, var_k, ev.vark_done)
                rot = L.ps_t[1][:, 0, :].rearrange("p (j n) -> p j n", j=NT)
                evens, odds = rot[:, :, RANK::2], rot[:, :, RANK + 1::2]
                for n, (x, trig) in enumerate(((evens, L.kcos), (odds, L.ksin), (evens, L.ksin), (odds, L.kcos))):
                    last = vec.tensor_tensor(krot[:, n, :, :], x, trig[:, :, :], ALU.mult)
                last.then_inc(ev.kr_done.sem, 1)

            def prep_kn(r):
                dve.wait_ge(ev.vark_done.sem, ev.vark_done.upto(r, 1))
                dve.wait_ge(ev.rsk_done.sem, ev.rsk_done.upto(r, 1))
                normalise(lambda j: kp[:, j, 0:RANK], kv_tile, mean_k, rstd_k, ev.kn_done)

            def prep_k(r):
                dve.wait_ge(ev.khi_done.sem, ev.khi_done.upto(r, 1))
                minus_hi(kT_lo[:, :], L.ps_t[0][:, 0, :], kT_hi[:, :]).then_inc(ev.klo_done.sem, 1)

            def query_cos(i, p):
                dve.wait_ge(ev.swap_done.sem, ev.swap_done.upto(i, p + 1))
                if p >= 1:
                    dve.wait_ge(ev.qhi_done.sem, ev.qhi_done.upto(i, p))
                vec.tensor_tensor(qf[:, :, :], L.ps_q[p % 2][:, :, :], L.qcos[:, :].unsqueeze(1).to_broadcast([P, 2, S]),
                                  ALU.mult).then_inc(ev.qcos_done.sem, 1)

            def query_lo(i, p):
                dve.wait_ge(ev.qhi_done.sem, ev.qhi_done.upto(i, p + 1))
                minus_hi(q_lo[p % 2][:, :, :], qf[:, :, :], q_hi[p % 2][:, :, :]).then_inc(ev.qlo_done.sem, 1)

            def maxima(i, h):
                dve.wait_ge(ev.s_full.sem, ev.s_full.upto(i, h + 1))
                vec.tensor_reduce(nmax[:, h, :], L.ps_s[h % 2][:, :, :], AX.X, ALU.max, negate=True).then_inc(ev.max_done.sem, 1)

            def inverse(i, h):
                dve.wait_ge(ev.exp_done.sem, ev.exp_done.upto(i, h + 1))
                vec.reciprocal(rinv[:, h, :], rsum[:, h, :]).then_inc(ev.rinv_done.sem, 1)

            def probs_lo(i, h):
                dve.wait_ge(ev.phi_done.sem, ev.phi_done.upto(i, h + 1))
                minus_hi(pT_lo[h % 3][:, :, :], L.ps_t[h % 2][:, :, :], pT_hi[h % 3][:, :, :]).then_inc(ev.plo_done.sem, 1)

            def attended_lo(i, p):
                dve.wait_ge(ev.ohi_done.sem, ev.ohi_done.upto(i, p + 1))
                for n in range(2):
                    last = minus_hi(o_lo[p % 2][half[n], :], L.ps_o[half[n], n, :], o_hi[p % 2][half[n], :])
                last.then_inc(ev.olo_done.sem, 1)

            def attention(i):
                query_cos(i, 0)
                query_lo(i, 0)
                for p in range(NP + 3):
                    if p < NP:
                        maxima(i, 2 * p)
                    if p + 1 < NP:
                        query_cos(i, p + 1)
                    if 2 <= p < NP + 2:
                        probs_lo(i, 2 * p - 3)
                    if p < NP:
                        inverse(i, 2 * p)
                    if 1 <= p < NP + 1:
                        probs_lo(i, 2 * p - 2)
                    if p < NP:
                        maxima(i, 2 * p + 1)
                    if 2 <= p < NP + 2:
                        attended_lo(i, p - 2)
                    if p < NP:
                        inverse(i, 2 * p + 1)
                    if p + 1 < NP:
                        query_lo(i, p + 1)

            def experts(i, prep):
                step = Steps(ev.ffn_step, i)
                dve.wait_ge(ev.out_done.sem, ev.out_done.upto(i, NP))
                dve.wait_ge(ev.out_stored.sem, ev.out_stored.before(i, 16))
                vec.tensor_tensor(x2[:, :, :], L.ps_y[:, :, :], xin[:, :, :], ALU.add).then_inc(ev.x2_done.sem, 1)
                dve.wait_ge(ev.x2_done.sem, ev.x2_done.upto(i, 1))
                moments(step, lambda j: x2[:, j, :], mean_f, var_f, ev.varf_done)
                dve.wait_ge(ev.varf_done.sem, ev.varf_done.upto(i, 1))
                dve.wait_ge(ev.rsf_done.sem, ev.rsf_done.upto(i, 1))
                normalise(lambda j: xhat[:, j, :], lambda j: x2[:, j, :], mean_f, rstd_f, ev.xhf_done)
                dve.wait_ge(ev.xfhi_done.sem, ev.xfhi_done.upto(i, 1))
                minus_hi(xf_lo[:, :, :], L.ps_t[0][:, :, :], xf_hi[:, :, :]).then_inc(ev.xflo_done.sem, 1)
                dve.wait_ge(ev.logits_full.sem, ev.logits_full.upto(i, 1))
                vec.tensor_reduce(lmax[:, :], L.ps_s[0][:, 0, 0:NT * E].rearrange("p (j e) -> p j e", j=NT), AX.X, ALU.max,
                                  negate=True).then_inc(ev.lmax_done.sem, 1)
                dve.wait_ge(ev.gate_exp_done.sem, ev.gate_exp_done.upto(i, 1))
                step(vec.reciprocal(einv[:, :], esum[:, :]))
                for j in range(NT):
                    last = vec.tensor_scalar(score[:, j, 0:E], eprob[:, j, :], einv[:, j:j + 1], None, ALU.mult)
                step(last, carry=True)
                for j in range(NT):
                    last = vec.max(top[:, j, :], score[:, j, 0:E])
                step(last)
                step(vec.tensor_copy(top[:, :, TOP:E], L.sentinel[:, 0:E - TOP].unsqueeze(1).to_broadcast([P, NT, E - TOP])),
                     carry=True)
                for j in range(NT):
                    last = vec.match_replace(rest[:, j, :], top[:, j, :], score[:, j, :], 0.0)
                step(last)
                step(vec.tensor_tensor(comb[:, :, :], score[:, :, 0:E], rest[:, :, 0:E], ALU.subtract))
                step(vec.tensor_copy(comb2[:, :, 0:E].bitcast(F32R), comb[:, :, :]))
                vec.tensor_tensor(comb2[:, :, LO:CK], comb[:, :, :], comb2[:, :, 0:E], ALU.subtract).then_inc(ev.comb_done.sem, 1)
                step.end()
                prep_step = Steps(ev.prep_step, i + 1) if prep else None
                for m in range(CH):
                    rows = chunk_rows(m)
                    dve.wait_ge(ev.silu_done.sem, ev.silu_done.upto(i, m + 1))
                    up, act = L.ps_q[m % 2][0:rows, 1, :], gate[m % 2][0:rows, :]
                    if m >= 2:
                        dve.wait_ge(ev.ulo_done.sem, ev.ulo_done.upto(i, m - 1))
                    if m < ES:
                        vec.tensor_tensor(unit[m % 2][0:rows, :], up, act, ALU.mult).then_inc(ev.su_done.sem, 1)
                    else:
                        c = m - ES
                        vec.tensor_tensor(prod[m % 2][:, :], up, act, ALU.mult).then_inc(ev.su_done.sem, 1)
                        dve.wait_ge(ev.su_done.sem, ev.su_done.upto(i, m + 1))
                        dve.wait_ge(ev.cb_full.sem, ev.cb_full.upto(i, c + 1))
                        vec.tensor_tensor(unit[m % 2][:, :], L.ps_s[c % 2][:, 0, :], prod[m % 2][:, :], ALU.mult
                                          ).then_inc(ev.cb_done.sem, 1)
                    if prep:
                        if m == 1:
                            prep_moments(i + 1, prep_step)
                        if m == 3:
                            prep_normal(i + 1)
                        if m == 5:
                            prep_x(i + 1)
                        if m == 8:
                            prep_kv(i + 1, prep_step)
                        if m == 9:
                            prep_kn(i + 1)
                        if m == 12:
                            prep_k(i + 1)
                            prep_step.end()
                dve.wait_ge(ev.down_done.sem, ev.down_done.upto(i, CH))
                vec.tensor_tensor(x2[:, :, :], L.ps_y[:, :, :], x2[:, :, :], ALU.add).then_inc(ev.osb_done.sem, 1)

            vec.tensor_copy(score[:, :, E:2 * E], L.sentinel[:, :].unsqueeze(1).to_broadcast([P, NT, E]))
            vec.memset(comb2[:, :, :], 0.0)
            vec.memset(qswap[0:RANK, :, :], 0.0).then_inc(ev.latent_zero, 1)
            step = Steps(ev.prep_step, 0)
            prep_moments(0, step)
            prep_normal(0)
            prep_x(0)
            prep_kv(0, step)
            prep_kn(0)
            prep_k(0)
            step.end()
            with dve.Fori(0, B - 1) as i:
                attention(i)
                experts(i, True)
            attention(B - 1)
            experts(B - 1, False)

        @block.gpsimd
        def _(pool):
            gp = nc.gpsimd

            def hi_of(hi, src):
                ones = one[0:src.shape[0], 0:1]
                while ones.ndim < src.ndim:
                    ones = ones.unsqueeze(1)
                return gp.tensor_tensor(hi, src, ones.to_broadcast(list(src.shape)), ALU.mult)

            def power(var, rstd, ready, done, r):
                pool.wait_ge(ready.sem, ready.upto(r, 1))
                gp.tensor_tensor(rstd[:, :], var[:, :], L.minus_half[:, :], ALU.pow).then_inc(done.sem, 1)

            def prep_kp(r):
                pool.wait_ge(ev.kr_done.sem, ev.kr_done.upto(r, 1))
                gp.tensor_tensor(kp[:, :, RANK:RANK + HR], krot[:, 0, :, :], krot[:, 1, :, :], ALU.subtract)
                gp.tensor_tensor(kp[:, :, RANK + HR:P], krot[:, 2, :, :], krot[:, 3, :, :], ALU.add)
                pool.wait_ge(ev.kn_done.sem, ev.kn_done.upto(r, 1))
                lat = kp[:, :, 0:RANK]
                wide = lambda t: t[:, :].unsqueeze(1).to_broadcast([P, NT, RANK])
                gp.tensor_tensor(lat, lat, wide(L.gamma), ALU.mult).then_inc(ev.kp_part.sem, 1)
                pool.wait_ge(ev.kp_part.sem, ev.kp_part.upto(r, 1))
                gp.tensor_tensor(lat, lat, wide(L.beta), ALU.add).then_inc(ev.kp_done.sem, 1)
                pool.wait_ge(ev.kp_done.sem, ev.kp_done.upto(r, 1))
                for n in range(2):
                    last = hi_of(kv_hi[:, :, n, :], lat)
                last.then_inc(ev.kvhi_done.sem, 1)
                pool.wait_ge(ev.kvhi_done.sem, ev.kvhi_done.upto(r, 1))
                for n in range(2):
                    last = gp.tensor_tensor(kv_lo[:, :, n, :], lat, kv_hi[:, :, n, :].bitcast(F32), ALU.subtract)
                last.then_inc(ev.kvlo_done.sem, 1)

            def rotate(i, p):
                pool.wait_ge(ev.swap_done.sem, ev.swap_done.upto(i, p + 1))
                gp.tensor_tensor(qswap[:, :, :], qswap[:, :, :], L.qsin[:, :].unsqueeze(1).to_broadcast([P, 2, S]), ALU.mult).then_inc(ev.qrot_part.sem, 1)
                pool.wait_ge(ev.qrot_part.sem, ev.qrot_part.upto(i, p + 1))
                pool.wait_ge(ev.qcos_done.sem, ev.qcos_done.upto(i, p + 1))
                gp.tensor_tensor(qf[:, :, :], qf[:, :, :], qswap[:, :, :], ALU.add).then_inc(ev.qrot_done.sem, 1)

            def normal(i, h):
                pool.wait_ge(ev.rinv_done.sem, ev.rinv_done.upto(i, h + 1))
                gp.tensor_tensor(probs[h % 3][:, :, :], probs[h % 3][:, :, :], rinv[:, h, :].unsqueeze(2).to_broadcast([P, NT, S]),
                                 ALU.mult).then_inc(ev.pn_done.sem, 1)

            def attention(i):
                rotate(i, 0)
                for p in range(NP):
                    if p + 1 < NP:
                        rotate(i, p + 1)
                    normal(i, 2 * p)
                    normal(i, 2 * p + 1)

            def experts(i, prep):
                power(var_f, rstd_f, ev.varf_done, ev.rsf_done, i)
                for m in range(CH):
                    if m < ES:
                        pool.wait_ge(ev.su_done.sem, ev.su_done.upto(i, m + 1))
                    else:
                        pool.wait_ge(ev.cb_done.sem, ev.cb_done.upto(i, m - ES + 1))
                    if m >= 3:
                        pool.wait_ge(ev.down_done.sem, ev.down_done.upto(i, m - 2))
                    hi_of(u_hi[m % 3], unit[m % 2][:, :]).then_inc(ev.uhi_done.sem, 1)
                    pool.wait_ge(ev.uhi_done.sem, ev.uhi_done.upto(i, m + 1))
                    gp.tensor_tensor(u_lo[m % 3], unit[m % 2][:, :], u_hi[m % 3].bitcast(F32),
                                     ALU.subtract).then_inc(ev.ulo_done.sem, 1)
                    if prep:
                        if m == 1:
                            power(var_a, rstd_a, ev.vara_done, ev.rsa_done, i + 1)
                        if m == 8:
                            power(var_k, rstd_k, ev.vark_done, ev.rsk_done, i + 1)
                        if m == 9:
                            prep_kp(i + 1)

            gp.memset(one[:, :], 1.0).then_inc(ev.ones_set, 1)
            pool.wait_ge(ev.ones_set, 1)
            pool.wait_ge(ev.latent_zero, 1)
            power(var_a, rstd_a, ev.vara_done, ev.rsa_done, 0)
            power(var_k, rstd_k, ev.vark_done, ev.rsk_done, 0)
            prep_kp(0)
            with pool.Fori(0, B - 1) as i:
                attention(i)
                experts(i, True)
            attention(B - 1)
            experts(B - 1, False)


def layer(nc, d):
    with ExitStack() as ctx:
        L = Layer(nc, ctx)
        weights(nc, L, d)
        loop(nc, L, d)


_INS = {"L0_attn_hidden_states": "x", "L0_attn_freqs_cis": "freqs", "L0_attn_Wq": "Wq", "L0_attn_Wkv_a": "Wkv_a",
        "L0_attn_kv_gamma": "gamma", "L0_attn_kv_beta": "beta", "L0_attn_Wkv_b": "Wkv_b", "L0_attn_Wout": "Wout",
        "L0_ffn_gate_w": "gate_w", "L0_ffn_w_gate": "w_gate", "L0_ffn_w_up": "w_up", "L0_ffn_w_down": "w_down",
        "L0_ffn_sw_gate": "sw_gate", "L0_ffn_sw_up": "sw_up", "L0_ffn_sw_down": "sw_down"}


def kernel(**inputs):
    import numpy as np
    import concourse.bacc as bacc
    from concourse.bass_utils import run_bass_kernel_spmd

    nc = bacc.Bacc("TRN2", target_bir_lowering=False, num_devices=1)
    arrays, d = {}, {}
    for name, short in _INS.items():
        a = np.ascontiguousarray(inputs[name])
        arrays[f"{short}_dram"] = a
        d[short] = nc.dram_tensor(f"{short}_dram", a.shape, F32, kind="ExternalInput").ap()
    d["out"] = nc.dram_tensor("out_dram", (B, S, D), F32, kind="ExternalOutput").ap()
    layer(nc, d)
    r = run_bass_kernel_spmd(nc, [arrays], core_ids=[0])
    return r.results[0]["out_dram"]
```

```python
from contextlib import ExitStack

import concourse.bass as bass
from concourse import mybir

F32 = mybir.dt.float32
F32R = mybir.dt.float32r
ALU = mybir.AluOpType
ACT = mybir.ActivationFunctionType
AX = mybir.AxisListType

P = 128
B, S, D = 8, 256, 256
NT = S // P
KD = D // P
NH, DN, DR, DV, RANK = 16, 128, 64, 128, 64
DQK = DN + DR
NP = NH // 2
HR = DR // 2
E, H = 8, 176
EH = E * H
HS = 2 * H
ER = EH // P
ES = -(-HS // P)
CH = ES + ER
LO = 32
CK = LO + E
TOP = 2
SCALE = float(DQK) ** -0.5
EPS = 1e-5
STAGE = 3
HALF = E // 2
STAGES = 4
GROUP = 4
TW = 2 * P + 3 * RANK


def chunk_rows(m):
    return min(P, HS - m * P) if m < ES else P


def flat2(t):
    return t[:, :, :].rearrange("p a b -> p (a b)")


class Events:

    def __init__(self, sem, per_round, head=0):
        self.sem, self.per_round, self.head = sem, per_round, head

    def upto(self, i, n):
        return i * self.per_round + (n + self.head)

    def before(self, i, n):
        assert n + self.head - self.per_round >= 1
        return i * self.per_round + (n + self.head - self.per_round)


class AllEvents:

    def __init__(self, nc, ctx):
        def count(name, per_round, head=0):
            return Events(ctx.enter_context(nc.semaphore(name)), per_round, head)

        self.x_loaded = count("x_loaded", 16)
        self.out_stored = count("out_stored", 16, head=16)
        self.q_full = count("q_full", NP)
        self.out_done = count("out_done", NP)
        self.s_full = count("s_full", NH)
        self.t_full = count("t_full", NH)
        self.pv_done = count("pv_done", NH)
        self.gu_full = count("gu_full", CH)
        self.down_done = count("down_done", CH)
        self.cb_full = count("cb_full", ER)
        self.xf_turned = count("xf_turned", 1)
        self.logits_full = count("logits_full", 1)
        self.comb_turned = count("comb_turned", 1)
        self.xa_turned = count("xa_turned", 1)
        self.kv_full = count("kv_full", 1)
        self.k_turned = count("k_turned", 1)
        self.swap_done = count("swap_done", NP)
        self.qhi_done = count("qhi_done", NP)
        self.ohi_done = count("ohi_done", NP)
        self.exp_done = count("exp_done", NH)
        self.phi_done = count("phi_done", NH)
        self.silu_done = count("silu_done", CH)
        self.xfhi_done = count("xfhi_done", 1)
        self.gate_exp_done = count("gate_exp_done", 1)
        self.combhi_done = count("combhi_done", 1)
        self.xahi_done = count("xahi_done", 1)
        self.khi_done = count("khi_done", 1)
        self.qcos_done = count("qcos_done", NP)
        self.qlo_done = count("qlo_done", NP)
        self.olo_done = count("olo_done", NP, head=1)
        self.max_done = count("max_done", NH)
        self.rinv_done = count("rinv_done", NH)
        self.plo_done = count("plo_done", NH)
        self.su_done = count("su_done", CH, head=CH)
        self.cb_done = count("cb_done", ER, head=ER)
        self.x2_done = count("x2_done", 1)
        self.varf_done = count("varf_done", 1)
        self.xhf_done = count("xhf_done", 1)
        self.xflo_done = count("xflo_done", 1)
        self.lmax_done = count("lmax_done", 1)
        self.comb_done = count("comb_done", 1)
        self.osb_done = count("osb_done", 1, head=1)
        self.vara_done = count("vara_done", 1)
        self.xha_done = count("xha_done", 1)
        self.xalo_done = count("xalo_done", 1)
        self.vark_done = count("vark_done", 1)
        self.kn_done = count("kn_done", 1)
        self.kr_done = count("kr_done", 1)
        self.klo_done = count("klo_done", 1)
        self.ffn_step = count("ffn_step", 9)
        self.prep_step = count("prep_step", 4)
        self.qrot_part = count("qrot_part", NP)
        self.qrot_done = count("qrot_done", NP)
        self.pn_done = count("pn_done", NH)
        self.uhi_done = count("uhi_done", CH)
        self.ulo_done = count("ulo_done", CH)
        self.rsf_done = count("rsf_done", 1)
        self.rsa_done = count("rsa_done", 1)
        self.rsk_done = count("rsk_done", 1)
        self.kp_part = count("kp_part", 1)
        self.kp_done = count("kp_done", 1)
        self.kvhi_done = count("kvhi_done", 1)
        self.kvlo_done = count("kvlo_done", 1)
        self.latent_zero = ctx.enter_context(nc.semaphore("latent_zero"))
        self.ones_set = ctx.enter_context(nc.semaphore("ones_set"))


class Layer:

    def __init__(self, nc, ctx):
        def sb(name, shape, dt=F32):
            return ctx.enter_context(nc.sbuf_tensor(name, shape, dt))

        def bank(name):
            return ctx.enter_context(nc.psum_tensor(name, [P, 2, S], F32))

        self.events = AllEvents(nc, ctx)
        self.wq_hi, self.wq_lo = (sb(f"wq_{x}", [P, KD, NH, P], F32R) for x in ("hi", "lo"))
        self.wo_hi, self.wo_lo = (sb(f"wo_{x}", [P, NP, D], F32R) for x in ("hi", "lo"))
        self.wkva_hi, self.wkva_lo = (sb(f"wkva_{x}", [P, KD, RANK + DR], F32R) for x in ("hi", "lo"))
        self.gw_hi, self.gw_lo = (sb(f"gw_{x}", [P, KD, E], F32R) for x in ("hi", "lo"))
        self.mg_hi, self.mg_lo = (sb(f"mg_{x}", [P, KD, EH], F32R) for x in ("hi", "lo"))
        self.mu_hi, self.mu_lo = (sb(f"mu_{x}", [P, KD, EH], F32R) for x in ("hi", "lo"))
        self.md_hi, self.md_lo = (sb(f"md_{x}", [P, ER, D], F32R) for x in ("hi", "lo"))
        self.sgu_hi, self.sgu_lo = (sb(f"sgu_{x}", [P, 2 * KD, HS], F32R) for x in ("hi", "lo"))
        self.sd_hi, self.sd_lo = (sb(f"sd_{x}", [P, ES, D], F32R) for x in ("hi", "lo"))
        self.ident = sb("ident", [P, P])
        self.sel = sb("sel", [CK, EH], F32R)
        self.qcos = sb("qcos", [P, S])
        self.qsin = sb("qsin", [P, S])
        self.kcos = sb("kcos", [P, NT, HR])
        self.ksin = sb("ksin", [P, NT, HR])
        self.gamma = sb("gamma", [P, RANK])
        self.beta = sb("beta", [P, RANK])
        self.minus_half = sb("minus_half", [P, NT])
        self.sentinel = sb("sentinel", [P, E])
        self.ps_q = [bank(f"ps_q{n}") for n in range(2)]
        self.ps_s = [bank(f"ps_s{n}") for n in range(2)]
        self.ps_t = [bank(f"ps_t{n}") for n in range(2)]
        self.ps_o = bank("ps_o")
        self.ps_y = bank("ps_y")


def weights(nc, L, d):
    with ExitStack() as ctx:
        def sb(name, shape, dt=F32):
            return ctx.enter_context(nc.sbuf_tensor(name, shape, dt))

        def sem(name):
            return ctx.enter_context(nc.semaphore(name))

        wq_raw = sb("wq_raw", [P, KD, NH, DQK])
        wkvb_raw = [sb(f"wkvb_raw{n}", [RANK, GROUP, DN + DV]) for n in range(2)]
        wout_raw = [sb(f"wout_raw{n}", [P, GROUP, D]) for n in range(2)]
        small_raw = sb("small_raw", [P, KD, RANK + DR + E])
        stage = [sb(f"stage{n}", [P, STAGE * D]) for n in range(STAGES)]
        sel_f = sb("sel_f", [CK, HALF * H])
        turned = [sb(f"turned{n}", [P, TW]) for n in range(2)]
        theta = sb("theta", [P, NT, 4, HR])
        turns = sb("turns", [P, NT, 4, HR])
        angle = sb("angle", [P, NT, 4, HR])
        cos4 = sb("cos4", [P, NT, 4, HR])
        sin4 = sb("sin4", [P, NT, 4, HR])

        theta_in, small_in = map(sem, ("theta_in", "small_in"))
        heads_in = [sem(f"heads_in{g}") for g in range(NH // GROUP)]
        stage_in = [sem(f"stage_in{n}") for n in range(STAGES)]
        stage_hi, stage_used = map(sem, ("stage_hi", "stage_used"))
        ident_step, sel_step, rope_hi = map(sem, ("ident_step", "sel_step", "rope_hi"))
        w_turned, w_evac, w_full, whi_done, wlo_done = map(sem, ("w_turned", "w_evac", "w_full", "whi_done", "wlo_done"))
        angle_step, angle_done, cos_angle, sin_done, cos_done, trig_turned, small_hi = map(
            sem, ("angle_step", "angle_done", "cos_angle", "sin_done", "cos_done", "trig_turned", "small_hi"))

        HEAD_LOADS = 16 * (KD + 2)

        tail = HS - (ES - 1) * P
        cut = (ES - 1) * D
        down_rows = d["w_down"].rearrange("e h n -> (e h) n").rearrange("(c p) n -> p c n", p=P)

        def expert_part(st, src, hi, lo, k, e):
            cols, st = slice(e * H, (e + HALF) * H), st[:, 0:HALF * H]
            return ([(st.rearrange("p (e h) -> p e h", e=HALF), src[e:e + HALF, k * P:(k + 1) * P, :].rearrange("e p h -> p e h"))],
                    [(hi[:, k, cols], lo[:, k, cols], st)])

        def down_part(st, at, to):
            cols, st = slice(at * D, to * D), st[:, 0:(to - at) * D]
            return ([(st.rearrange("p (c n) -> p c n", n=D), down_rows[:, at:to, :])],
                    [(flat2(L.md_hi)[:, cols], flat2(L.md_lo)[:, cols], st)])

        def shared_part(st, src, n):
            cols, st = slice(n * KD * HS, (n + 1) * KD * HS), st[:, 0:KD * HS]
            return ([(st.rearrange("p (k h) -> p k h", k=KD), src.rearrange("(k p) h -> p k h", p=P))],
                    [(flat2(L.sgu_hi)[:, cols], flat2(L.sgu_lo)[:, cols], st)])

        def shared_down_part(st):
            return ([(st[:, 0:cut].rearrange("p (c n) -> p c n", c=ES - 1), d["sw_down"][0:(ES - 1) * P, :].rearrange("(c p) n -> p c n", p=P)),
                     (st[0:tail, cut:cut + D], d["sw_down"][(ES - 1) * P:HS, :])],
                    [(flat2(L.sd_hi)[:, 0:cut], flat2(L.sd_lo)[:, 0:cut], st[:, 0:cut]),
                     (L.sd_hi[0:tail, ES - 1, :], L.sd_lo[0:tail, ES - 1, :], st[0:tail, cut:cut + D])])

        parts = [(shared_part, src, n) for n, src in enumerate((d["sw_gate"], d["sw_up"]))] + [(shared_down_part,)]
        for src, hi, lo in ((d["w_gate"], L.mg_hi, L.mg_lo), (d["w_up"], L.mu_hi, L.mu_lo)):
            parts += [(expert_part, src, hi, lo, k, e) for k in range(KD) for e in (0, HALF)]
        parts += [(down_part, at, min(at + STAGE, ER)) for at in range(0, ER, STAGE)]
        staged = [make(stage[n % STAGES], *args) for n, (make, *args) in enumerate(parts)]
        loads_upto = [16 * sum(len(staged[m][0]) for m in range(n % STAGES, n + 1, STAGES)) for n in range(len(staged))]
        splits_upto = [sum(len(staged[m][1]) for m in range(n + 1)) for n in range(len(staged))]
        parts_after = [[n for n in range(len(staged)) if min(n + 1, NH - 1) == h] for h in range(NH)]

        with nc.Block() as block:
            @block.sync
            def _(sp):
                for r in range(4):
                    sp.dma_start(theta[:, :, r, :], d["freqs"].rearrange("(j p) f -> p j f", p=P)).then_inc(theta_in, 16)
                by_head = "(k p) (h n) -> p k h n"

                def load_heads(g):
                    heads = slice(g * GROUP, (g + 1) * GROUP)
                    if g >= 2:
                        sp.wait_ge(w_full, GROUP * (g - 1))
                    sp.dma_start(wkvb_raw[g % 2][:, :, :], d["Wkv_b"].rearrange("c (h n) -> c h n", h=NH)[:, heads, :]).then_inc(heads_in[g], 16)
                    for k in range(KD):
                        sp.dma_start(wq_raw[:, k, heads, :],
                                     d["Wq"].rearrange(by_head, p=P, h=NH)[:, k, heads, :]).then_inc(heads_in[g], 16)
                    sp.dma_start(wout_raw[g % 2][:, :, :], d["Wout"].rearrange("(h n) m -> n h m", n=DV)[:, heads, :]).then_inc(heads_in[g], 16)

                load_heads(0)
                load_heads(1)
                for n, (loads, _) in enumerate(staged):
                    if n >= STAGES:
                        if n % STAGES == 0 and n // STAGES + 1 < NH // GROUP:
                            load_heads(n // STAGES + 1)
                        sp.wait_ge(stage_used, splits_upto[n - STAGES])
                    for to, src in loads:
                        sp.dma_start(to, src).then_inc(stage_in[n % STAGES], 16)
                for events in (L.events.su_done, L.events.cb_done, L.events.olo_done, L.events.osb_done, L.events.out_stored):
                    sp.sem_inc(events.sem, events.head)

            @block.scalar
            def _(act):
                act.dma_start(small_raw[:, :, 0:RANK + DR], d["Wkv_a"].rearrange("(k p) n -> p k n", p=P)).then_inc(small_in, 16)
                act.dma_start(small_raw[:, :, RANK + DR:], d["gate_w"].rearrange("(k p) n -> p k n", p=P)).then_inc(small_in, 16)
                act.dma_start(L.gamma[:, :], d["gamma"].partition_broadcast(P)).then_inc(small_in, 16)
                act.dma_start(L.beta[:, :], d["beta"].partition_broadcast(P)).then_inc(small_in, 16)
                act.wait_ge(angle_done, 1)
                nc.scalar.activation(sin4[:, :, :, :], angle[:, :, :, :], ACT.Sin).then_inc(sin_done, 1)
                act.wait_ge(cos_angle, 1)
                nc.scalar.activation(cos4[:, :, :, :], turns[:, :, :, :], ACT.Sin).then_inc(cos_done, 1)
                act.wait_ge(small_in, 64)
                nc.scalar.activation(L.wkva_hi[:, :, :], small_raw[:, :, 0:RANK + DR], ACT.Copy).then_inc(small_hi, 1)
                nc.scalar.activation(L.gw_hi[:, :, :], small_raw[:, :, RANK + DR:], ACT.Copy).then_inc(small_hi, 1)

                def split_hi(n):
                    act.wait_ge(stage_in[n % STAGES], loads_upto[n])
                    for hi, _, src in staged[n][1]:
                        nc.scalar.activation(hi, src, ACT.Copy).then_inc(stage_hi, 1)

                def evacuate(h):
                    act.wait_ge(w_turned, h + 1)
                    if h >= 2:
                        act.wait_ge(w_full, h - 1)
                    nc.scalar.activation(turned[h % 2][:, :], flat2(L.ps_t[h % 2])[:, 0:TW], ACT.Copy).then_inc(w_evac, 1)

                evacuate(0)
                for h in range(NH):
                    if h + 1 < NH:
                        evacuate(h + 1)
                    act.wait_ge(w_full, h + 1)
                    prod = flat2(L.ps_s[h % 2])
                    rows = slice(RANK * (h % 2), RANK * (h % 2) + RANK)
                    nc.scalar.activation(L.wq_hi[:, :, h, 0:RANK], prod[:, 0:KD * RANK].rearrange("p (k c) -> p k c", k=KD), ACT.Copy)
                    nc.scalar.activation(L.wo_hi[rows, h // 2, :], prod[rows, KD * RANK:KD * RANK + D], ACT.Copy).then_inc(whi_done, 1)
                    for n in parts_after[h]:
                        split_hi(n)

            @block.tensor
            def _(pe):
                pe.wait_ge(ident_step, 2)
                pe.wait_ge(sin_done, 1)
                pe.wait_ge(cos_done, 1)
                for n, trig in enumerate((cos4, sin4)):
                    for j in range(NT):
                        last = nc.tensor.transpose(L.ps_q[n][:, 0, j * P:(j + 1) * P],
                                                   trig[:, j, :, :].rearrange("p r f -> p (r f)"), L.ident[:, :])
                last.then_inc(trig_turned, 1)
                def turn(h):
                    if h % GROUP == 0:
                        pe.wait_ge(heads_in[h // GROUP], HEAD_LOADS)
                    if h >= 2:
                        pe.wait_ge(w_evac, h - 1)
                    to = flat2(L.ps_t[h % 2])
                    for k in range(KD):
                        nc.tensor.transpose(to[:, k * P:(k + 1) * P], wq_raw[:, k, h, 0:DN], L.ident[:, :])
                    at = KD * P
                    for part in (0, DN, DN):
                        last = nc.tensor.transpose(to[:, at:at + RANK], wkvb_raw[h // GROUP % 2][:, h % GROUP, part:part + DN], L.ident[0:RANK, 0:RANK])
                        at += RANK
                    last.then_inc(w_turned, 1)

                turn(0)
                for h in range(NH):
                    if h + 1 < NH:
                        turn(h + 1)
                    pe.wait_ge(w_evac, h + 1)
                    if h >= 2:
                        pe.wait_ge(wlo_done, h - 1)
                    to, t = flat2(L.ps_s[h % 2]), turned[h % 2]
                    for k in range(KD):
                        nc.tensor.matmul(to[:, k * RANK:(k + 1) * RANK], t[:, k * P:(k + 1) * P],
                                         t[:, KD * P:KD * P + RANK], start=True, stop=True)
                    nc.tensor.matmul(to[:, KD * RANK:KD * RANK + D], t[:, KD * P + RANK:TW], wout_raw[h // GROUP % 2][:, h % GROUP, :],
                                     start=True, stop=True).then_inc(w_full, 1)

            @block.vector
            def _(dve):
                nc.vector.memset(L.minus_half[:, :], -0.5)
                for n in range(E):
                    nc.vector.memset(L.sentinel[:, n:n + 1], -1.0 - n)
                nc.vector.memset(L.qcos[0:RANK, :], SCALE)
                nc.vector.memset(L.qsin[0:RANK, :], 0.0)
                steps = 0

                def step(ins):
                    nonlocal steps
                    steps += 1
                    ins.then_inc(angle_step, 1)
                    dve.wait_ge(angle_step, steps)

                two_pi, first, second = 6.283185307179586, 6.28125, 1.93500518798828125e-3
                to_round = 12582912.0
                th, tu, an = (t[:, :, :, :].rearrange("p j r f -> p (j r f)") for t in (theta, turns, angle))
                dve.wait_ge(theta_in, 64)
                step(nc.vector.tensor_scalar(tu, th, 1.0 / two_pi, to_round, ALU.mult, ALU.add))
                step(nc.vector.tensor_scalar(tu, tu, -to_round, None, ALU.add))
                step(nc.vector.scalar_tensor_tensor(an, tu, -first, th, ALU.mult, ALU.add))
                step(nc.vector.scalar_tensor_tensor(an, tu, -second, an, ALU.mult, ALU.add))
                step(nc.vector.scalar_tensor_tensor(an, tu, -(two_pi - first - second), an, ALU.mult, ALU.add))
                nc.vector.tensor_scalar(an, an, 3.1415925, -3.1415925, ALU.min, ALU.max).then_inc(angle_done, 1)
                dve.wait_ge(angle_done, 1)
                step(nc.vector.scalar_tensor_tensor(tu, an, -1.0, an, ALU.mult, ALU.min))
                nc.vector.tensor_scalar(tu, tu, two_pi / 4, None, ALU.add).then_inc(cos_angle, 1)
                dve.wait_ge(trig_turned, 1)
                even, odd = slice(RANK, RANK + HR), slice(RANK + HR, RANK + DR)
                nc.vector.tensor_scalar(L.qcos[RANK:P, :], L.ps_q[0][RANK:P, 0, :], SCALE, None, ALU.mult)
                nc.vector.tensor_scalar(L.qsin[even, :], L.ps_q[1][even, 0, :], -SCALE, None, ALU.mult)
                nc.vector.tensor_scalar(L.qsin[odd, :], L.ps_q[1][odd, 0, :], SCALE, None, ALU.mult)
                dve.wait_ge(sin_done, 1)
                dve.wait_ge(cos_done, 1)
                nc.vector.tensor_copy(L.kcos[:, :, :], cos4[:, :, 0, :])
                nc.vector.tensor_copy(L.ksin[:, :, :], sin4[:, :, 0, :])
                dve.wait_ge(small_hi, 2)
                nc.vector.tensor_tensor(L.wkva_lo[:, :, :], small_raw[:, :, 0:RANK + DR], L.wkva_hi[:, :, :].bitcast(F32), ALU.subtract)
                nc.vector.tensor_tensor(L.gw_lo[:, :, :], small_raw[:, :, RANK + DR:], L.gw_hi[:, :, :].bitcast(F32), ALU.subtract)
                for h in range(NH):
                    dve.wait_ge(whi_done, h + 1)
                    prod = flat2(L.ps_s[h % 2])
                    rows = slice(RANK * (h % 2), RANK * (h % 2) + RANK)
                    nc.vector.tensor_tensor(L.wq_lo[:, :, h, 0:RANK], prod[:, 0:KD * RANK].rearrange("p (k c) -> p k c", k=KD),
                                            L.wq_hi[:, :, h, 0:RANK].bitcast(F32), ALU.subtract)
                    nc.vector.tensor_tensor(L.wo_lo[rows, h // 2, :], prod[rows, KD * RANK:KD * RANK + D],
                                            L.wo_hi[rows, h // 2, :].bitcast(F32), ALU.subtract).then_inc(wlo_done, 1)
                    for n in parts_after[h]:
                        dve.wait_ge(stage_hi, splits_upto[n])
                        for hi, lo, src in staged[n][1]:
                            nc.vector.tensor_tensor(lo, src, hi.bitcast(F32), ALU.subtract).then_inc(stage_used, 1)

            @block.gpsimd
            def _(pool):
                nc.gpsimd.memset(L.ident[:, :], 0.0).then_inc(ident_step, 1)
                pool.wait_ge(ident_step, 1)
                nc.gpsimd.affine_select(out=L.ident[:, :], in_=L.ident[:, :], compare_op=ALU.not_equal, fill=1.0, base=0,
                                        pattern=[[-1, P]], channel_multiplier=1).then_inc(ident_step, 1)
                steps = 0
                for at in (0, HALF * H):
                    rows_of = [sel_f[row:row + E, :] for row in (0, LO)]
                    nc.gpsimd.memset(sel_f[:, :], 0.0).then_inc(sel_step, 1)
                    pool.wait_ge(sel_step, steps + 1)
                    for part in rows_of:
                        nc.gpsimd.memset(part, 1.0).then_inc(sel_step, 1)
                    pool.wait_ge(sel_step, steps + 3)
                    for part in rows_of:
                        nc.gpsimd.affine_select(out=part, in_=part, compare_op=ALU.is_ge, fill=0.0, base=at,
                                                pattern=[[1, HALF * H]], channel_multiplier=-H).then_inc(sel_step, 1)
                    pool.wait_ge(sel_step, steps + 5)
                    for part in rows_of:
                        nc.gpsimd.affine_select(out=part, in_=part, compare_op=ALU.is_ge, fill=0.0, base=H - 1 - at,
                                                pattern=[[-1, HALF * H]], channel_multiplier=H).then_inc(sel_step, 1)
                    pool.wait_ge(sel_step, steps + 7)
                    nc.gpsimd.tensor_copy(L.sel[:, at:at + HALF * H], sel_f[:, :]).then_inc(sel_step, 1)
                    pool.wait_ge(sel_step, steps + 8)
                    steps += 8
                for loaded in heads_in:
                    pool.wait_ge(loaded, HEAD_LOADS)
                for k in range(KD):
                    for odd in range(2):
                        src = wq_raw[:, k, :, DN + odd:DQK:2]
                        cols = slice(RANK + odd * HR, RANK + (odd + 1) * HR)
                        nc.gpsimd.tensor_copy(L.wq_hi[:, k, :, cols], src).then_inc(rope_hi, 1)
                        pool.wait_ge(rope_hi, 2 * k + odd + 1)
                        nc.gpsimd.tensor_tensor(L.wq_lo[:, k, :, cols], src, L.wq_hi[:, k, :, cols].bitcast(F32), ALU.subtract)


def loop(nc, L, d):
    ev = L.events
    with ExitStack() as ctx:
        def sb(name, shape, dt=F32):
            return ctx.enter_context(nc.sbuf_tensor(name, shape, dt))

        xin = sb("xin", [P, NT, D])
        xhat = sb("xhat", [P, NT, D])
        x2 = sb("x2", [P, NT, D])
        bn = sb("bn", [P, NT, 6])
        one = sb("one", [P, 1])
        carrier = sb("carrier", [P, 1])
        mean_a, mean_k, mean_f = (sb(f"mean_{x}", [P, NT, 2]) for x in "akf")
        var_a, var_k, var_f = (sb(f"var_{x}", [P, NT]) for x in "akf")
        rstd_a, rstd_k, rstd_f = (sb(f"rstd_{x}", [P, NT]) for x in "akf")
        xa_hi, xa_lo = (sb(f"xa_{x}", [P, KD, S], F32R) for x in ("hi", "lo"))
        xf_hi, xf_lo = (sb(f"xf_{x}", [P, KD, S], F32R) for x in ("hi", "lo"))
        kp = sb("kp", [P, NT, P])
        krot = sb("krot", [P, 4, NT, HR])
        kT_hi, kT_lo = (sb(f"kT_{x}", [P, S], F32R) for x in ("hi", "lo"))
        kv_hi, kv_lo = (sb(f"kv_{x}", [P, NT, 2, RANK], F32R) for x in ("hi", "lo"))
        qswap = [sb(f"qswap{n}", [P, 2, S]) for n in range(2)]
        qf = [sb(f"qf{n}", [P, 2, S]) for n in range(2)]
        q_hi, q_lo = ([sb(f"q_{x}{n}", [P, 2, S], F32R) for n in range(2)] for x in ("hi", "lo"))
        nmax = sb("nmax", [P, NH, NT])
        rsum = sb("rsum", [P, NH, NT])
        rinv = sb("rinv", [P, NH, NT])
        probs = [sb(f"probs{n}", [P, NT, S]) for n in range(3)]
        pT_hi, pT_lo = ([sb(f"pT_{x}{n}", [P, NT, S], F32R) for n in range(3)] for x in ("hi", "lo"))
        o_hi, o_lo = ([sb(f"o_{x}{n}", [P, S], F32R) for n in range(2)] for x in ("hi", "lo"))
        lmax = sb("lmax", [P, NT])
        esum = sb("esum", [P, NT])
        einv = sb("einv", [P, NT])
        eprob = sb("eprob", [P, NT, E])
        score = sb("score", [P, NT, 2 * E])
        top = sb("top", [P, NT, E])
        rest = sb("rest", [P, NT, 2 * E])
        comb = sb("comb", [P, NT, E])
        comb2 = sb("comb2", [P, NT, P])
        cT = sb("cT", [CK, S], F32R)
        gate, prod, unit = ([probs[n][:, m, :] for m in range(NT)] for n in range(3))
        u_hi, u_lo = ([t[:, 0, :] for t in ring] for ring in (pT_hi, pT_lo))

        half = (slice(0, RANK), slice(RANK, P))
        even, odd = slice(RANK, RANK + HR), slice(RANK + HR, P)

        def three(out, pairs, start=True, stop=True, skip=False):
            last = None
            terms = [t for sh, sl, mh, ml in pairs for t in ((sh, mh), (sh, ml), (sl, mh))]
            for n, (stat, mov) in enumerate(terms):
                last = nc.tensor.matmul(out, stat, mov, start=start and n == 0, stop=stop and n == len(terms) - 1,
                                        skip_group_check=skip)
            return last

        def tile(j):
            return slice(j * P, (j + 1) * P)

        def due(p):
            return 0 <= p < NP

        block = ctx.enter_context(nc.Block())

        @block.sync
        def _(sp):
            by_token = "(j p) m -> p j m"
            sp.dma_start(xin[:, :, :], d["x"][0, :, :].rearrange(by_token, p=P)).then_inc(ev.x_loaded.sem, 16)

            def store(i):
                sp.wait_ge(ev.osb_done.sem, ev.osb_done.upto(i, 1))
                sp.dma_start(d["out"][bass.ds(i, 1), :, :].rearrange("b (j p) m -> p (b j) m", p=P),
                             x2[:, :, :]).then_inc(ev.out_stored.sem, 16)

            with sp.Fori(0, B - 1) as i:
                sp.wait_ge(ev.x2_done.sem, ev.x2_done.upto(i, 1))
                sp.dma_start(xin[:, :, :], d["x"][bass.ds(i + 1, 1), :, :].rearrange("b (j p) m -> p (b j) m", p=P)
                             ).then_inc(ev.x_loaded.sem, 16)
                store(i)
            store(B - 1)
            sp.wait_ge(ev.out_stored.sem, ev.out_stored.upto(B - 1, 16))

        @block.tensor
        def _(pe):
            def prep_turn(r):
                pe.wait_ge(ev.xha_done.sem, ev.xha_done.upto(r, 1))
                for k in range(KD):
                    for j in range(NT):
                        last = nc.tensor.transpose(L.ps_t[0][:, k, tile(j)], xhat[:, j, tile(k)], L.ident[:, :])
                last.then_inc(ev.xa_turned.sem, 1)

            def prep_kv(r):
                pe.wait_ge(ev.xahi_done.sem, ev.xahi_done.upto(r, 1))
                pe.wait_ge(ev.xalo_done.sem, ev.xalo_done.upto(r, 1))
                for j in range(NT):
                    last = three(L.ps_t[1][:, 0, tile(j)],
                                 [(xa_hi[:, k, tile(j)], xa_lo[:, k, tile(j)], L.wkva_hi[:, k, :], L.wkva_lo[:, k, :])
                                  for k in range(KD)])
                last.then_inc(ev.kv_full.sem, 1)

            def prep_k(r):
                pe.wait_ge(ev.kp_done.sem, ev.kp_done.upto(r, 1))
                for j in range(NT):
                    last = nc.tensor.transpose(L.ps_t[0][:, 0, tile(j)], kp[:, j, :], L.ident[:, :])
                last.then_inc(ev.k_turned.sem, 1)

            def query(i, p):
                if p < 2:
                    pe.wait_ge(ev.su_done.sem, ev.su_done.before(i, CH - 1 + p))
                else:
                    pe.wait_ge(ev.qcos_done.sem, ev.qcos_done.upto(i, p - 1))
                for n in range(2):
                    h = 2 * p + n
                    last = three(L.ps_q[p % 2][:, n, :],
                                 [(L.wq_hi[:, k, h, :], L.wq_lo[:, k, h, :], xa_hi[:, k, :], xa_lo[:, k, :]) for k in range(KD)])
                last.then_inc(ev.q_full.sem, 1)

            def scores(i, h):
                p, n = divmod(h, 2)
                pe.wait_ge(ev.qlo_done.sem, ev.qlo_done.upto(i, p + 1))
                if h == 0:
                    pe.wait_ge(ev.klo_done.sem, ev.klo_done.upto(i, 1))
                if h < 2:
                    pe.wait_ge(ev.cb_done.sem, ev.cb_done.before(i, ER))
                else:
                    pe.wait_ge(ev.exp_done.sem, ev.exp_done.upto(i, h - 1))
                for j in range(NT):
                    last = three(L.ps_s[h % 2][:, j, :],
                                 [(q_hi[p % 2][:, n, tile(j)], q_lo[p % 2][:, n, tile(j)], kT_hi[:, :], kT_lo[:, :])])
                last.then_inc(ev.s_full.sem, 1)

            def turn(i, h):
                pe.wait_ge(ev.pn_done.sem, ev.pn_done.upto(i, h + 1))
                if h == 0:
                    pe.wait_ge(ev.klo_done.sem, ev.klo_done.upto(i, 1))
                elif h == 1:
                    pe.wait_ge(ev.kn_done.sem, ev.kn_done.upto(i, 1))
                else:
                    pe.wait_ge(ev.plo_done.sem, ev.plo_done.upto(i, h - 1))
                for c in range(NT):
                    for j in range(NT):
                        last = nc.tensor.transpose(L.ps_t[h % 2][:, c, tile(j)], probs[h % 3][:, j, tile(c)], L.ident[:, :])
                last.then_inc(ev.t_full.sem, 1)

            def attend(i, h):
                p, n = divmod(h, 2)
                pe.wait_ge(ev.plo_done.sem, ev.plo_done.upto(i, h + 1))
                if n == 0:
                    pe.wait_ge(ev.olo_done.sem, ev.olo_done.upto(i, p))
                if h == 0:
                    pe.wait_ge(ev.kvlo_done.sem, ev.kvlo_done.upto(i, 1))
                twice = "p n c -> p (n c)"
                last = three(L.ps_o[:, n, :],
                             [(kv_hi[:, c, :, :].rearrange(twice), kv_lo[:, c, :, :].rearrange(twice),
                               pT_hi[h % 3][:, c, :], pT_lo[h % 3][:, c, :]) for c in range(NT)])
                last.then_inc(ev.pv_done.sem, 1)

            def project(i, p):
                pe.wait_ge(ev.olo_done.sem, ev.olo_done.upto(i, p + 1))
                if p == 0:
                    pe.wait_ge(ev.osb_done.sem, ev.osb_done.before(i, 1))
                for j in range(NT):
                    last = three(L.ps_y[:, j, :], [(o_hi[p % 2][:, tile(j)], o_lo[p % 2][:, tile(j)], L.wo_hi[:, p, :], L.wo_lo[:, p, :])],
                                 start=p == 0 and j == 0, stop=p == NP - 1, skip=True)
                last.then_inc(ev.out_done.sem, 1)

            def attention(i):
                pe.wait_ge(ev.xalo_done.sem, ev.xalo_done.upto(i, 1))
                for r in range(-4, NP + 3):
                    if due(r + 4):
                        query(i, r + 4)
                    if due(r - 1):
                        turn(i, 2 * (r - 1) + 1)
                    if due(r + 1):
                        scores(i, 2 * (r + 1))
                    if due(r - 3):
                        project(i, r - 3)
                    if due(r + 1):
                        scores(i, 2 * (r + 1) + 1)
                    if due(r - 1):
                        attend(i, 2 * (r - 1))
                    if due(r):
                        turn(i, 2 * r)
                    if due(r - 1):
                        attend(i, 2 * (r - 1) + 1)

            def gate_up(i, m):
                if m < 2:
                    pe.wait_ge(ev.qcos_done.sem, ev.qcos_done.upto(i, NP - 1 + m))
                else:
                    pe.wait_ge(ev.su_done.sem, ev.su_done.upto(i, m - 1))
                rows = chunk_rows(m)
                for n in range(2):
                    if m < ES:
                        cols = slice(m * P, m * P + rows)
                        w = [(L.sgu_hi[:, n * KD + k, cols], L.sgu_lo[:, n * KD + k, cols]) for k in range(KD)]
                    else:
                        hi, lo = ((L.mg_hi, L.mg_lo), (L.mu_hi, L.mu_lo))[n]
                        w = [(hi[:, k, tile(m - ES)], lo[:, k, tile(m - ES)]) for k in range(KD)]
                    last = three(L.ps_q[m % 2][0:rows, n, :],
                                 [(*w[k], xf_hi[:, k, :], xf_lo[:, k, :]) for k in range(KD)])
                last.then_inc(ev.gu_full.sem, 1)

            def spread(i, m):
                c = m - ES
                if c == 0:
                    pe.wait_ge(ev.combhi_done.sem, ev.combhi_done.upto(i, 1))
                if c >= 2:
                    pe.wait_ge(ev.cb_done.sem, ev.cb_done.upto(i, c - 1))
                nc.tensor.matmul(L.ps_s[c % 2][:, 0, :], L.sel[:, tile(c)], cT[:, :], start=True, stop=True
                                 ).then_inc(ev.cb_full.sem, 1)

            def down(i, m):
                pe.wait_ge(ev.ulo_done.sem, ev.ulo_done.upto(i, m + 1))
                if m == 0:
                    pe.wait_ge(ev.x2_done.sem, ev.x2_done.upto(i, 1))
                rows = chunk_rows(m)
                hi, lo, c = (L.sd_hi, L.sd_lo, m) if m < ES else (L.md_hi, L.md_lo, m - ES)
                for j in range(NT):
                    last = three(L.ps_y[:, j, :], [(u_hi[m % 3][0:rows, tile(j)], u_lo[m % 3][0:rows, tile(j)],
                                                    hi[0:rows, c, :], lo[0:rows, c, :])],
                                 start=m == 0 and j == 0, stop=m == CH - 1, skip=True)
                last.then_inc(ev.down_done.sem, 1)

            def experts(i, prep):
                pe.wait_ge(ev.xhf_done.sem, ev.xhf_done.upto(i, 1))
                pe.wait_ge(ev.plo_done.sem, ev.plo_done.upto(i, NH))
                for k in range(KD):
                    for j in range(NT):
                        last = nc.tensor.transpose(L.ps_t[0][:, k, tile(j)], xhat[:, j, tile(k)], L.ident[:, :])
                last.then_inc(ev.xf_turned.sem, 1)
                pe.wait_ge(ev.xfhi_done.sem, ev.xfhi_done.upto(i, 1))
                pe.wait_ge(ev.xflo_done.sem, ev.xflo_done.upto(i, 1))
                pe.wait_ge(ev.exp_done.sem, ev.exp_done.upto(i, NH))
                for j in range(NT):
                    last = three(L.ps_s[0][:, 0, j * E:(j + 1) * E],
                                 [(xf_hi[:, k, tile(j)], xf_lo[:, k, tile(j)], L.gw_hi[:, k, :], L.gw_lo[:, k, :]) for k in range(KD)])
                last.then_inc(ev.logits_full.sem, 1)
                for m in range(CH + 2):
                    if m < CH:
                        gate_up(i, m)
                    if m == ES - 1:
                        pe.wait_ge(ev.comb_done.sem, ev.comb_done.upto(i, 1))
                        for j in range(NT):
                            last = nc.tensor.transpose(L.ps_s[1][:, 0, tile(j)], comb2[:, j, :], L.ident[:, :])
                        last.then_inc(ev.comb_turned.sem, 1)
                    if ES <= m < CH:
                        spread(i, m)
                    if m >= 2:
                        down(i, m - 2)
                    if prep:
                        if m == 4:
                            prep_turn(i + 1)
                        if m == 6:
                            prep_kv(i + 1)
                        if m == 11:
                            prep_k(i + 1)

            prep_turn(0)
            prep_kv(0)
            prep_k(0)
            with pe.Fori(0, B - 1) as i:
                attention(i)
                experts(i, True)
            attention(B - 1)
            experts(B - 1, False)

        @block.scalar
        def _(act):
            copy = lambda out, src: nc.scalar.activation(out, src, ACT.Copy)

            def prep_x(r):
                act.wait_ge(ev.xa_turned.sem, ev.xa_turned.upto(r, 1))
                copy(xa_hi[:, :, :], L.ps_t[0][:, :, :]).then_inc(ev.xahi_done.sem, 1)

            def prep_k(r):
                act.wait_ge(ev.k_turned.sem, ev.k_turned.upto(r, 1))
                copy(kT_hi[:, :], L.ps_t[0][:, 0, :]).then_inc(ev.khi_done.sem, 1)

            def swap(i, p):
                act.wait_ge(ev.q_full.sem, ev.q_full.upto(i, p + 1))
                if p >= 2:
                    act.wait_ge(ev.qrot_done.sem, ev.qrot_done.upto(i, p - 1))
                copy(qswap[p % 2][even, :, :], L.ps_q[p % 2][odd, :, :])
                copy(qswap[p % 2][odd, :, :], L.ps_q[p % 2][even, :, :]).then_inc(ev.swap_done.sem, 1)

            def query_hi(i, p):
                act.wait_ge(ev.qrot_done.sem, ev.qrot_done.upto(i, p + 1))
                if p >= 2:
                    act.wait_ge(ev.s_full.sem, ev.s_full.upto(i, 2 * p - 2))
                copy(q_hi[p % 2][:, :, :], qf[p % 2][:, :, :]).then_inc(ev.qhi_done.sem, 1)

            def exps(i, h):
                act.wait_ge(ev.max_done.sem, ev.max_done.upto(i, h + 1))
                if h >= 3:
                    act.wait_ge(ev.t_full.sem, ev.t_full.upto(i, h - 2))
                for j in range(NT):
                    last = nc.scalar.activation(probs[h % 3][:, j, :], L.ps_s[h % 2][:, j, :], ACT.Exp,
                                                bias=nmax[:, h, j:j + 1], accum_out=rsum[:, h, j:j + 1])
                last.then_inc(ev.exp_done.sem, 1)

            def probs_hi(i, h):
                act.wait_ge(ev.t_full.sem, ev.t_full.upto(i, h + 1))
                if h >= 3:
                    act.wait_ge(ev.pv_done.sem, ev.pv_done.upto(i, h - 2))
                copy(pT_hi[h % 3][:, :, :], L.ps_t[h % 2][:, :, :]).then_inc(ev.phi_done.sem, 1)

            def attended_hi(i, p):
                act.wait_ge(ev.pv_done.sem, ev.pv_done.upto(i, 2 * p + 2))
                if p >= 2:
                    act.wait_ge(ev.out_done.sem, ev.out_done.upto(i, p - 1))
                for n in range(2):
                    last = copy(o_hi[p % 2][half[n], :], L.ps_o[half[n], n, :])
                last.then_inc(ev.ohi_done.sem, 1)

            def attention(i):
                for r in range(-4, NP + 1):
                    if due(r):
                        exps(i, 2 * r + 1)
                    if due(r - 1):
                        probs_hi(i, 2 * (r - 1) + 1)
                    if due(r + 2):
                        query_hi(i, r + 2)
                    if due(r + 4):
                        swap(i, r + 4)
                    if due(r + 1):
                        exps(i, 2 * (r + 1))
                    if due(r):
                        probs_hi(i, 2 * r)
                    if due(r - 1):
                        attended_hi(i, r - 1)

            def experts(i, prep):
                act.wait_ge(ev.xf_turned.sem, ev.xf_turned.upto(i, 1))
                copy(xf_hi[:, :, :], L.ps_t[0][:, :, :]).then_inc(ev.xfhi_done.sem, 1)
                act.wait_ge(ev.lmax_done.sem, ev.lmax_done.upto(i, 1))
                for j in range(NT):
                    last = nc.scalar.activation(eprob[:, j, :], L.ps_s[0][:, 0, j * E:(j + 1) * E], ACT.Exp,
                                                bias=lmax[:, j:j + 1], accum_out=esum[:, j:j + 1])
                last.then_inc(ev.gate_exp_done.sem, 1)
                for m in range(CH):
                    act.wait_ge(ev.gu_full.sem, ev.gu_full.upto(i, m + 1))
                    if m >= 2:
                        act.wait_ge(ev.su_done.sem, ev.su_done.upto(i, m - 1))
                    rows = chunk_rows(m)
                    nc.scalar.activation(gate[m % 2][0:rows, :], L.ps_q[m % 2][0:rows, 0, :], ACT.Silu).then_inc(ev.silu_done.sem, 1)
                    if m == ES - 1:
                        act.wait_ge(ev.comb_turned.sem, ev.comb_turned.upto(i, 1))
                        copy(cT[:, :], L.ps_s[1][0:CK, 0, :]).then_inc(ev.combhi_done.sem, 1)
                    if prep:
                        if m == 4:
                            prep_x(i + 1)
                        if m == 11:
                            prep_k(i + 1)

            prep_x(0)
            prep_k(0)
            with act.Fori(0, B - 1) as i:
                attention(i)
                experts(i, True)
            attention(B - 1)
            experts(B - 1, False)

        @block.vector
        def _(dve):
            vec = nc.vector

            def minus_hi(lo, src, hi):
                return vec.tensor_tensor(lo, src, hi.bitcast(F32), ALU.subtract)

            class Steps:

                def __init__(self, events, i):
                    self.events, self.i, self.n = events, i, 0

                def __call__(self, ins, carry=False):
                    self.n += 1
                    ins.then_inc(self.events.sem, 1)
                    dve.wait_ge(self.events.sem, self.events.upto(self.i, self.n))
                    if carry:
                        vec.memset(carrier[:, :], 0.0)

                def end(self):
                    assert self.n == self.events.per_round

            def moments(step, src, mean, var, done):
                for j in range(NT):
                    last = vec.bn_stats(bn[:, j, :], src(j))
                step(last, carry=True)
                for j in range(NT):
                    last = vec.bn_aggr(mean[:, j, :], bn[:, j, :])
                step(last)
                vec.tensor_scalar(var[:, :], mean[:, :, 1], EPS, None, ALU.add).then_inc(done.sem, 1)

            def normalise(out, src, mean, rstd, done):
                for j in range(NT):
                    last = vec.tensor_scalar(out(j), src(j), mean[:, j, 0:1], rstd[:, j:j + 1], ALU.subtract, ALU.mult)
                last.then_inc(done.sem, 1)

            def kv_tile(j):
                return L.ps_t[1][:, 0, j * P:j * P + RANK]

            def prep_moments(r, step):
                dve.wait_ge(ev.x_loaded.sem, ev.x_loaded.upto(r, 16))
                moments(step, lambda j: xin[:, j, :], mean_a, var_a, ev.vara_done)

            def prep_normal(r):
                dve.wait_ge(ev.vara_done.sem, ev.vara_done.upto(r, 1))
                dve.wait_ge(ev.rsa_done.sem, ev.rsa_done.upto(r, 1))
                normalise(lambda j: xhat[:, j, :], lambda j: xin[:, j, :], mean_a, rstd_a, ev.xha_done)

            def prep_x(r):
                dve.wait_ge(ev.xahi_done.sem, ev.xahi_done.upto(r, 1))
                minus_hi(xa_lo[:, :, :], L.ps_t[0][:, :, :], xa_hi[:, :, :]).then_inc(ev.xalo_done.sem, 1)

            def prep_kv(r, step):
                dve.wait_ge(ev.kv_full.sem, ev.kv_full.upto(r, 1))
                moments(step, kv_tile, mean_k, var_k, ev.vark_done)
                rot = L.ps_t[1][:, 0, :].rearrange("p (j n) -> p j n", j=NT)
                evens, odds = rot[:, :, RANK::2], rot[:, :, RANK + 1::2]
                for n, (x, trig) in enumerate(((evens, L.kcos), (odds, L.ksin), (evens, L.ksin), (odds, L.kcos))):
                    last = vec.tensor_tensor(krot[:, n, :, :], x, trig[:, :, :], ALU.mult)
                last.then_inc(ev.kr_done.sem, 1)

            def prep_kn(r):
                dve.wait_ge(ev.vark_done.sem, ev.vark_done.upto(r, 1))
                dve.wait_ge(ev.rsk_done.sem, ev.rsk_done.upto(r, 1))
                normalise(lambda j: kp[:, j, 0:RANK], kv_tile, mean_k, rstd_k, ev.kn_done)

            def prep_k(r):
                dve.wait_ge(ev.khi_done.sem, ev.khi_done.upto(r, 1))
                minus_hi(kT_lo[:, :], L.ps_t[0][:, 0, :], kT_hi[:, :]).then_inc(ev.klo_done.sem, 1)

            def query_cos(i, p):
                dve.wait_ge(ev.swap_done.sem, ev.swap_done.upto(i, p + 1))
                if p >= 2:
                    dve.wait_ge(ev.qlo_done.sem, ev.qlo_done.upto(i, p - 1))
                vec.tensor_tensor(qf[p % 2][:, :, :], L.ps_q[p % 2][:, :, :], L.qcos[:, :].unsqueeze(1).to_broadcast([P, 2, S]),
                                  ALU.mult).then_inc(ev.qcos_done.sem, 1)

            def query_lo(i, p):
                dve.wait_ge(ev.qhi_done.sem, ev.qhi_done.upto(i, p + 1))
                minus_hi(q_lo[p % 2][:, :, :], qf[p % 2][:, :, :], q_hi[p % 2][:, :, :]).then_inc(ev.qlo_done.sem, 1)

            def maxima(i, h):
                dve.wait_ge(ev.s_full.sem, ev.s_full.upto(i, h + 1))
                vec.tensor_reduce(nmax[:, h, :], L.ps_s[h % 2][:, :, :], AX.X, ALU.max, negate=True).then_inc(ev.max_done.sem, 1)

            def inverse(i, h):
                dve.wait_ge(ev.exp_done.sem, ev.exp_done.upto(i, h + 1))
                vec.reciprocal(rinv[:, h, :], rsum[:, h, :]).then_inc(ev.rinv_done.sem, 1)

            def probs_lo(i, h):
                dve.wait_ge(ev.phi_done.sem, ev.phi_done.upto(i, h + 1))
                minus_hi(pT_lo[h % 3][:, :, :], L.ps_t[h % 2][:, :, :], pT_hi[h % 3][:, :, :]).then_inc(ev.plo_done.sem, 1)

            def attended_lo(i, p):
                dve.wait_ge(ev.ohi_done.sem, ev.ohi_done.upto(i, p + 1))
                for n in range(2):
                    last = minus_hi(o_lo[p % 2][half[n], :], L.ps_o[half[n], n, :], o_hi[p % 2][half[n], :])
                last.then_inc(ev.olo_done.sem, 1)

            def attention(i):
                for r in range(-3, NP + 2):
                    if due(r + 1):
                        query_lo(i, r + 1)
                    if due(r + 3):
                        query_cos(i, r + 3)
                    if due(r):
                        inverse(i, 2 * r)
                    if due(r - 1):
                        probs_lo(i, 2 * (r - 1))
                    if due(r - 2):
                        attended_lo(i, r - 2)
                    if due(r):
                        inverse(i, 2 * r + 1)
                    if due(r + 1):
                        maxima(i, 2 * (r + 1))
                    if due(r - 1):
                        probs_lo(i, 2 * (r - 1) + 1)
                    if due(r + 1):
                        maxima(i, 2 * (r + 1) + 1)

            def experts(i, prep):
                step = Steps(ev.ffn_step, i)
                dve.wait_ge(ev.out_done.sem, ev.out_done.upto(i, NP))
                dve.wait_ge(ev.out_stored.sem, ev.out_stored.before(i, 16))
                vec.tensor_tensor(x2[:, :, :], L.ps_y[:, :, :], xin[:, :, :], ALU.add).then_inc(ev.x2_done.sem, 1)
                dve.wait_ge(ev.x2_done.sem, ev.x2_done.upto(i, 1))
                moments(step, lambda j: x2[:, j, :], mean_f, var_f, ev.varf_done)
                dve.wait_ge(ev.varf_done.sem, ev.varf_done.upto(i, 1))
                dve.wait_ge(ev.rsf_done.sem, ev.rsf_done.upto(i, 1))
                normalise(lambda j: xhat[:, j, :], lambda j: x2[:, j, :], mean_f, rstd_f, ev.xhf_done)
                dve.wait_ge(ev.xfhi_done.sem, ev.xfhi_done.upto(i, 1))
                minus_hi(xf_lo[:, :, :], L.ps_t[0][:, :, :], xf_hi[:, :, :]).then_inc(ev.xflo_done.sem, 1)
                dve.wait_ge(ev.logits_full.sem, ev.logits_full.upto(i, 1))
                vec.tensor_reduce(lmax[:, :], L.ps_s[0][:, 0, 0:NT * E].rearrange("p (j e) -> p j e", j=NT), AX.X, ALU.max,
                                  negate=True).then_inc(ev.lmax_done.sem, 1)
                dve.wait_ge(ev.gate_exp_done.sem, ev.gate_exp_done.upto(i, 1))
                step(vec.reciprocal(einv[:, :], esum[:, :]))
                for j in range(NT):
                    last = vec.tensor_scalar(score[:, j, 0:E], eprob[:, j, :], einv[:, j:j + 1], None, ALU.mult)
                step(last, carry=True)
                for j in range(NT):
                    last = vec.max(top[:, j, :], score[:, j, 0:E])
                step(last)
                step(vec.tensor_copy(top[:, :, TOP:E], L.sentinel[:, 0:E - TOP].unsqueeze(1).to_broadcast([P, NT, E - TOP])),
                     carry=True)
                for j in range(NT):
                    last = vec.match_replace(rest[:, j, :], top[:, j, :], score[:, j, :], 0.0)
                step(last)
                step(vec.tensor_tensor(comb[:, :, :], score[:, :, 0:E], rest[:, :, 0:E], ALU.subtract))
                step(vec.tensor_copy(comb2[:, :, 0:E].bitcast(F32R), comb[:, :, :]))
                vec.tensor_tensor(comb2[:, :, LO:CK], comb[:, :, :], comb2[:, :, 0:E], ALU.subtract).then_inc(ev.comb_done.sem, 1)
                step.end()
                prep_step = Steps(ev.prep_step, i + 1) if prep else None
                for m in range(CH):
                    rows = chunk_rows(m)
                    dve.wait_ge(ev.silu_done.sem, ev.silu_done.upto(i, m + 1))
                    up, act = L.ps_q[m % 2][0:rows, 1, :], gate[m % 2][0:rows, :]
                    if m >= 2:
                        dve.wait_ge(ev.ulo_done.sem, ev.ulo_done.upto(i, m - 1))
                    if m < ES:
                        vec.tensor_tensor(unit[m % 2][0:rows, :], up, act, ALU.mult).then_inc(ev.su_done.sem, 1)
                    else:
                        c = m - ES
                        vec.tensor_tensor(prod[m % 2], up, act, ALU.mult).then_inc(ev.su_done.sem, 1)
                        dve.wait_ge(ev.su_done.sem, ev.su_done.upto(i, m + 1))
                        dve.wait_ge(ev.cb_full.sem, ev.cb_full.upto(i, c + 1))
                        vec.tensor_tensor(unit[m % 2], L.ps_s[c % 2][:, 0, :], prod[m % 2], ALU.mult
                                          ).then_inc(ev.cb_done.sem, 1)
                    if prep:
                        if m == 1:
                            prep_moments(i + 1, prep_step)
                        if m == 3:
                            prep_normal(i + 1)
                        if m == 5:
                            prep_x(i + 1)
                        if m == 8:
                            prep_kv(i + 1, prep_step)
                        if m == 9:
                            prep_kn(i + 1)
                        if m == 12:
                            prep_k(i + 1)
                            prep_step.end()
                dve.wait_ge(ev.down_done.sem, ev.down_done.upto(i, CH))
                vec.tensor_tensor(x2[:, :, :], L.ps_y[:, :, :], x2[:, :, :], ALU.add).then_inc(ev.osb_done.sem, 1)

            vec.tensor_copy(score[:, :, E:2 * E], L.sentinel[:, :].unsqueeze(1).to_broadcast([P, NT, E]))
            vec.memset(comb2[:, :, :], 0.0)
            for n in range(2):
                last = vec.memset(qswap[n][0:RANK, :, :], 0.0)
            last.then_inc(ev.latent_zero, 1)
            step = Steps(ev.prep_step, 0)
            prep_moments(0, step)
            prep_normal(0)
            prep_x(0)
            prep_kv(0, step)
            prep_kn(0)
            prep_k(0)
            step.end()
            with dve.Fori(0, B - 1) as i:
                attention(i)
                experts(i, True)
            attention(B - 1)
            experts(B - 1, False)

        @block.gpsimd
        def _(pool):
            gp = nc.gpsimd

            def hi_of(hi, src):
                ones = one[0:src.shape[0], 0:1]
                while ones.ndim < src.ndim:
                    ones = ones.unsqueeze(1)
                return gp.tensor_tensor(hi, src, ones.to_broadcast(list(src.shape)), ALU.mult)

            def power(var, rstd, ready, done, r):
                pool.wait_ge(ready.sem, ready.upto(r, 1))
                gp.tensor_tensor(rstd[:, :], var[:, :], L.minus_half[:, :], ALU.pow).then_inc(done.sem, 1)

            def prep_kp(r):
                pool.wait_ge(ev.kr_done.sem, ev.kr_done.upto(r, 1))
                gp.tensor_tensor(kp[:, :, RANK:RANK + HR], krot[:, 0, :, :], krot[:, 1, :, :], ALU.subtract)
                gp.tensor_tensor(kp[:, :, RANK + HR:P], krot[:, 2, :, :], krot[:, 3, :, :], ALU.add)
                pool.wait_ge(ev.kn_done.sem, ev.kn_done.upto(r, 1))
                lat = kp[:, :, 0:RANK]
                wide = lambda t: t[:, :].unsqueeze(1).to_broadcast([P, NT, RANK])
                gp.tensor_tensor(lat, lat, wide(L.gamma), ALU.mult).then_inc(ev.kp_part.sem, 1)
                pool.wait_ge(ev.kp_part.sem, ev.kp_part.upto(r, 1))
                gp.tensor_tensor(lat, lat, wide(L.beta), ALU.add).then_inc(ev.kp_done.sem, 1)
                pool.wait_ge(ev.kp_done.sem, ev.kp_done.upto(r, 1))
                for n in range(2):
                    last = hi_of(kv_hi[:, :, n, :], lat)
                last.then_inc(ev.kvhi_done.sem, 1)
                pool.wait_ge(ev.kvhi_done.sem, ev.kvhi_done.upto(r, 1))
                for n in range(2):
                    last = gp.tensor_tensor(kv_lo[:, :, n, :], lat, kv_hi[:, :, n, :].bitcast(F32), ALU.subtract)
                last.then_inc(ev.kvlo_done.sem, 1)

            def rotate(i, p):
                pool.wait_ge(ev.swap_done.sem, ev.swap_done.upto(i, p + 1))
                qs = qswap[p % 2][:, :, :]
                gp.tensor_tensor(qs, qs, L.qsin[:, :].unsqueeze(1).to_broadcast([P, 2, S]), ALU.mult).then_inc(ev.qrot_part.sem, 1)

            def rotate_add(i, p):
                pool.wait_ge(ev.qrot_part.sem, ev.qrot_part.upto(i, p + 1))
                pool.wait_ge(ev.qcos_done.sem, ev.qcos_done.upto(i, p + 1))
                gp.tensor_tensor(qf[p % 2][:, :, :], qf[p % 2][:, :, :], qswap[p % 2][:, :, :], ALU.add).then_inc(ev.qrot_done.sem, 1)

            def normal(i, h):
                pool.wait_ge(ev.rinv_done.sem, ev.rinv_done.upto(i, h + 1))
                gp.tensor_tensor(probs[h % 3][:, :, :], probs[h % 3][:, :, :], rinv[:, h, :].unsqueeze(2).to_broadcast([P, NT, S]),
                                 ALU.mult).then_inc(ev.pn_done.sem, 1)

            def attention(i):
                for r in range(-3, NP - 1):
                    if due(r + 3):
                        rotate(i, r + 3)
                    if due(r + 3):
                        rotate_add(i, r + 3)
                    if due(r + 1):
                        normal(i, 2 * (r + 1))
                    if due(r + 1):
                        normal(i, 2 * (r + 1) + 1)

            def experts(i, prep):
                power(var_f, rstd_f, ev.varf_done, ev.rsf_done, i)
                for m in range(CH):
                    if m < ES:
                        pool.wait_ge(ev.su_done.sem, ev.su_done.upto(i, m + 1))
                    else:
                        pool.wait_ge(ev.cb_done.sem, ev.cb_done.upto(i, m - ES + 1))
                    if m >= 3:
                        pool.wait_ge(ev.down_done.sem, ev.down_done.upto(i, m - 2))
                    hi_of(u_hi[m % 3], unit[m % 2]).then_inc(ev.uhi_done.sem, 1)
                    pool.wait_ge(ev.uhi_done.sem, ev.uhi_done.upto(i, m + 1))
                    gp.tensor_tensor(u_lo[m % 3], unit[m % 2], u_hi[m % 3].bitcast(F32),
                                     ALU.subtract).then_inc(ev.ulo_done.sem, 1)
                    if prep:
                        if m == 1:
                            power(var_a, rstd_a, ev.vara_done, ev.rsa_done, i + 1)
                        if m == 8:
                            power(var_k, rstd_k, ev.vark_done, ev.rsk_done, i + 1)
                        if m == 9:
                            prep_kp(i + 1)

            gp.memset(one[:, :], 1.0).then_inc(ev.ones_set, 1)
            pool.wait_ge(ev.ones_set, 1)
            pool.wait_ge(ev.latent_zero, 1)
            power(var_a, rstd_a, ev.vara_done, ev.rsa_done, 0)
            power(var_k, rstd_k, ev.vark_done, ev.rsk_done, 0)
            prep_kp(0)
            with pool.Fori(0, B - 1) as i:
                attention(i)
                experts(i, True)
            attention(B - 1)
            experts(B - 1, False)


def layer(nc, d):
    with ExitStack() as ctx:
        L = Layer(nc, ctx)
        weights(nc, L, d)
        loop(nc, L, d)


_INS = {"L0_attn_hidden_states": "x", "L0_attn_freqs_cis": "freqs", "L0_attn_Wq": "Wq", "L0_attn_Wkv_a": "Wkv_a",
        "L0_attn_kv_gamma": "gamma", "L0_attn_kv_beta": "beta", "L0_attn_Wkv_b": "Wkv_b", "L0_attn_Wout": "Wout",
        "L0_ffn_gate_w": "gate_w", "L0_ffn_w_gate": "w_gate", "L0_ffn_w_up": "w_up", "L0_ffn_w_down": "w_down",
        "L0_ffn_sw_gate": "sw_gate", "L0_ffn_sw_up": "sw_up", "L0_ffn_sw_down": "sw_down"}


def kernel(**inputs):
    import numpy as np
    import concourse.bacc as bacc
    from concourse.bass_utils import run_bass_kernel_spmd

    nc = bacc.Bacc("TRN2", target_bir_lowering=False, num_devices=1)
    arrays, d = {}, {}
    for name, short in _INS.items():
        a = np.ascontiguousarray(inputs[name])
        arrays[f"{short}_dram"] = a
        d[short] = nc.dram_tensor(f"{short}_dram", a.shape, F32, kind="ExternalInput").ap()
    d["out"] = nc.dram_tensor("out_dram", (B, S, D), F32, kind="ExternalOutput").ap()
    layer(nc, d)
    r = run_bass_kernel_spmd(nc, [arrays], core_ids=[0])
    return r.results[0]["out_dram"]
```

```python
from contextlib import ExitStack

import concourse.bass as bass
from concourse import mybir

F32 = mybir.dt.float32
F32R = mybir.dt.float32r
ALU = mybir.AluOpType
ACT = mybir.ActivationFunctionType
AX = mybir.AxisListType

P = 128
B, S, D = 8, 256, 256
NT = S // P
KD = D // P
NH, DN, DR, DV, RANK = 16, 128, 64, 128, 64
DQK = DN + DR
NP = NH // 2
HR = DR // 2
E, H = 8, 176
EH = E * H
HS = 2 * H
ER = EH // P
ES = -(-HS // P)
CH = ES + ER
LO = 32
CK = LO + E
TOP = 2
SCALE = float(DQK) ** -0.5
EPS = 1e-5
DOWN = 3
HALF = E // 2
GROUP = 2
RING = 5
TW = 2 * P + 3 * RANK


def chunk_rows(m):
    return min(P, HS - m * P) if m < ES else P


def flat2(t):
    return t[:, :, :].rearrange("p a b -> p (a b)")


class Events:

    def __init__(self, sem, per_round, head=0):
        self.sem, self.per_round, self.head = sem, per_round, head

    def upto(self, i, n):
        return i * self.per_round + (n + self.head)

    def before(self, i, n):
        assert n + self.head - self.per_round >= 1
        return i * self.per_round + (n + self.head - self.per_round)


class AllEvents:

    def __init__(self, nc, ctx):
        def count(name, per_round, head=0):
            return Events(ctx.enter_context(nc.semaphore(name)), per_round, head)

        self.x_loaded = count("x_loaded", 16)
        self.xnext_loaded = count("xnext_loaded", 16)
        self.out_stored = count("out_stored", 16, head=16)
        self.q_full = count("q_full", NP)
        self.out_done = count("out_done", NP)
        self.s_full = count("s_full", NH)
        self.t_full = count("t_full", NH)
        self.pv_done = count("pv_done", NH, head=NH)
        self.gu_full = count("gu_full", CH)
        self.down_done = count("down_done", CH)
        self.cb_full = count("cb_full", ER)
        self.xf_turned = count("xf_turned", 1)
        self.logits_full = count("logits_full", 1)
        self.comb_turned = count("comb_turned", 1)
        self.xa_turned = count("xa_turned", 1)
        self.kv_full = count("kv_full", 1)
        self.k_turned = count("k_turned", 1)
        self.swap_done = count("swap_done", NP)
        self.qhi_done = count("qhi_done", NP)
        self.ohi_done = count("ohi_done", NP)
        self.exp_done = count("exp_done", NH, head=NH)
        self.phi_done = count("phi_done", NH)
        self.silu_done = count("silu_done", CH)
        self.xfhi_done = count("xfhi_done", 1)
        self.gate_exp_done = count("gate_exp_done", 1)
        self.combhi_done = count("combhi_done", 1)
        self.xahi_done = count("xahi_done", 1)
        self.khi_done = count("khi_done", 1)
        self.qcos_done = count("qcos_done", NP, head=NP)
        self.qlo_done = count("qlo_done", NP)
        self.olo_done = count("olo_done", NP, head=1)
        self.max_done = count("max_done", NH)
        self.rinv_done = count("rinv_done", NH)
        self.plo_done = count("plo_done", NH)
        self.su_done = count("su_done", CH, head=CH)
        self.cb_done = count("cb_done", ER, head=ER)
        self.x2_done = count("x2_done", 1)
        self.varf_done = count("varf_done", 1)
        self.xhf_done = count("xhf_done", 1)
        self.xflo_done = count("xflo_done", 1)
        self.lmax_done = count("lmax_done", 1)
        self.comb_done = count("comb_done", 1)
        self.osb_done = count("osb_done", 1, head=1)
        self.vara_done = count("vara_done", 1)
        self.xha_done = count("xha_done", 1)
        self.xalo_done = count("xalo_done", 1)
        self.vark_done = count("vark_done", 1)
        self.kn_done = count("kn_done", 1)
        self.kr_done = count("kr_done", 1)
        self.klo_done = count("klo_done", 1)
        self.ffn_step = count("ffn_step", 9)
        self.prep_x_step = count("prep_x_step", 2)
        self.prep_k_step = count("prep_k_step", 2)
        self.qrot_part = count("qrot_part", NP)
        self.qrot_done = count("qrot_done", NP)
        self.pn_done = count("pn_done", NH)
        self.uhi_done = count("uhi_done", CH)
        self.ulo_done = count("ulo_done", CH, head=CH)
        self.rsf_done = count("rsf_done", 1)
        self.rsa_done = count("rsa_done", 1)
        self.rsk_done = count("rsk_done", 1)
        self.kp_part = count("kp_part", 1)
        self.kp_done = count("kp_done", 1)
        self.kvhi_done = count("kvhi_done", 1)
        self.kvlo_done = count("kvlo_done", 1)
        self.zeros_set = ctx.enter_context(nc.semaphore("zeros_set"))
        self.part_in = [ctx.enter_context(nc.semaphore(f"part_in{n}")) for n in range(3 + 4 * KD + -(-ER // DOWN))]
        self.part_hi, self.part_lo = (ctx.enter_context(nc.semaphore(f"part_{x}")) for x in ("hi", "lo"))
        self.ones_set = ctx.enter_context(nc.semaphore("ones_set"))


class Layer:

    def __init__(self, nc, ctx):
        def sb(name, shape, dt=F32):
            return ctx.enter_context(nc.sbuf_tensor(name, shape, dt))

        def bank(name):
            return ctx.enter_context(nc.psum_tensor(name, [P, 2, S], F32))

        self.events = AllEvents(nc, ctx)
        self.wq_hi, self.wq_lo = (sb(f"wq_{x}", [P, KD, NH, P], F32R) for x in ("hi", "lo"))
        self.wo_hi, self.wo_lo = (sb(f"wo_{x}", [P, NP, D], F32R) for x in ("hi", "lo"))
        self.wkva_hi, self.wkva_lo = (sb(f"wkva_{x}", [P, KD, RANK + DR], F32R) for x in ("hi", "lo"))
        self.gw_hi, self.gw_lo = (sb(f"gw_{x}", [P, KD, E], F32R) for x in ("hi", "lo"))
        experts = {"mg": [P, KD, EH], "mu": [P, KD, EH], "md": [P, ER, D], "sgu": [P, 2 * KD, HS], "sd": [P, ES, D]}
        self.mg_hi, self.mu_hi, self.md_hi, self.sgu_hi, self.sd_hi = (
            sb(f"{name}_hi", shape, F32R) for name, shape in experts.items())
        with ExitStack() as loaded:
            self.mg_raw, self.mu_raw, self.md_raw, self.sgu_raw, self.sd_raw = (
                loaded.enter_context(nc.sbuf_tensor(f"{name}_raw", shape, F32)) for name, shape in experts.items())
        self.mg_lo, self.mu_lo, self.md_lo, self.sgu_lo, self.sd_lo = (
            sb(f"{name}_lo", shape, F32R) for name, shape in experts.items())
        self.ident = sb("ident", [P, P])
        self.sel = sb("sel", [CK, EH], F32R)
        self.qcos = sb("qcos", [P, S])
        self.qsin = sb("qsin", [P, S])
        self.kcos = sb("kcos", [P, NT, HR])
        self.ksin = sb("ksin", [P, NT, HR])
        self.gamma = sb("gamma", [P, RANK])
        self.beta = sb("beta", [P, RANK])
        self.minus_half = sb("minus_half", [P, NT])
        self.sentinel = sb("sentinel", [P, E])
        self.xnext = sb("xnext", [P, NT, D])
        self.xhat_a = sb("xhat_a", [P, NT, D])
        self.bn = sb("bn", [P, NT, 6])
        self.one = sb("one", [P, 1])
        self.carrier = sb("carrier", [P, 1])
        self.mean_a, self.mean_k = (sb(f"mean_{x}", [P, NT, 2]) for x in "ak")
        self.var_a, self.var_k = (sb(f"var_{x}", [P, NT]) for x in "ak")
        self.rstd_a, self.rstd_k = (sb(f"rstd_{x}", [P, NT]) for x in "ak")
        self.kp = sb("kp", [P, NT, P])
        self.krot = sb("krot", [P, 4, NT, HR])
        self.xa_hi, self.xa_lo = (sb(f"xa_{x}", [P, KD, S], F32R) for x in ("hi", "lo"))
        self.kT_hi, self.kT_lo = (sb(f"kT_{x}", [P, S], F32R) for x in ("hi", "lo"))
        self.kv_hi, self.kv_lo = (sb(f"kv_{x}", [P, NT, 3, RANK], F32R) for x in ("hi", "lo"))
        self.ps_q = [bank(f"ps_q{n}") for n in range(2)]
        self.ps_s = [bank(f"ps_s{n}") for n in range(2)]
        self.ps_t = [bank(f"ps_t{n}") for n in range(2)]
        self.ps_o = bank("ps_o")
        self.ps_y = bank("ps_y")


def tile(j):
    return slice(j * P, (j + 1) * P)


def products(nc):
    def three(out, pairs, start=True, stop=True, skip=False):
        last = None
        terms = [t for sh, sl, mh, ml in pairs for t in ((sh, mh), (sh, ml), (sl, mh))]
        for n, (stat, mov) in enumerate(terms):
            last = nc.tensor.matmul(out, stat, mov, start=start and n == 0, stop=stop and n == len(terms) - 1,
                                    skip_group_check=skip)
        return last

    return three


def prepare_pe(nc, L, pe):
    ev, three = L.events, products(nc)
    xhat_a, xa_hi, xa_lo, kp = L.xhat_a, L.xa_hi, L.xa_lo, L.kp

    def prep_turn(r):
        pe.wait_ge(ev.xha_done.sem, ev.xha_done.upto(r, 1))
        pe.wait_ge(ev.exp_done.sem, ev.exp_done.before(r, NH - 1))
        for k in range(KD):
            for j in range(NT):
                last = nc.tensor.transpose(L.ps_s[0][:, k, tile(j)], xhat_a[:, j, tile(k)], L.ident[:, :])
        last.then_inc(ev.xa_turned.sem, 1)

    def prep_kv(r):
        pe.wait_ge(ev.xahi_done.sem, ev.xahi_done.upto(r, 1))
        pe.wait_ge(ev.xalo_done.sem, ev.xalo_done.upto(r, 1))
        pe.wait_ge(ev.exp_done.sem, ev.exp_done.before(r, NH))
        for j in range(NT):
            last = three(L.ps_s[1][:, 0, tile(j)],
                         [(xa_hi[:, k, tile(j)], xa_lo[:, k, tile(j)], L.wkva_hi[:, k, :], L.wkva_lo[:, k, :])
                          for k in range(KD)])
        last.then_inc(ev.kv_full.sem, 1)

    def prep_k(r):
        pe.wait_ge(ev.kp_done.sem, ev.kp_done.upto(r, 1))
        for j in range(NT):
            last = nc.tensor.transpose(L.ps_s[0][:, 0, tile(j)], kp[:, j, :], L.ident[:, :])
        last.then_inc(ev.k_turned.sem, 1)

    return prep_turn, prep_kv, prep_k


def prepare_act(nc, L, act):
    ev, xa_hi, kT_hi = L.events, L.xa_hi, L.kT_hi
    copy = lambda out, src: nc.scalar.activation(out, src, ACT.Copy)

    def prep_x(r):
        act.wait_ge(ev.xa_turned.sem, ev.xa_turned.upto(r, 1))
        copy(xa_hi[:, :, :], L.ps_s[0][:, :, :]).then_inc(ev.xahi_done.sem, 1)

    def prep_k(r):
        act.wait_ge(ev.k_turned.sem, ev.k_turned.upto(r, 1))
        copy(kT_hi[:, :], L.ps_s[0][:, 0, :]).then_inc(ev.khi_done.sem, 1)

    return prep_x, prep_k


def chains(nc, L, dve):
    vec, bn, carrier = nc.vector, L.bn, L.carrier

    def minus_hi(lo, src, hi):
        return vec.tensor_tensor(lo, src, hi.bitcast(F32), ALU.subtract)

    class Steps:

        def __init__(self, events, i):
            self.events, self.i, self.n = events, i, 0

        def __call__(self, ins, carry=False):
            self.n += 1
            ins.then_inc(self.events.sem, 1)
            dve.wait_ge(self.events.sem, self.events.upto(self.i, self.n))
            if carry:
                vec.memset(carrier[:, :], 0.0)

        def end(self):
            assert self.n == self.events.per_round

    def moments(step, src, mean, var, done):
        for j in range(NT):
            last = vec.bn_stats(bn[:, j, :], src(j))
        step(last, carry=True)
        for j in range(NT):
            last = vec.bn_aggr(mean[:, j, :], bn[:, j, :])
        step(last)
        vec.tensor_scalar(var[:, :], mean[:, :, 1], EPS, None, ALU.add).then_inc(done.sem, 1)

    def normalise(out, src, mean, rstd, done):
        for j in range(NT):
            last = vec.tensor_scalar(out(j), src(j), mean[:, j, 0:1], rstd[:, j:j + 1], ALU.subtract, ALU.mult)
        last.then_inc(done.sem, 1)

    return Steps, moments, normalise, minus_hi


def prepare_dve(nc, L, dve):
    ev, vec = L.events, nc.vector
    Steps, moments, normalise, minus_hi = chains(nc, L, dve)
    xnext, xhat_a, xa_hi, xa_lo, kp, krot, kT_hi, kT_lo = L.xnext, L.xhat_a, L.xa_hi, L.xa_lo, L.kp, L.krot, L.kT_hi, L.kT_lo
    mean_a, var_a, rstd_a, mean_k, var_k, rstd_k = L.mean_a, L.var_a, L.rstd_a, L.mean_k, L.var_k, L.rstd_k

    def kv_tile(j):
        return L.ps_s[1][:, 0, j * P:j * P + RANK]

    def prep_moments(r):
        step = Steps(ev.prep_x_step, r)
        dve.wait_ge(ev.xnext_loaded.sem, ev.xnext_loaded.upto(r, 16))
        moments(step, lambda j: xnext[:, j, :], mean_a, var_a, ev.vara_done)
        step.end()

    def prep_normal(r):
        dve.wait_ge(ev.vara_done.sem, ev.vara_done.upto(r, 1))
        dve.wait_ge(ev.rsa_done.sem, ev.rsa_done.upto(r, 1))
        normalise(lambda j: xhat_a[:, j, :], lambda j: xnext[:, j, :], mean_a, rstd_a, ev.xha_done)

    def prep_x(r):
        dve.wait_ge(ev.xahi_done.sem, ev.xahi_done.upto(r, 1))
        minus_hi(xa_lo[:, :, :], L.ps_s[0][:, :, :], xa_hi[:, :, :]).then_inc(ev.xalo_done.sem, 1)

    def prep_kv(r):
        step = Steps(ev.prep_k_step, r)
        dve.wait_ge(ev.kv_full.sem, ev.kv_full.upto(r, 1))
        moments(step, kv_tile, mean_k, var_k, ev.vark_done)
        step.end()
        rot = L.ps_s[1][:, 0, :].rearrange("p (j n) -> p j n", j=NT)
        evens, odds = rot[:, :, RANK::2], rot[:, :, RANK + 1::2]
        for n, (x, trig) in enumerate(((evens, L.kcos), (odds, L.ksin), (evens, L.ksin), (odds, L.kcos))):
            last = vec.tensor_tensor(krot[:, n, :, :], x, trig[:, :, :], ALU.mult)
        last.then_inc(ev.kr_done.sem, 1)

    def prep_kn(r):
        dve.wait_ge(ev.vark_done.sem, ev.vark_done.upto(r, 1))
        dve.wait_ge(ev.rsk_done.sem, ev.rsk_done.upto(r, 1))
        normalise(lambda j: kp[:, j, 0:RANK], kv_tile, mean_k, rstd_k, ev.kn_done)

    def prep_k(r):
        dve.wait_ge(ev.khi_done.sem, ev.khi_done.upto(r, 1))
        minus_hi(kT_lo[:, :], L.ps_s[0][:, 0, :], kT_hi[:, :]).then_inc(ev.klo_done.sem, 1)

    return prep_moments, prep_normal, prep_x, prep_kv, prep_kn, prep_k


def rounding(nc, L):
    gp, one = nc.gpsimd, L.one

    def hi_of(hi, src):
        ones = one[0:src.shape[0], 0:1]
        while ones.ndim < src.ndim:
            ones = ones.unsqueeze(1)
        return gp.tensor_tensor(hi, src, ones.to_broadcast(list(src.shape)), ALU.mult)

    return hi_of


def prepare_pool(nc, L, pool):
    ev, gp, hi_of = L.events, nc.gpsimd, rounding(nc, L)
    kp, krot, kv_hi, kv_lo = L.kp, L.krot, L.kv_hi, L.kv_lo

    def power(var, rstd, ready, done, r):
        pool.wait_ge(ready.sem, ready.upto(r, 1))
        gp.tensor_tensor(rstd[:, :], var[:, :], L.minus_half[:, :], ALU.pow).then_inc(done.sem, 1)

    def prep_kp(r):
        pool.wait_ge(ev.kr_done.sem, ev.kr_done.upto(r, 1))
        gp.tensor_tensor(kp[:, :, RANK:RANK + HR], krot[:, 0, :, :], krot[:, 1, :, :], ALU.subtract)
        gp.tensor_tensor(kp[:, :, RANK + HR:P], krot[:, 2, :, :], krot[:, 3, :, :], ALU.add)
        pool.wait_ge(ev.kn_done.sem, ev.kn_done.upto(r, 1))
        lat = kp[:, :, 0:RANK]
        wide = lambda t: t[:, :].unsqueeze(1).to_broadcast([P, NT, RANK])
        gp.tensor_tensor(lat, lat, wide(L.gamma), ALU.mult).then_inc(ev.kp_part.sem, 1)
        pool.wait_ge(ev.kp_part.sem, ev.kp_part.upto(r, 1))
        gp.tensor_tensor(lat, lat, wide(L.beta), ALU.add).then_inc(ev.kp_done.sem, 1)

    def prep_latents_hi(r):
        pool.wait_ge(ev.kp_done.sem, ev.kp_done.upto(r, 1))
        pool.wait_ge(ev.pv_done.sem, ev.pv_done.before(r, NH))
        hi_of(kv_hi[:, :, 1, :], kp[:, :, 0:RANK]).then_inc(ev.kvhi_done.sem, 1)

    def prep_latents_lo(r):
        pool.wait_ge(ev.kvhi_done.sem, ev.kvhi_done.upto(r, 1))
        gp.tensor_tensor(kv_lo[:, :, 1, :], kp[:, :, 0:RANK], kv_hi[:, :, 1, :].bitcast(F32),
                         ALU.subtract).then_inc(ev.kvlo_done.sem, 1)

    return power, prep_kp, prep_latents_hi, prep_latents_lo


def expert_parts(L, d):
    down_rows = d["w_down"].rearrange("e h n -> (e h) n").rearrange("(c p) n -> p c n", p=P)

    def part(which, src, *at, form=lambda t: t):
        hi, lo, raw = (t[at] for t in which)
        return [(form(raw), src)], [(hi, lo, raw)]

    def shared(src, n):
        return part((L.sgu_hi, L.sgu_lo, L.sgu_raw), src.rearrange("(k p) h -> p k h", p=P),
                    slice(0, P), slice(n * KD, (n + 1) * KD), slice(0, HS))

    def expert(src, which, k, e):
        return part(which, src[e:e + HALF, k * P:(k + 1) * P, :].rearrange("e p h -> p e h"),
                    slice(0, P), k, slice(e * H, (e + HALF) * H), form=lambda t: t.rearrange("p (e h) -> p e h", e=HALF))

    def down(at, to):
        return part((L.md_hi, L.md_lo, L.md_raw), down_rows[:, at:to, :], slice(0, P), slice(at, to), slice(0, D))

    def shared_down(rows, at, to):
        return part((L.sd_hi, L.sd_lo, L.sd_raw), d["sw_down"][at * P:at * P + (to - at - 1) * P + rows, :].rearrange("(c p) n -> p c n", p=rows),
                    slice(0, rows), slice(at, to), slice(0, D))

    loads, splits = shared_down(P, 0, ES - 1)
    short = shared_down(HS - (ES - 1) * P, ES - 1, ES)
    loads, splits = loads + short[0], splits + short[1]
    parts = [shared(d["sw_gate"], 0), shared(d["sw_up"], 1), (loads, splits)]
    downs = [down(at, min(at + DOWN, ER)) for at in range(0, ER, DOWN)]
    for n, e in enumerate((0, HALF)):
        parts += [expert(src, which, k, e) for src, which in ((d["w_gate"], (L.mg_hi, L.mg_lo, L.mg_raw)), (d["w_up"], (L.mu_hi, L.mu_lo, L.mu_raw)))
                  for k in range(KD)]
        parts += downs[2 * n:2 * n + 2]
    return parts


SHARED_PARTS = 3


def splits_upto(L, n):
    return sum(len(splits) for _, splits in L.parts[0:n + 1])


def part_hi(nc, L, act):
    def split_hi(n):
        loads, splits = L.parts[n]
        act.wait_ge(L.events.part_in[n], 16 * len(loads))
        for hi, _, raw in splits:
            nc.scalar.activation(hi, raw, ACT.Copy).then_inc(L.events.part_hi, 1)
    return split_hi


def part_lo(nc, L, dve):
    def split_lo(n):
        dve.wait_ge(L.events.part_hi, splits_upto(L, n))
        for hi, lo, raw in L.parts[n][1]:
            nc.vector.tensor_tensor(lo, raw, hi.bitcast(F32), ALU.subtract).then_inc(L.events.part_lo, 1)
    return split_lo


def weights(nc, L, d):
    with ExitStack() as ctx:
        def sb(name, shape, dt=F32):
            return ctx.enter_context(nc.sbuf_tensor(name, shape, dt))

        def sem(name):
            return ctx.enter_context(nc.semaphore(name))

        wq_raw = [sb(f"wq_raw{n}", [P, KD, GROUP, DQK]) for n in range(RING)]
        wkvb_raw = [sb(f"wkvb_raw{n}", [RANK, GROUP, DN + DV]) for n in range(RING)]
        wout_raw = [sb(f"wout_raw{n}", [P, GROUP, D]) for n in range(RING)]
        small_raw = sb("small_raw", [P, KD, RANK + DR + E])
        sel_f = sb("sel_f", [CK, HALF * H])
        turned = [sb(f"turned{n}", [P, TW]) for n in range(2)]
        theta = sb("theta", [P, NT, 4, HR])
        turns = sb("turns", [P, NT, 4, HR])
        angle = sb("angle", [P, NT, 4, HR])
        cos4, sin4 = (L.xhat_a[:, n, :].rearrange("p (j r f) -> p j r f", j=NT, r=4) for n in range(2))

        theta_in, small_in = map(sem, ("theta_in", "small_in"))
        heads_in = [sem(f"heads_in{g}") for g in range(NH // GROUP)]
        ident_step, sel_step, rope_hi, rope_lo = map(sem, ("ident_step", "sel_step", "rope_hi", "rope_lo"))
        sel_rounded = sem("sel_rounded")
        w_turned, w_evac, w_full, whi_done, wlo_done = map(sem, ("w_turned", "w_evac", "w_full", "whi_done", "wlo_done"))
        angle_step, angle_done, cos_angle, sin_done, cos_done, trig_turned, small_hi = map(
            sem, ("angle_step", "angle_done", "cos_angle", "sin_done", "cos_done", "trig_turned", "small_hi"))

        ROPE_STEPS = KD
        HEAD_LOADS = 16 * (KD + 2)

        made = L.ps_o, L.ps_y

        def rope_of(g, k):
            heads = slice(g * GROUP, (g + 1) * GROUP)
            parts = (t[:, k, heads, RANK:P].rearrange("p h (o r) -> p h o r", o=2) for t in (L.wq_hi, L.wq_lo))
            return *parts, wq_raw[g % RING][:, k, :, DN:DQK].rearrange("p h (r o) -> p h o r", o=2)

        with nc.Block() as block:
            @block.sync
            def _(sp):
                ev = L.events
                for events in (ev.su_done, ev.cb_done, ev.ulo_done, ev.qcos_done, ev.exp_done, ev.pv_done, ev.olo_done, ev.osb_done,
                               ev.out_stored):
                    sp.sem_inc(events.sem, events.head)
                for r in range(4):
                    sp.dma_start(theta[:, :, r, :], d["freqs"].rearrange("(j p) f -> p j f", p=P)).then_inc(theta_in, 16)
                sp.dma_start(L.xnext[:, :, :], d["x"][0, :, :].rearrange("(j p) m -> p j m", p=P)).then_inc(ev.xnext_loaded.sem, 16)
                by_head = "(k p) (h n) -> p k h n"

                def load_heads(g):
                    heads = slice(g * GROUP, (g + 1) * GROUP)
                    if g >= RING:
                        sp.wait_ge(w_full, GROUP * (g - RING + 1))
                        sp.wait_ge(rope_lo, ROPE_STEPS * (g - RING + 1))
                    sp.dma_start(wkvb_raw[g % RING][:, :, :], d["Wkv_b"].rearrange("c (h n) -> c h n", h=NH)[:, heads, :]).then_inc(heads_in[g], 16)
                    for k in range(KD):
                        sp.dma_start(wq_raw[g % RING][:, k, :, :],
                                     d["Wq"].rearrange(by_head, p=P, h=NH)[:, k, heads, :]).then_inc(heads_in[g], 16)
                    sp.dma_start(wout_raw[g % RING][:, :, :], d["Wout"].rearrange("(h n) m -> n h m", n=DV)[:, heads, :]).then_inc(heads_in[g], 16)

                for g in range(NH // GROUP):
                    load_heads(g)
                for n, (loads, _) in enumerate(L.parts):
                    for to, src in loads:
                        sp.dma_start(to, src).then_inc(L.events.part_in[n], 16)

            @block.scalar
            def _(act):
                act.dma_start(small_raw[:, :, 0:RANK + DR], d["Wkv_a"].rearrange("(k p) n -> p k n", p=P)).then_inc(small_in, 16)
                act.dma_start(small_raw[:, :, RANK + DR:], d["gate_w"].rearrange("(k p) n -> p k n", p=P)).then_inc(small_in, 16)
                act.dma_start(L.gamma[:, :], d["gamma"].partition_broadcast(P)).then_inc(small_in, 16)
                act.dma_start(L.beta[:, :], d["beta"].partition_broadcast(P)).then_inc(small_in, 16)
                act.wait_ge(angle_done, 1)
                nc.scalar.activation(sin4[:, :, :, :], angle[:, :, :, :], ACT.Sin).then_inc(sin_done, 1)
                act.wait_ge(cos_angle, 1)
                nc.scalar.activation(cos4[:, :, :, :], turns[:, :, :, :], ACT.Sin).then_inc(cos_done, 1)
                act.wait_ge(small_in, 64)
                nc.scalar.activation(L.wkva_hi[:, :, :], small_raw[:, :, 0:RANK + DR], ACT.Copy).then_inc(small_hi, 1)
                nc.scalar.activation(L.gw_hi[:, :, :], small_raw[:, :, RANK + DR:], ACT.Copy).then_inc(small_hi, 1)

                prep_x, prep_k = prepare_act(nc, L, act)

                def evacuate(h):
                    act.wait_ge(w_turned, h + 1)
                    if h >= 2:
                        act.wait_ge(w_full, h - 1)
                    nc.scalar.activation(turned[h % 2][:, :], flat2(L.ps_t[h % 2])[:, 0:TW], ACT.Copy).then_inc(w_evac, 1)

                evacuate(0)
                for h in range(NH):
                    if h + 1 < NH:
                        evacuate(h + 1)
                    act.wait_ge(w_full, h + 1)
                    prod = flat2(made[h % 2])
                    rows = slice(RANK * (h % 2), RANK * (h % 2) + RANK)
                    nc.scalar.activation(L.wq_hi[:, :, h, 0:RANK], prod[:, 0:KD * RANK].rearrange("p (k c) -> p k c", k=KD), ACT.Copy)
                    nc.scalar.activation(L.wo_hi[rows, h // 2, :], prod[rows, KD * RANK:KD * RANK + D], ACT.Copy).then_inc(whi_done, 1)
                    if h == 4:
                        prep_x(0)
                    if h == 14:
                        prep_k(0)

            @block.tensor
            def _(pe):
                pe.wait_ge(ident_step, 2)
                for n in range(40):
                    nc.tensor.transpose(L.ps_t[0][:, 0, 0:P], L.ident[:, :], L.ident[:, :])
                pe.wait_ge(sin_done, 1)
                pe.wait_ge(cos_done, 1)
                for n, trig in enumerate((cos4, sin4)):
                    for j in range(NT):
                        last = nc.tensor.transpose(L.ps_q[n][:, 0, j * P:(j + 1) * P],
                                                   trig[:, j, :, :].rearrange("p r f -> p (r f)"), L.ident[:, :])
                last.then_inc(trig_turned, 1)

                prep_turn, prep_kv, prep_k = prepare_pe(nc, L, pe)

                def turn(h):
                    if h % GROUP == 0:
                        pe.wait_ge(heads_in[h // GROUP], HEAD_LOADS)
                    if h >= 2:
                        pe.wait_ge(w_evac, h - 1)
                    to = flat2(L.ps_t[h % 2])
                    for k in range(KD):
                        nc.tensor.transpose(to[:, k * P:(k + 1) * P], wq_raw[h // GROUP % RING][:, k, h % GROUP, 0:DN], L.ident[:, :])
                    at = KD * P
                    for part in (0, DN, DN):
                        last = nc.tensor.transpose(to[:, at:at + RANK], wkvb_raw[h // GROUP % RING][:, h % GROUP, part:part + DN], L.ident[0:RANK, 0:RANK])
                        at += RANK
                    last.then_inc(w_turned, 1)

                turn(0)
                for h in range(NH):
                    if h + 1 < NH:
                        turn(h + 1)
                    pe.wait_ge(w_evac, h + 1)
                    if h >= 2:
                        pe.wait_ge(wlo_done, h - 1)
                    to, t = flat2(made[h % 2]), turned[h % 2]
                    for k in range(KD):
                        nc.tensor.matmul(to[:, k * RANK:(k + 1) * RANK], t[:, k * P:(k + 1) * P],
                                         t[:, KD * P:KD * P + RANK], start=True, stop=True)
                    nc.tensor.matmul(to[:, KD * RANK:KD * RANK + D], t[:, KD * P + RANK:TW], wout_raw[h // GROUP % RING][:, h % GROUP, :],
                                     start=True, stop=True).then_inc(w_full, 1)
                    if h == 3:
                        prep_turn(0)
                    if h == 6:
                        prep_kv(0)
                    if h == 13:
                        prep_k(0)

            @block.vector
            def _(dve):
                nc.vector.memset(L.minus_half[:, :], -0.5)
                for n in range(E):
                    nc.vector.memset(L.sentinel[:, n:n + 1], -1.0 - n)
                nc.vector.memset(L.qcos[0:RANK, :], SCALE)
                nc.vector.memset(L.qsin[0:RANK, :], 0.0)
                steps = 0

                def step(ins):
                    nonlocal steps
                    steps += 1
                    ins.then_inc(angle_step, 1)
                    dve.wait_ge(angle_step, steps)

                two_pi, first, second = 6.283185307179586, 6.28125, 1.93500518798828125e-3
                to_round = 12582912.0
                th, tu, an = (t[:, :, :, :].rearrange("p j r f -> p (j r f)") for t in (theta, turns, angle))
                dve.wait_ge(theta_in, 64)
                step(nc.vector.tensor_scalar(tu, th, 1.0 / two_pi, to_round, ALU.mult, ALU.add))
                step(nc.vector.tensor_scalar(tu, tu, -to_round, None, ALU.add))
                step(nc.vector.scalar_tensor_tensor(an, tu, -first, th, ALU.mult, ALU.add))
                step(nc.vector.scalar_tensor_tensor(an, tu, -second, an, ALU.mult, ALU.add))
                step(nc.vector.scalar_tensor_tensor(an, tu, -(two_pi - first - second), an, ALU.mult, ALU.add))
                nc.vector.tensor_scalar(an, an, 3.1415925, -3.1415925, ALU.min, ALU.max).then_inc(angle_done, 1)
                dve.wait_ge(angle_done, 1)
                step(nc.vector.scalar_tensor_tensor(tu, an, -1.0, an, ALU.mult, ALU.min))
                nc.vector.tensor_scalar(tu, tu, two_pi / 4, None, ALU.add).then_inc(cos_angle, 1)
                dve.wait_ge(trig_turned, 1)
                even, odd = slice(RANK, RANK + HR), slice(RANK + HR, RANK + DR)
                nc.vector.tensor_scalar(L.qcos[RANK:P, :], L.ps_q[0][RANK:P, 0, :], SCALE, None, ALU.mult)
                nc.vector.tensor_scalar(L.qsin[even, :], L.ps_q[1][even, 0, :], -SCALE, None, ALU.mult)
                nc.vector.tensor_scalar(L.qsin[odd, :], L.ps_q[1][odd, 0, :], SCALE, None, ALU.mult)
                dve.wait_ge(sin_done, 1)
                dve.wait_ge(cos_done, 1)
                nc.vector.tensor_copy(L.kcos[:, :, :], cos4[:, :, 0, :])
                nc.vector.tensor_copy(L.ksin[:, :, :], sin4[:, :, 0, :])
                dve.wait_ge(small_hi, 2)
                nc.vector.tensor_tensor(L.wkva_lo[:, :, :], small_raw[:, :, 0:RANK + DR], L.wkva_hi[:, :, :].bitcast(F32), ALU.subtract)
                nc.vector.tensor_tensor(L.gw_lo[:, :, :], small_raw[:, :, RANK + DR:], L.gw_hi[:, :, :].bitcast(F32), ALU.subtract)
                nc.vector.memset(L.kp[:, :, :], 0.0).then_inc(L.events.zeros_set, 1)
                dve.wait_ge(L.events.zeros_set, 1)
                zeros = L.kp[:, :, :].rearrange("p j (n c) -> p j n c", c=RANK)
                nc.vector.tensor_copy(L.kv_hi[:, :, 0:3:2, :], zeros)
                nc.vector.tensor_copy(L.kv_lo[:, :, 0:3:2, :], zeros).then_inc(L.events.zeros_set, 1)
                prep_moments, prep_normal, prep_x, prep_kv, prep_kn, prep_k = prepare_dve(nc, L, dve)

                def round_sel(half):
                    dve.wait_ge(sel_step, 7 * half + 7)
                    nc.vector.tensor_copy(L.sel[:, half * HALF * H:(half + 1) * HALF * H], sel_f[:, :]).then_inc(sel_rounded, 1)

                prep_moments(0)
                round_sel(0)
                for h in range(NH):
                    if h == 2:
                        prep_normal(0)
                    if h == 5:
                        prep_x(0)
                    if h == 8:
                        prep_kv(0)
                    if h == 9:
                        dve.wait_ge(L.events.zeros_set, 2)
                        prep_kn(0)
                    if h == 15:
                        prep_k(0)
                    if h == 6:
                        round_sel(1)
                    dve.wait_ge(whi_done, h + 1)
                    prod = flat2(made[h % 2])
                    rows = slice(RANK * (h % 2), RANK * (h % 2) + RANK)
                    nc.vector.tensor_tensor(L.wq_lo[:, :, h, 0:RANK], prod[:, 0:KD * RANK].rearrange("p (k c) -> p k c", k=KD),
                                            L.wq_hi[:, :, h, 0:RANK].bitcast(F32), ALU.subtract)
                    nc.vector.tensor_tensor(L.wo_lo[rows, h // 2, :], prod[rows, KD * RANK:KD * RANK + D],
                                            L.wo_hi[rows, h // 2, :].bitcast(F32), ALU.subtract).then_inc(wlo_done, 1)
                    if h % GROUP == GROUP - 1:
                        g = h // GROUP
                        dve.wait_ge(rope_hi, ROPE_STEPS * (g + 1))
                        for k in range(KD):
                            hi, lo, src = rope_of(g, k)
                            nc.vector.tensor_tensor(lo, src, hi.bitcast(F32), ALU.subtract).then_inc(rope_lo, 1)

            @block.gpsimd
            def _(pool):
                nc.gpsimd.memset(L.ident[:, :], 0.0).then_inc(ident_step, 1)
                pool.wait_ge(ident_step, 1)
                nc.gpsimd.affine_select(out=L.ident[:, :], in_=L.ident[:, :], compare_op=ALU.not_equal, fill=1.0, base=0,
                                        pattern=[[-1, P]], channel_multiplier=1).then_inc(ident_step, 1)
                def make_sel(half):
                    at, steps = half * HALF * H, 7 * half
                    rows_of = [sel_f[row:row + E, :] for row in (0, LO)]
                    if half:
                        pool.wait_ge(sel_rounded, 1)
                    nc.gpsimd.memset(sel_f[:, :], 0.0).then_inc(sel_step, 1)
                    pool.wait_ge(sel_step, steps + 1)
                    for part in rows_of:
                        nc.gpsimd.memset(part, 1.0).then_inc(sel_step, 1)
                    pool.wait_ge(sel_step, steps + 3)
                    for part in rows_of:
                        nc.gpsimd.affine_select(out=part, in_=part, compare_op=ALU.is_ge, fill=0.0, base=at,
                                                pattern=[[1, HALF * H]], channel_multiplier=-H).then_inc(sel_step, 1)
                    pool.wait_ge(sel_step, steps + 5)
                    for part in rows_of:
                        nc.gpsimd.affine_select(out=part, in_=part, compare_op=ALU.is_ge, fill=0.0, base=H - 1 - at,
                                                pattern=[[-1, HALF * H]], channel_multiplier=H).then_inc(sel_step, 1)
                    pool.wait_ge(sel_step, steps + 7)

                make_sel(0)
                ev = L.events
                power, prep_kp, prep_latents_hi, prep_latents_lo = prepare_pool(nc, L, pool)
                nc.gpsimd.memset(L.one[:, :], 1.0).then_inc(ev.ones_set, 1)
                pool.wait_ge(ev.ones_set, 1)
                pool.wait_ge(ev.zeros_set, 2)
                power(L.var_a, L.rstd_a, ev.vara_done, ev.rsa_done, 0)
                for g, loaded in enumerate(heads_in):
                    pool.wait_ge(loaded, HEAD_LOADS)
                    for k in range(KD):
                        hi, _, src = rope_of(g, k)
                        nc.gpsimd.tensor_copy(hi, src).then_inc(rope_hi, 1)
                    if (g + 1) * GROUP == 4:
                        make_sel(1)
                    if (g + 1) * GROUP == 8:
                        power(L.var_k, L.rstd_k, ev.vark_done, ev.rsk_done, 0)
                    if (g + 1) * GROUP == 12:
                        pool.wait_ge(small_in, 64)
                        prep_kp(0)
                        prep_latents_hi(0)
                        prep_latents_lo(0)


def loop(nc, L, d):
    ev = L.events
    with ExitStack() as ctx:
        def sb(name, shape, dt=F32):
            return ctx.enter_context(nc.sbuf_tensor(name, shape, dt))

        xin = sb("xin", [P, NT, D])
        xhat_f = sb("xhat_f", [P, NT, D])
        x2 = sb("x2", [P, NT, D])
        xf_hi, xf_lo = (sb(f"xf_{x}", [P, KD, S], F32R) for x in ("hi", "lo"))
        xa_hi, xa_lo, kT_hi, kT_lo, kv_hi, kv_lo = L.xa_hi, L.xa_lo, L.kT_hi, L.kT_lo, L.kv_hi, L.kv_lo
        mean_f, var_f, rstd_f = sb("mean_f", [P, NT, 2]), sb("var_f", [P, NT]), sb("rstd_f", [P, NT])
        qswap = [sb(f"qswap{n}", [P, 2, S]) for n in range(2)]
        qf = [sb(f"qf{n}", [P, 2, S]) for n in range(2)]
        q_hi, q_lo = ([sb(f"q_{x}{n}", [P, 2, S], F32R) for n in range(2)] for x in ("hi", "lo"))
        nmax = sb("nmax", [P, NH, NT])
        rsum = sb("rsum", [P, NH, NT])
        rinv = sb("rinv", [P, NH, NT])
        probs = [sb(f"probs{n}", [P, NT, S]) for n in range(3)]
        pT_hi, pT_lo = ([sb(f"pT_{x}{n}", [P, NT, S], F32R) for n in range(3)] for x in ("hi", "lo"))
        o_hi, o_lo = ([sb(f"o_{x}{n}", [P, S], F32R) for n in range(2)] for x in ("hi", "lo"))
        lmax = sb("lmax", [P, NT])
        esum = sb("esum", [P, NT])
        einv = sb("einv", [P, NT])
        eprob = sb("eprob", [P, NT, E])
        score = sb("score", [P, NT, 2 * E])
        top = sb("top", [P, NT, E])
        rest = sb("rest", [P, NT, 2 * E])
        comb = sb("comb", [P, NT, E])
        comb2 = sb("comb2", [P, NT, P])
        cT = o_hi[0][0:CK, :]
        gate, prod, unit = ([probs[n][:, m, :] for m in range(NT)] for n in range(3))
        u_hi, u_lo = ([t[:, 0, :] for t in ring] for ring in (pT_hi, pT_lo))

        half = (slice(1, 3), slice(0, 2))
        even, odd = slice(RANK, RANK + HR), slice(RANK + HR, P)

        three = products(nc)
        parts_after_round = {5: 2, 6: 3, 7: 4, 8: 5}
        parts_after_chunk = {m: 6 + m for m in range(9)}

        def due(p):
            return 0 <= p < NP

        block = ctx.enter_context(nc.Block())

        @block.sync
        def _(sp):
            by_token = "(j p) m -> p j m"
            sp.dma_start(xin[:, :, :], d["x"][0, :, :].rearrange(by_token, p=P)).then_inc(ev.x_loaded.sem, 16)

            def store(i):
                sp.wait_ge(ev.osb_done.sem, ev.osb_done.upto(i, 1))
                sp.dma_start(d["out"][bass.ds(i, 1), :, :].rearrange("b (j p) m -> p (b j) m", p=P),
                             x2[:, :, :]).then_inc(ev.out_stored.sem, 16)

            with sp.Fori(0, B - 1) as i:
                following = d["x"][bass.ds(i + 1, 1), :, :].rearrange("b (j p) m -> p (b j) m", p=P)
                sp.wait_ge(ev.xha_done.sem, ev.xha_done.upto(i, 1))
                sp.dma_start(L.xnext[:, :, :], following).then_inc(ev.xnext_loaded.sem, 16)
                sp.wait_ge(ev.x2_done.sem, ev.x2_done.upto(i, 1))
                sp.dma_start(xin[:, :, :], following).then_inc(ev.x_loaded.sem, 16)
                store(i)
            store(B - 1)
            sp.wait_ge(ev.out_stored.sem, ev.out_stored.upto(B - 1, 16))

        @block.tensor
        def _(pe):
            prep_turn, prep_kv, prep_k = prepare_pe(nc, L, pe)
            gate_up_part = {0: 1, ES: SHARED_PARTS + 2 * KD - 1, ES + HALF * H // P: SHARED_PARTS + 4 * KD + 1}
            down_part = {0: SHARED_PARTS - 1, ES: SHARED_PARTS + 2 * KD, ES + DOWN: SHARED_PARTS + 2 * KD + 1,
                         ES + 2 * DOWN: SHARED_PARTS + 4 * KD + 2, ES + 3 * DOWN: SHARED_PARTS + 4 * KD + 3}

            def keep_busy(n):
                for _ in range(n):
                    nc.tensor.matmul(L.ps_o[:, 0, :], xa_hi[:, 0, 0:P], xa_hi[:, 0, :], start=True, stop=True)

            def query(i, p):
                if p == 0:
                    pe.wait_ge(ev.xalo_done.sem, ev.xalo_done.upto(i, 1))
                if p < 2:
                    pe.wait_ge(ev.qcos_done.sem, ev.qcos_done.before(i, NP - 1 + p))
                else:
                    pe.wait_ge(ev.qcos_done.sem, ev.qcos_done.upto(i, p - 1))
                    if p < 4:
                        pe.wait_ge(ev.su_done.sem, ev.su_done.before(i, CH - 3 + p))
                for n in range(2):
                    h = 2 * p + n
                    last = three(L.ps_q[p % 2][:, n, :],
                                 [(L.wq_hi[:, k, h, :], L.wq_lo[:, k, h, :], xa_hi[:, k, :], xa_lo[:, k, :]) for k in range(KD)])
                last.then_inc(ev.q_full.sem, 1)

            def scores(i, h):
                p, n = divmod(h, 2)
                pe.wait_ge(ev.qlo_done.sem, ev.qlo_done.upto(i, p + 1))
                if h == 0:
                    pe.wait_ge(ev.klo_done.sem, ev.klo_done.upto(i, 1))
                elif h == 1:
                    pe.wait_ge(ev.kn_done.sem, ev.kn_done.upto(i, 1))
                else:
                    pe.wait_ge(ev.exp_done.sem, ev.exp_done.upto(i, h - 1))
                for j in range(NT):
                    last = three(L.ps_s[h % 2][:, j, :],
                                 [(q_hi[p % 2][:, n, tile(j)], q_lo[p % 2][:, n, tile(j)], kT_hi[:, :], kT_lo[:, :])])
                last.then_inc(ev.s_full.sem, 1)

            def turn(i, h):
                pe.wait_ge(ev.pn_done.sem, ev.pn_done.upto(i, h + 1))
                if h < 2:
                    pe.wait_ge(ev.cb_done.sem, ev.cb_done.before(i, ER))
                else:
                    pe.wait_ge(ev.plo_done.sem, ev.plo_done.upto(i, h - 1))
                for c in range(NT):
                    for j in range(NT):
                        last = nc.tensor.transpose(L.ps_t[h % 2][:, c, tile(j)], probs[h % 3][:, j, tile(c)], L.ident[:, :])
                last.then_inc(ev.t_full.sem, 1)

            def attend(i, h):
                p, n = divmod(h, 2)
                pe.wait_ge(ev.plo_done.sem, ev.plo_done.upto(i, h + 1))
                if n == 0:
                    pe.wait_ge(ev.olo_done.sem, ev.olo_done.upto(i, p))
                if h == 0:
                    pe.wait_ge(ev.kvlo_done.sem, ev.kvlo_done.upto(i, 1))
                both = "p n c -> p (n c)"
                last = three(L.ps_o[:, 0, :],
                             [(kv_hi[:, c, half[n], :].rearrange(both), kv_lo[:, c, half[n], :].rearrange(both),
                               pT_hi[h % 3][:, c, :], pT_lo[h % 3][:, c, :]) for c in range(NT)], start=n == 0, stop=n == 1, skip=True)
                last.then_inc(ev.pv_done.sem, 1)

            def project(i, p):
                pe.wait_ge(ev.olo_done.sem, ev.olo_done.upto(i, p + 1))
                if p == 0:
                    pe.wait_ge(ev.osb_done.sem, ev.osb_done.before(i, 1))
                for j in range(NT):
                    last = three(L.ps_y[:, j, :], [(o_hi[p % 2][:, tile(j)], o_lo[p % 2][:, tile(j)], L.wo_hi[:, p, :], L.wo_lo[:, p, :])],
                                 start=p == 0 and j == 0, stop=p == NP - 1, skip=True)
                last.then_inc(ev.out_done.sem, 1)

            def attention(i, prep):
                for r in range(NP + 3):
                    if due(r + 4):
                        query(i, r + 4)
                    if due(r - 1):
                        turn(i, 2 * (r - 1) + 1)
                    if due(r + 1):
                        scores(i, 2 * (r + 1))
                    if due(r - 3):
                        project(i, r - 3)
                    if due(r + 1):
                        scores(i, 2 * (r + 1) + 1)
                    if prep and r == NP:
                        prep_turn(i + 1)
                    if due(r - 1):
                        attend(i, 2 * (r - 1))
                    if due(r):
                        turn(i, 2 * r)
                    if due(r - 1):
                        attend(i, 2 * (r - 1) + 1)

            def gate_up(i, m, prep, first):
                if m < 2 and prep:
                    pe.wait_ge(ev.qcos_done.sem, ev.qcos_done.upto(i + 1, m + 1))
                elif m < 2:
                    pe.wait_ge(ev.qcos_done.sem, ev.qcos_done.upto(i, NP - 1 + m))
                else:
                    pe.wait_ge(ev.su_done.sem, ev.su_done.upto(i, m - 1))
                if first and m in gate_up_part:
                    pe.wait_ge(ev.part_lo, splits_upto(L, gate_up_part[m]))
                rows = chunk_rows(m)
                for n in range(2):
                    if m < ES:
                        cols = slice(m * P, m * P + rows)
                        w = [(L.sgu_hi[:, n * KD + k, cols], L.sgu_lo[:, n * KD + k, cols]) for k in range(KD)]
                    else:
                        hi, lo = ((L.mg_hi, L.mg_lo), (L.mu_hi, L.mu_lo))[n]
                        w = [(hi[:, k, tile(m - ES)], lo[:, k, tile(m - ES)]) for k in range(KD)]
                    last = three(L.ps_q[m % 2][0:rows, n, :],
                                 [(*w[k], xf_hi[:, k, :], xf_lo[:, k, :]) for k in range(KD)])
                last.then_inc(ev.gu_full.sem, 1)

            def spread(i, m):
                c = m - ES
                if c == 0:
                    pe.wait_ge(ev.combhi_done.sem, ev.combhi_done.upto(i, 1))
                if c >= 2:
                    pe.wait_ge(ev.cb_done.sem, ev.cb_done.upto(i, c - 1))
                nc.tensor.matmul(L.ps_t[c % 2][:, 0, :], L.sel[:, tile(c)], cT, start=True, stop=True
                                 ).then_inc(ev.cb_full.sem, 1)

            def down(i, m, first):
                pe.wait_ge(ev.ulo_done.sem, ev.ulo_done.upto(i, m + 1))
                if m == 0:
                    pe.wait_ge(ev.x2_done.sem, ev.x2_done.upto(i, 1))
                if first and m in down_part:
                    pe.wait_ge(ev.part_lo, splits_upto(L, down_part[m]))
                rows = chunk_rows(m)
                hi, lo, c = (L.sd_hi, L.sd_lo, m) if m < ES else (L.md_hi, L.md_lo, m - ES)
                for j in range(NT):
                    last = three(L.ps_y[:, j, :], [(u_hi[m % 3][0:rows, tile(j)], u_lo[m % 3][0:rows, tile(j)],
                                                    hi[0:rows, c, :], lo[0:rows, c, :])],
                                 start=m == 0 and j == 0, stop=m == CH - 1, skip=True)
                last.then_inc(ev.down_done.sem, 1)

            def experts(i, prep, first=False):
                if prep:
                    query(i + 1, 0)
                    query(i + 1, 1)
                keep_busy(10 if prep else 36)
                pe.wait_ge(ev.xhf_done.sem, ev.xhf_done.upto(i, 1))
                pe.wait_ge(ev.plo_done.sem, ev.plo_done.upto(i, NH))
                for k in range(KD):
                    for j in range(NT):
                        last = nc.tensor.transpose(L.ps_t[0][:, k, tile(j)], xhat_f[:, j, tile(k)], L.ident[:, :])
                last.then_inc(ev.xf_turned.sem, 1)
                if prep:
                    prep_kv(i + 1)
                if not prep:
                    keep_busy(6)
                pe.wait_ge(ev.xfhi_done.sem, ev.xfhi_done.upto(i, 1))
                for part in range(2):
                    if part == 1:
                        pe.wait_ge(ev.xflo_done.sem, ev.xflo_done.upto(i, 1))
                    for j in range(NT):
                        for k in range(KD):
                            for x, w in (((xf_hi, L.gw_hi), (xf_hi, L.gw_lo)), ((xf_lo, L.gw_hi),))[part]:
                                last = nc.tensor.matmul(L.ps_t[1][:, 0, j * E:(j + 1) * E], x[:, k, tile(j)], w[:, k, :],
                                                        start=part == 0 and j == 0 and k == 0 and w is L.gw_hi,
                                                        stop=part == 1 and k == KD - 1, skip_group_check=True)
                last.then_inc(ev.logits_full.sem, 1)
                for m in range(CH):
                    gate_up(i, m, prep, first)
                    if m == ES:
                        pe.wait_ge(ev.comb_done.sem, ev.comb_done.upto(i, 1))
                        for j in range(NT):
                            last = nc.tensor.transpose(L.ps_o[:, 0, tile(j)], comb2[:, j, :], L.ident[:, :])
                        last.then_inc(ev.comb_turned.sem, 1)
                        down(i, 0, first)
                    if m >= ES:
                        spread(i, m)
                        down(i, m - 2, first)
                    if prep and m == ES + 2:
                        prep_k(i + 1)
                if prep:
                    query(i + 1, 2)
                down(i, CH - 2, first)
                if prep:
                    query(i + 1, 3)
                    scores(i + 1, 0)
                    scores(i + 1, 1)
                down(i, CH - 1, first)

            query(0, 0)
            query(0, 1)
            query(0, 2)
            query(0, 3)
            scores(0, 0)
            scores(0, 1)
            attention(0, True)
            experts(0, True, first=True)
            with pe.Fori(1, B - 1) as i:
                attention(i, True)
                experts(i, True)
            attention(B - 1, False)
            experts(B - 1, False)

        @block.scalar
        def _(act):
            copy = lambda out, src: nc.scalar.activation(out, src, ACT.Copy)
            prep_x, prep_k = prepare_act(nc, L, act)
            split_hi = part_hi(nc, L, act)

            def swap(i, p):
                act.wait_ge(ev.q_full.sem, ev.q_full.upto(i, p + 1))
                if p >= 2:
                    act.wait_ge(ev.qrot_done.sem, ev.qrot_done.upto(i, p - 1))
                copy(qswap[p % 2][even, :, :], L.ps_q[p % 2][odd, :, :])
                copy(qswap[p % 2][odd, :, :], L.ps_q[p % 2][even, :, :]).then_inc(ev.swap_done.sem, 1)

            def query_hi(i, p):
                act.wait_ge(ev.qrot_done.sem, ev.qrot_done.upto(i, p + 1))
                if p >= 2:
                    act.wait_ge(ev.s_full.sem, ev.s_full.upto(i, 2 * p - 2))
                copy(q_hi[p % 2][:, :, :], qf[p % 2][:, :, :]).then_inc(ev.qhi_done.sem, 1)

            def exps(i, h):
                act.wait_ge(ev.max_done.sem, ev.max_done.upto(i, h + 1))
                if h >= 3:
                    act.wait_ge(ev.t_full.sem, ev.t_full.upto(i, h - 2))
                else:
                    used, n = ((ev.su_done, CH), (ev.cb_done, ER), (ev.ulo_done, CH))[h]
                    act.wait_ge(used.sem, used.before(i, n))
                for j in range(NT):
                    last = nc.scalar.activation(probs[h % 3][:, j, :], L.ps_s[h % 2][:, j, :], ACT.Exp,
                                                bias=nmax[:, h, j:j + 1], accum_out=rsum[:, h, j:j + 1])
                last.then_inc(ev.exp_done.sem, 1)

            def probs_hi(i, h):
                act.wait_ge(ev.t_full.sem, ev.t_full.upto(i, h + 1))
                if h >= 3:
                    act.wait_ge(ev.pv_done.sem, ev.pv_done.upto(i, h - 2))
                copy(pT_hi[h % 3][:, :, :], L.ps_t[h % 2][:, :, :]).then_inc(ev.phi_done.sem, 1)

            def attended_hi(i, p):
                act.wait_ge(ev.pv_done.sem, ev.pv_done.upto(i, 2 * p + 2))
                if p >= 2:
                    act.wait_ge(ev.out_done.sem, ev.out_done.upto(i, p - 1))
                copy(o_hi[p % 2][:, :], L.ps_o[:, 0, :]).then_inc(ev.ohi_done.sem, 1)

            def attention(i, prep, first=False):
                for r in range(NP + 1):
                    if due(r):
                        exps(i, 2 * r + 1)
                    if due(r - 1):
                        probs_hi(i, 2 * (r - 1) + 1)
                    if due(r + 2):
                        query_hi(i, r + 2)
                    if due(r + 4):
                        swap(i, r + 4)
                    if due(r + 1):
                        exps(i, 2 * (r + 1))
                    if due(r):
                        probs_hi(i, 2 * r)
                    if prep and r == NP:
                        prep_x(i + 1)
                    if due(r - 1):
                        attended_hi(i, r - 1)
                    if first and r in parts_after_round:
                        split_hi(parts_after_round[r])

            def experts(i, prep, first=False):
                if prep:
                    swap(i + 1, 0)
                    swap(i + 1, 1)
                act.wait_ge(ev.xf_turned.sem, ev.xf_turned.upto(i, 1))
                copy(xf_hi[:, :, :], L.ps_t[0][:, :, :]).then_inc(ev.xfhi_done.sem, 1)
                if prep:
                    query_hi(i + 1, 0)
                act.wait_ge(ev.lmax_done.sem, ev.lmax_done.upto(i, 1))
                for j in range(NT):
                    last = nc.scalar.activation(eprob[:, j, :], L.ps_t[1][:, 0, j * E:(j + 1) * E], ACT.Exp,
                                                bias=lmax[:, j:j + 1], accum_out=esum[:, j:j + 1])
                last.then_inc(ev.gate_exp_done.sem, 1)
                for m in range(CH):
                    act.wait_ge(ev.gu_full.sem, ev.gu_full.upto(i, m + 1))
                    if m >= 2:
                        act.wait_ge(ev.su_done.sem, ev.su_done.upto(i, m - 1))
                    rows = chunk_rows(m)
                    nc.scalar.activation(gate[m % 2][0:rows, :], L.ps_q[m % 2][0:rows, 0, :], ACT.Silu).then_inc(ev.silu_done.sem, 1)
                    if prep and m == 1:
                        query_hi(i + 1, 1)
                    if m == ES - 1:
                        act.wait_ge(ev.comb_turned.sem, ev.comb_turned.upto(i, 1))
                        copy(cT, L.ps_o[0:CK, 0, :]).then_inc(ev.combhi_done.sem, 1)
                    if prep and m == ES + 2:
                        prep_k(i + 1)
                    if first and m in parts_after_chunk:
                        split_hi(parts_after_chunk[m])
                if prep:
                    swap(i + 1, 2)
                    swap(i + 1, 3)
                    exps(i + 1, 0)

            nc.scalar.activation(esum[:, 0:1], L.one[:, :], ACT.Exp)
            swap(0, 0)
            split_hi(0)
            swap(0, 1)
            split_hi(1)
            query_hi(0, 0)
            query_hi(0, 1)
            swap(0, 2)
            swap(0, 3)
            exps(0, 0)
            attention(0, True, first=True)
            experts(0, True, first=True)
            with act.Fori(1, B - 1) as i:
                attention(i, True)
                experts(i, True)
            attention(B - 1, False)
            experts(B - 1, False)

        @block.vector
        def _(dve):
            vec = nc.vector
            Steps, moments, normalise, minus_hi = chains(nc, L, dve)
            prep_moments, prep_normal, prep_x, prep_kv, prep_kn, prep_k = prepare_dve(nc, L, dve)
            split_lo = part_lo(nc, L, dve)

            def query_cos(i, p):
                dve.wait_ge(ev.swap_done.sem, ev.swap_done.upto(i, p + 1))
                if p >= 2:
                    dve.wait_ge(ev.qlo_done.sem, ev.qlo_done.upto(i, p - 1))
                vec.tensor_tensor(qf[p % 2][:, :, :], L.ps_q[p % 2][:, :, :], L.qcos[:, :].unsqueeze(1).to_broadcast([P, 2, S]),
                                  ALU.mult).then_inc(ev.qcos_done.sem, 1)

            def query_lo(i, p):
                dve.wait_ge(ev.qhi_done.sem, ev.qhi_done.upto(i, p + 1))
                minus_hi(q_lo[p % 2][:, :, :], qf[p % 2][:, :, :], q_hi[p % 2][:, :, :]).then_inc(ev.qlo_done.sem, 1)

            def maxima(i, h):
                dve.wait_ge(ev.s_full.sem, ev.s_full.upto(i, h + 1))
                vec.tensor_reduce(nmax[:, h, :], L.ps_s[h % 2][:, :, :], AX.X, ALU.max, negate=True).then_inc(ev.max_done.sem, 1)

            def inverse(i, h):
                dve.wait_ge(ev.exp_done.sem, ev.exp_done.upto(i, h + 1))
                vec.reciprocal(rinv[:, h, :], rsum[:, h, :]).then_inc(ev.rinv_done.sem, 1)

            def probs_lo(i, h):
                dve.wait_ge(ev.phi_done.sem, ev.phi_done.upto(i, h + 1))
                minus_hi(pT_lo[h % 3][:, :, :], L.ps_t[h % 2][:, :, :], pT_hi[h % 3][:, :, :]).then_inc(ev.plo_done.sem, 1)

            def attended_lo(i, p):
                dve.wait_ge(ev.ohi_done.sem, ev.ohi_done.upto(i, p + 1))
                minus_hi(o_lo[p % 2][:, :], L.ps_o[:, 0, :], o_hi[p % 2][:, :]).then_inc(ev.olo_done.sem, 1)

            def attention(i, prep, first=False):
                for r in range(NP + 2):
                    if r >= 1 and due(r + 1):
                        query_lo(i, r + 1)
                    if due(r + 3):
                        query_cos(i, r + 3)
                    if due(r):
                        inverse(i, 2 * r)
                    if prep and r == NP - 1:
                        prep_normal(i + 1)
                    if due(r - 1):
                        probs_lo(i, 2 * (r - 1))
                    if due(r - 2):
                        attended_lo(i, r - 2)
                    if due(r):
                        inverse(i, 2 * r + 1)
                    if due(r + 1):
                        maxima(i, 2 * (r + 1))
                    if due(r - 1):
                        probs_lo(i, 2 * (r - 1) + 1)
                    if due(r + 1):
                        maxima(i, 2 * (r + 1) + 1)
                    if prep and r == 3:
                        prep_moments(i + 1)
                    if first and r - 1 in parts_after_round:
                        split_lo(parts_after_round[r - 1])
                if prep:
                    prep_x(i + 1)

            def route(i, step):
                dve.wait_ge(ev.gate_exp_done.sem, ev.gate_exp_done.upto(i, 1))
                step(vec.reciprocal(einv[:, :], esum[:, :]))
                for j in range(NT):
                    last = vec.tensor_scalar(score[:, j, 0:E], eprob[:, j, :], einv[:, j:j + 1], None, ALU.mult)
                step(last, carry=True)
                for j in range(NT):
                    last = vec.max(top[:, j, :], score[:, j, 0:E])
                step(last)
                step(vec.tensor_copy(top[:, :, TOP:E], L.sentinel[:, 0:E - TOP].unsqueeze(1).to_broadcast([P, NT, E - TOP])),
                     carry=True)
                for j in range(NT):
                    last = vec.match_replace(rest[:, j, :], top[:, j, :], score[:, j, :], 0.0)
                step(last)
                step(vec.tensor_tensor(comb[:, :, :], score[:, :, 0:E], rest[:, :, 0:E], ALU.subtract))
                step(vec.tensor_copy(comb2[:, :, 0:E].bitcast(F32R), comb[:, :, :]))
                vec.tensor_tensor(comb2[:, :, LO:CK], comb[:, :, :], comb2[:, :, 0:E], ALU.subtract).then_inc(ev.comb_done.sem, 1)

            def experts(i, prep, first=False):
                step = Steps(ev.ffn_step, i)
                dve.wait_ge(ev.out_done.sem, ev.out_done.upto(i, NP))
                dve.wait_ge(ev.out_stored.sem, ev.out_stored.before(i, 16))
                dve.wait_ge(ev.x_loaded.sem, ev.x_loaded.upto(i, 16))
                vec.tensor_tensor(x2[:, :, :], L.ps_y[:, :, :], xin[:, :, :], ALU.add).then_inc(ev.x2_done.sem, 1)
                dve.wait_ge(ev.x2_done.sem, ev.x2_done.upto(i, 1))
                moments(step, lambda j: x2[:, j, :], mean_f, var_f, ev.varf_done)
                dve.wait_ge(ev.varf_done.sem, ev.varf_done.upto(i, 1))
                dve.wait_ge(ev.rsf_done.sem, ev.rsf_done.upto(i, 1))
                normalise(lambda j: xhat_f[:, j, :], lambda j: x2[:, j, :], mean_f, rstd_f, ev.xhf_done)
                if prep:
                    query_cos(i + 1, 0)
                dve.wait_ge(ev.xfhi_done.sem, ev.xfhi_done.upto(i, 1))
                minus_hi(xf_lo[:, :, :], L.ps_t[0][:, :, :], xf_hi[:, :, :]).then_inc(ev.xflo_done.sem, 1)
                if prep:
                    query_cos(i + 1, 1)
                    query_lo(i + 1, 0)
                dve.wait_ge(ev.logits_full.sem, ev.logits_full.upto(i, 1))
                vec.tensor_reduce(lmax[:, :], L.ps_t[1][:, 0, 0:NT * E].rearrange("p (j e) -> p j e", j=NT), AX.X, ALU.max,
                                  negate=True).then_inc(ev.lmax_done.sem, 1)
                if prep:
                    prep_kv(i + 1)
                for m in range(CH):
                    rows = chunk_rows(m)
                    dve.wait_ge(ev.silu_done.sem, ev.silu_done.upto(i, m + 1))
                    up, act = L.ps_q[m % 2][0:rows, 1, :], gate[m % 2][0:rows, :]
                    if m >= 2:
                        dve.wait_ge(ev.ulo_done.sem, ev.ulo_done.upto(i, m - 1))
                    if m < ES:
                        vec.tensor_tensor(unit[m % 2][0:rows, :], up, act, ALU.mult).then_inc(ev.su_done.sem, 1)
                    else:
                        c = m - ES
                        vec.tensor_tensor(prod[m % 2], up, act, ALU.mult).then_inc(ev.su_done.sem, 1)
                        dve.wait_ge(ev.su_done.sem, ev.su_done.upto(i, m + 1))
                        dve.wait_ge(ev.cb_full.sem, ev.cb_full.upto(i, c + 1))
                        vec.tensor_tensor(unit[m % 2], L.ps_t[c % 2][:, 0, :], prod[m % 2], ALU.mult
                                          ).then_inc(ev.cb_done.sem, 1)
                    if prep and m == 0:
                        prep_kn(i + 1)
                    if m == 1:
                        route(i, step)
                        step.end()
                    if prep and m == 2:
                        query_lo(i + 1, 1)
                    if prep and m == ES + 2:
                        prep_k(i + 1)
                    if first and m in parts_after_chunk:
                        split_lo(parts_after_chunk[m])
                if prep:
                    query_cos(i + 1, 2)
                    maxima(i + 1, 0)
                    maxima(i + 1, 1)
                dve.wait_ge(ev.down_done.sem, ev.down_done.upto(i, CH))
                vec.tensor_tensor(x2[:, :, :], L.ps_y[:, :, :], x2[:, :, :], ALU.add).then_inc(ev.osb_done.sem, 1)

            def rotated(p):
                dve.wait_ge(ev.swap_done.sem, ev.swap_done.upto(0, p + 1))
                qs = qswap[p % 2][:, :, :]
                vec.tensor_tensor(qs, qs, L.qsin[:, :].unsqueeze(1).to_broadcast([P, 2, S]), ALU.mult).then_inc(ev.qrot_part.sem, 1)
                query_cos(0, p)
                dve.wait_ge(ev.qrot_part.sem, ev.qrot_part.upto(0, p + 1))
                dve.wait_ge(ev.qcos_done.sem, ev.qcos_done.upto(0, p + 1))
                vec.tensor_tensor(qf[p % 2][:, :, :], qf[p % 2][:, :, :], qs, ALU.add).then_inc(ev.qrot_done.sem, 1)

            vec.tensor_copy(score[:, :, E:2 * E], L.sentinel[:, :].unsqueeze(1).to_broadcast([P, NT, E]))
            vec.memset(comb2[:, :, :], 0.0)
            for n in range(2):
                last = vec.memset(qswap[n][0:RANK, :, :], 0.0)
            last.then_inc(ev.zeros_set, 1)
            dve.wait_ge(ev.zeros_set, 3)
            rotated(0)
            split_lo(0)
            query_cos(0, 1)
            split_lo(1)
            query_lo(0, 0)
            query_lo(0, 1)
            query_cos(0, 2)
            maxima(0, 0)
            maxima(0, 1)
            attention(0, True, first=True)
            experts(0, True, first=True)
            with dve.Fori(1, B - 1) as i:
                attention(i, True)
                experts(i, True)
            attention(B - 1, False)
            experts(B - 1, False)

        @block.gpsimd
        def _(pool):
            gp, hi_of = nc.gpsimd, rounding(nc, L)
            power, prep_kp, prep_latents_hi, prep_latents_lo = prepare_pool(nc, L, pool)

            def rotate(i, p):
                pool.wait_ge(ev.swap_done.sem, ev.swap_done.upto(i, p + 1))
                qs = qswap[p % 2][:, :, :]
                gp.tensor_tensor(qs, qs, L.qsin[:, :].unsqueeze(1).to_broadcast([P, 2, S]), ALU.mult).then_inc(ev.qrot_part.sem, 1)

            def rotate_add(i, p):
                pool.wait_ge(ev.qrot_part.sem, ev.qrot_part.upto(i, p + 1))
                pool.wait_ge(ev.qcos_done.sem, ev.qcos_done.upto(i, p + 1))
                gp.tensor_tensor(qf[p % 2][:, :, :], qf[p % 2][:, :, :], qswap[p % 2][:, :, :], ALU.add).then_inc(ev.qrot_done.sem, 1)

            def normal(i, h):
                pool.wait_ge(ev.rinv_done.sem, ev.rinv_done.upto(i, h + 1))
                gp.tensor_tensor(probs[h % 3][:, :, :], probs[h % 3][:, :, :], rinv[:, h, :].unsqueeze(2).to_broadcast([P, NT, S]),
                                 ALU.mult).then_inc(ev.pn_done.sem, 1)

            def attention(i, prep):
                for r in range(NP - 1):
                    normal(i, 2 * (r + 1))
                    if prep and r == NP // 2:
                        power(L.var_a, L.rstd_a, ev.vara_done, ev.rsa_done, i + 1)
                    normal(i, 2 * (r + 1) + 1)
                    if due(r + 4):
                        rotate(i, r + 4)
                        rotate_add(i, r + 4)

            def experts(i, prep):
                power(var_f, rstd_f, ev.varf_done, ev.rsf_done, i)
                if prep:
                    for p in range(2):
                        rotate(i + 1, p)
                        rotate_add(i + 1, p)
                    power(L.var_k, L.rstd_k, ev.vark_done, ev.rsk_done, i + 1)
                for m in range(CH):
                    if m < ES:
                        pool.wait_ge(ev.su_done.sem, ev.su_done.upto(i, m + 1))
                    else:
                        pool.wait_ge(ev.cb_done.sem, ev.cb_done.upto(i, m - ES + 1))
                    if m >= 3:
                        pool.wait_ge(ev.down_done.sem, ev.down_done.upto(i, m - 2))
                    hi_of(u_hi[m % 3], unit[m % 2]).then_inc(ev.uhi_done.sem, 1)
                    pool.wait_ge(ev.uhi_done.sem, ev.uhi_done.upto(i, m + 1))
                    gp.tensor_tensor(u_lo[m % 3], unit[m % 2], u_hi[m % 3].bitcast(F32),
                                     ALU.subtract).then_inc(ev.ulo_done.sem, 1)
                    if prep and m == 1:
                        prep_kp(i + 1)
                    if prep and m == ES + 3:
                        prep_latents_hi(i + 1)
                    if prep and m == ES + 5:
                        prep_latents_lo(i + 1)
                if prep:
                    for p in (2, 3):
                        rotate(i + 1, p)
                        rotate_add(i + 1, p)
                        if p == 2:
                            normal(i + 1, 0)
                            normal(i + 1, 1)

            pool.wait_ge(ev.zeros_set, 3)
            rotate(0, 1)
            rotate_add(0, 1)
            rotate(0, 2)
            rotate_add(0, 2)
            normal(0, 0)
            normal(0, 1)
            rotate(0, 3)
            rotate_add(0, 3)
            with pool.Fori(0, B - 1) as i:
                attention(i, True)
                experts(i, True)
            attention(B - 1, False)
            experts(B - 1, False)


def layer(nc, d):
    with ExitStack() as ctx:
        L = Layer(nc, ctx)
        L.parts = expert_parts(L, d)
        weights(nc, L, d)
        loop(nc, L, d)


_INS = {"L0_attn_hidden_states": "x", "L0_attn_freqs_cis": "freqs", "L0_attn_Wq": "Wq", "L0_attn_Wkv_a": "Wkv_a",
        "L0_attn_kv_gamma": "gamma", "L0_attn_kv_beta": "beta", "L0_attn_Wkv_b": "Wkv_b", "L0_attn_Wout": "Wout",
        "L0_ffn_gate_w": "gate_w", "L0_ffn_w_gate": "w_gate", "L0_ffn_w_up": "w_up", "L0_ffn_w_down": "w_down",
        "L0_ffn_sw_gate": "sw_gate", "L0_ffn_sw_up": "sw_up", "L0_ffn_sw_down": "sw_down"}


def kernel(**inputs):
    import numpy as np
    import concourse.bacc as bacc
    from concourse.bass_utils import run_bass_kernel_spmd

    nc = bacc.Bacc("TRN2", target_bir_lowering=False, num_devices=1)
    arrays, d = {}, {}
    for name, short in _INS.items():
        a = np.ascontiguousarray(inputs[name])
        arrays[f"{short}_dram"] = a
        d[short] = nc.dram_tensor(f"{short}_dram", a.shape, F32, kind="ExternalInput").ap()
    d["out"] = nc.dram_tensor("out_dram", (B, S, D), F32, kind="ExternalOutput").ap()
    layer(nc, d)
    r = run_bass_kernel_spmd(nc, [arrays], core_ids=[0])
    return r.results[0]["out_dram"]
```
